# Optimizing a Trainium2 kernel written in Bass

```python
import numpy as np
import jax
import jax.numpy as jnp

def _softmax(x, axis=-1):
    return jax.nn.softmax(x, axis=axis)

def _gelu(x):
    return jax.nn.gelu(x, approximate=True)

def _silu(x):
    return jax.nn.silu(x)

def _sigmoid(x):
    return jax.nn.sigmoid(x)

def _layernorm(x, axis=-1, eps=1e-05):
    m = jnp.mean(x, axis=axis, keepdims=True)
    v = jnp.var(x, axis=axis, keepdims=True)
    return (x - m) / jnp.sqrt(v + eps)

def _scatter_add(tgt, idx, src, axis=0):
    return tgt.at[idx].add(src)

def _segment_sum(src, seg, n):
    return jax.ops.segment_sum(src, seg, n)
kernel_name = 'mk_sandwich_d2_jaxref_r8_f2f84b'

def setup_inputs(seed: int=0):
    np.random.seed(seed)
    _w = jnp.asarray

    def _L0_attn_setup():
        import jax, jax.numpy as jnp
        import numpy as np
        D_MODEL = 256
        N_HEADS = 16
        HEAD_DIM = D_MODEL // N_HEADS
        key = jax.random.key(seed)
        ks = jax.random.split(key, 5)
        scale = 1.0 / np.sqrt(D_MODEL)
        x = jax.random.normal(ks[0], (2, 256, D_MODEL), dtype=jnp.float32)
        W_qkv = jax.random.normal(ks[1], (D_MODEL, 3 * D_MODEL), dtype=jnp.float32) * scale
        b_qkv = jnp.zeros((3 * D_MODEL,), dtype=jnp.float32)
        W_out = jax.random.normal(ks[2], (D_MODEL, D_MODEL), dtype=jnp.float32) * scale
        b_out = jnp.zeros((D_MODEL,), dtype=jnp.float32)
        return {'x': x, 'W_qkv': W_qkv, 'b_qkv': b_qkv, 'W_out': W_out, 'b_out': b_out}
    _L0_attn_in = _L0_attn_setup()

    def _L0_ffn_setup():
        import jax, jax.numpy as jnp
        import numpy as np
        D = 256
        M = 128
        E = 32
        K = 6
        G = 8
        KG = 4
        SH = 256
        SCALE = 2.5

        def _route(xf, Wr, br):
            T = xf.shape[0]
            s = jax.nn.sigmoid(xf @ Wr.T + br)
            sg = s.reshape(T, G, E // G)
            group_w = jax.lax.top_k(sg, 2)[0].sum(-1)
            top_g = jax.lax.top_k(group_w, KG)[1]
            gmask = jnp.zeros((T, G), bool).at[jnp.arange(T)[:, None], top_g].set(True)
            masked = jnp.where(gmask[:, :, None], sg, 0.0).reshape(T, E)
            idx = jax.lax.top_k(masked, K)[1]
            w = jnp.take_along_axis(s, idx, axis=1)
            w = w / (w.sum(-1, keepdims=True) + 1e-20)
            return (idx, w * SCALE)
        key = jax.random.key(seed)
        ks = jax.random.split(key, 7)
        w = 0.02
        return {'hidden_tensor': jax.random.normal(ks[0], (2, 256, D), dtype=jnp.float32), 'Wr': jax.random.normal(ks[1], (E, D), dtype=jnp.float32) * w, 'br': jax.random.normal(ks[2], (E,), dtype=jnp.float32) * w, 'W1': jax.random.normal(ks[3], (E, M, D), dtype=jnp.float32) * w, 'W2': jax.random.normal(ks[4], (E, D, M), dtype=jnp.float32) * w, 'Ws1': jax.random.normal(ks[5], (SH, D), dtype=jnp.float32) * w, 'Ws2': jax.random.normal(ks[6], (D, SH), dtype=jnp.float32) * w}
    _L0_ffn_in = _L0_ffn_setup()

    def _L1_attn_setup():
        import jax, jax.numpy as jnp
        import numpy as np
        import math
        N_HEAD = 16
        LAYER = 1
        LAMBDA_INIT = 0.8 - 0.6 * math.exp(-0.3 * (LAYER - 1))
        key = jax.random.key(seed)
        ks = jax.random.split(key, 7)
        B, T, E = (2, 256, 256)
        s = 0.02
        return {'x': jax.random.normal(ks[0], (B, T, E), dtype=jnp.float32), 'W_attn': jax.random.normal(ks[1], (E, 3 * E), dtype=jnp.float32) * s, 'W_proj': jax.random.normal(ks[2], (E, E), dtype=jnp.float32) * s, 'lambda_q1': jax.random.normal(ks[3], (E,), dtype=jnp.float32) * 0.1, 'lambda_k1': jax.random.normal(ks[4], (E,), dtype=jnp.float32) * 0.1, 'lambda_q2': jax.random.normal(ks[5], (E,), dtype=jnp.float32) * 0.1, 'lambda_k2': jax.random.normal(ks[6], (E,), dtype=jnp.float32) * 0.1}
    _L1_attn_in = _L1_attn_setup()

    def _L1_ffn_setup():
        import jax, jax.numpy as jnp
        import numpy as np
        import math
        B, S, D = (2, 128, 256)
        H, KVH, HD = (16, 4, 128)
        E, K, FF = (8, 2, 896)
        EPS = 1e-05
        ROPE_BASE = 1000000.0

        def rmsnorm(x, w, eps=EPS):
            xf = x.astype(jnp.float32)
            var = jnp.mean(xf * xf, axis=-1, keepdims=True)
            return (xf * jax.lax.rsqrt(var + eps)).astype(x.dtype) * w

        def apply_rope(x, cos, sin):
            x1 = x[..., 0::2]
            x2 = x[..., 1::2]
            r1 = x1 * cos - x2 * sin
            r2 = x1 * sin + x2 * cos
            return jnp.stack([r1, r2], axis=-1).reshape(x.shape)
        key = jax.random.key(seed)
        ks = jax.random.split(key, 12)
        sc = 0.02
        inp = {'x': jax.random.normal(ks[0], (B, S, D), jnp.float32), 'ln_w': jnp.ones((D,), jnp.float32), 'ff_ln_w': jnp.ones((D,), jnp.float32), 'wq': jax.random.normal(ks[1], (D, H * HD), jnp.float32) * sc, 'wk': jax.random.normal(ks[2], (D, KVH * HD), jnp.float32) * sc, 'wv': jax.random.normal(ks[3], (D, KVH * HD), jnp.float32) * sc, 'wo': jax.random.normal(ks[4], (H * HD, D), jnp.float32) * sc, 'gate_w': jax.random.normal(ks[5], (D, E), jnp.float32) * sc, 'w1': jax.random.normal(ks[6], (E, D, FF), jnp.float32) * sc, 'w3': jax.random.normal(ks[7], (E, D, FF), jnp.float32) * sc, 'w2': jax.random.normal(ks[8], (E, FF, D), jnp.float32) * sc}
        return inp
    _L1_ffn_in = _L1_ffn_setup()
    _d = {'L0_attn_x': _L0_attn_in['x'], 'L0_attn_W_qkv': _L0_attn_in['W_qkv'], 'L0_attn_b_qkv': _L0_attn_in['b_qkv'], 'L0_attn_W_out': _L0_attn_in['W_out'], 'L0_attn_b_out': _L0_attn_in['b_out'], 'L0_ffn_Wr': _L0_ffn_in['Wr'], 'L0_ffn_br': _L0_ffn_in['br'], 'L0_ffn_W1': _L0_ffn_in['W1'], 'L0_ffn_W2': _L0_ffn_in['W2'], 'L0_ffn_Ws1': _L0_ffn_in['Ws1'], 'L0_ffn_Ws2': _L0_ffn_in['Ws2'], 'L1_attn_W_attn': _L1_attn_in['W_attn'], 'L1_attn_W_proj': _L1_attn_in['W_proj'], 'L1_attn_lambda_q1': _L1_attn_in['lambda_q1'], 'L1_attn_lambda_k1': _L1_attn_in['lambda_k1'], 'L1_attn_lambda_q2': _L1_attn_in['lambda_q2'], 'L1_attn_lambda_k2': _L1_attn_in['lambda_k2'], 'L1_ffn_ln_w': _L1_ffn_in['ln_w'], 'L1_ffn_ff_ln_w': _L1_ffn_in['ff_ln_w'], 'L1_ffn_wq': _L1_ffn_in['wq'], 'L1_ffn_wk': _L1_ffn_in['wk'], 'L1_ffn_wv': _L1_ffn_in['wv'], 'L1_ffn_wo': _L1_ffn_in['wo'], 'L1_ffn_gate_w': _L1_ffn_in['gate_w'], 'L1_ffn_w1': _L1_ffn_in['w1'], 'L1_ffn_w3': _L1_ffn_in['w3'], 'L1_ffn_w2': _L1_ffn_in['w2']}
    _x0 = _d['L0_attn_x']
    _d['L0_attn_x'] = jax.random.normal(jax.random.fold_in(jax.random.key(seed), 1), (4, 512, 256), dtype=_x0.dtype)
    del _x0
    return _d

def reference(L0_attn_x, L0_attn_W_qkv, L0_attn_b_qkv, L0_attn_W_out, L0_attn_b_out, L0_ffn_Wr, L0_ffn_br, L0_ffn_W1, L0_ffn_W2, L0_ffn_Ws1, L0_ffn_Ws2, L1_attn_W_attn, L1_attn_W_proj, L1_attn_lambda_q1, L1_attn_lambda_k1, L1_attn_lambda_q2, L1_attn_lambda_k2, L1_ffn_ln_w, L1_ffn_ff_ln_w, L1_ffn_wq, L1_ffn_wk, L1_ffn_wv, L1_ffn_wo, L1_ffn_gate_w, L1_ffn_w1, L1_ffn_w3, L1_ffn_w2):

    def _L0_attn_ref(x, W_qkv, b_qkv, W_out, b_out):
        import jax, jax.numpy as jnp
        import numpy as np
        D_MODEL = 256
        N_HEADS = 16
        HEAD_DIM = D_MODEL // N_HEADS
        bsz, seq_len, _ = x.shape
        qkv = x @ W_qkv + b_qkv
        qkv = qkv.reshape(bsz, seq_len, 3, N_HEADS, HEAD_DIM)
        qkv = jnp.transpose(qkv, (2, 0, 3, 1, 4))
        q, k, v = (qkv[0], qkv[1], qkv[2])
        scores = jnp.einsum('bhqd,bhkd->bhqk', q, k) / np.sqrt(HEAD_DIM).astype(np.float32)
        causal = jnp.tril(jnp.ones((seq_len, seq_len), dtype=bool))
        scores = jnp.where(causal[None, None], scores, -jnp.inf)
        attn = jax.nn.softmax(scores, axis=-1)
        out = jnp.einsum('bhqk,bhkd->bhqd', attn, v)
        out = jnp.transpose(out, (0, 2, 1, 3)).reshape(bsz, seq_len, D_MODEL)
        y = out @ W_out + b_out
        return y

    def _L0_ffn_ref(hidden_tensor, Wr, br, W1, W2, Ws1, Ws2):
        import jax, jax.numpy as jnp
        import numpy as np
        D = 256
        M = 128
        E = 32
        K = 6
        G = 8
        KG = 4
        SH = 256
        SCALE = 2.5

        def _route(xf, Wr, br):
            T = xf.shape[0]
            s = jax.nn.sigmoid(xf @ Wr.T + br)
            sg = s.reshape(T, G, E // G)
            group_w = jax.lax.top_k(sg, 2)[0].sum(-1)
            top_g = jax.lax.top_k(group_w, KG)[1]
            gmask = jnp.zeros((T, G), bool).at[jnp.arange(T)[:, None], top_g].set(True)
            masked = jnp.where(gmask[:, :, None], sg, 0.0).reshape(T, E)
            idx = jax.lax.top_k(masked, K)[1]
            w = jnp.take_along_axis(s, idx, axis=1)
            w = w / (w.sum(-1, keepdims=True) + 1e-20)
            return (idx, w * SCALE)
        B, Tlen, C = hidden_tensor.shape
        xf = hidden_tensor.reshape(-1, C).astype(jnp.float32)
        T = xf.shape[0]
        idx, w = _route(xf, Wr, br)
        gate = jnp.zeros((T, E), w.dtype).at[jnp.arange(T)[:, None], idx].add(w)

        def step(acc, ew):
            w1, w2, g = ew
            h = jnp.square(jax.nn.relu(xf @ w1.T)) @ w2.T
            return (acc + g[:, None] * h, None)
        acc, _ = jax.lax.scan(step, jnp.zeros_like(xf), (W1, W2, gate.T))
        moe_out = acc.reshape(B, Tlen, C).astype(hidden_tensor.dtype)
        shared = jnp.square(jax.nn.relu(hidden_tensor @ Ws1.T)) @ Ws2.T
        return shared + moe_out

    def _L1_attn_ref(x, W_attn, W_proj, lambda_q1, lambda_k1, lambda_q2, lambda_k2):
        import jax, jax.numpy as jnp
        import numpy as np
        import math
        N_HEAD = 16
        LAYER = 1
        LAMBDA_INIT = 0.8 - 0.6 * math.exp(-0.3 * (LAYER - 1))
        B, T, E = x.shape
        C = E // 2
        H = N_HEAD
        hd = E // H // 2
        scale = hd ** (-0.5)
        qkv = x @ W_attn
        q1 = qkv[..., 0 * C:1 * C].reshape(B, T, H, hd)
        k1 = qkv[..., 1 * C:2 * C].reshape(B, T, H, hd)
        q2 = qkv[..., 2 * C:3 * C].reshape(B, T, H, hd)
        k2 = qkv[..., 3 * C:4 * C].reshape(B, T, H, hd)
        v = qkv[..., 4 * C:6 * C].reshape(B, T, H, 2 * hd)
        lam = jnp.exp(jnp.dot(lambda_q1, lambda_k1)) - jnp.exp(jnp.dot(lambda_q2, lambda_k2)) + LAMBDA_INIT
        attn1 = jnp.einsum('bthd,bshd->bhts', q1, k1) * scale
        attn2 = jnp.einsum('bthd,bshd->bhts', q2, k2) * scale
        score = jax.nn.softmax(attn1 - lam * attn2, axis=-1)
        out = jnp.einsum('bhts,bshd->bthd', score, v)
        out = (1.0 - LAMBDA_INIT) * out.reshape(B, T, E)
        return out @ W_proj

    def _L1_ffn_ref(x, ln_w, ff_ln_w, wq, wk, wv, wo, gate_w, w1, w3, w2):
        import jax, jax.numpy as jnp
        import numpy as np
        import math
        B, S, D = (2, 128, 256)
        H, KVH, HD = (16, 4, 128)
        E, K, FF = (8, 2, 896)
        EPS = 1e-05
        ROPE_BASE = 1000000.0

        def rmsnorm(x, w, eps=EPS):
            xf = x.astype(jnp.float32)
            var = jnp.mean(xf * xf, axis=-1, keepdims=True)
            return (xf * jax.lax.rsqrt(var + eps)).astype(x.dtype) * w

        def apply_rope(x, cos, sin):
            x1 = x[..., 0::2]
            x2 = x[..., 1::2]
            r1 = x1 * cos - x2 * sin
            r2 = x1 * sin + x2 * cos
            return jnp.stack([r1, r2], axis=-1).reshape(x.shape)
        Bx, Sx, Dx = x.shape
        residual = x
        h = rmsnorm(x, ln_w)
        q = (h @ wq).reshape(Bx, Sx, H, HD)
        k = (h @ wk).reshape(Bx, Sx, KVH, HD)
        v = (h @ wv).reshape(Bx, Sx, KVH, HD)
        pos = jnp.arange(Sx, dtype=jnp.float32)
        inv_freq = ROPE_BASE ** (-jnp.arange(0, HD, 2, dtype=jnp.float32) / HD)
        ang = pos[:, None] * inv_freq[None, :]
        cos = jnp.cos(ang)[None, :, None, :]
        sin = jnp.sin(ang)[None, :, None, :]
        q = apply_rope(q, cos, sin)
        k = apply_rope(k, cos, sin)
        rep = H // KVH
        k = jnp.repeat(k, rep, axis=2)
        v = jnp.repeat(v, rep, axis=2)
        scores = jnp.einsum('bqhd,bkhd->bhqk', q, k) / math.sqrt(HD)
        causal = jnp.tril(jnp.ones((Sx, Sx), dtype=bool))
        scores = jnp.where(causal[None, None], scores, jnp.finfo(scores.dtype).min)
        attn = jax.nn.softmax(scores, axis=-1)
        o = jnp.einsum('bhqk,bkhd->bqhd', attn, v).reshape(Bx, Sx, H * HD)
        x = o @ wo + residual
        residual = x
        h = rmsnorm(x, ff_ln_w)
        ht = h.reshape(-1, Dx)
        logits = ht @ gate_w
        top_vals, top_idx = jax.lax.top_k(logits, K)
        gates = jax.nn.softmax(top_vals, axis=-1)
        out = jnp.zeros_like(ht)
        for e in range(E):
            we = jnp.sum(gates * (top_idx == e), axis=-1)
            ye = jax.nn.silu(ht @ w1[e]) * (ht @ w3[e]) @ w2[e]
            out = out + we[:, None] * ye
        return out.reshape(Bx, Sx, Dx) + residual
    x = L0_attn_x
    x = x + _layernorm(_L0_attn_ref(_layernorm(x, axis=-1), L0_attn_W_qkv, L0_attn_b_qkv, L0_attn_W_out, L0_attn_b_out), axis=-1)
    x = x + _layernorm(_L0_ffn_ref(_layernorm(x, axis=-1), L0_ffn_Wr, L0_ffn_br, L0_ffn_W1, L0_ffn_W2, L0_ffn_Ws1, L0_ffn_Ws2), axis=-1)
    x = x + _layernorm(_L1_attn_ref(_layernorm(x, axis=-1), L1_attn_W_attn, L1_attn_W_proj, L1_attn_lambda_q1, L1_attn_lambda_k1, L1_attn_lambda_q2, L1_attn_lambda_k2), axis=-1)
    x = x + _layernorm(_L1_ffn_ref(_layernorm(x, axis=-1), L1_ffn_ln_w, L1_ffn_ff_ln_w, L1_ffn_wq, L1_ffn_wk, L1_ffn_wv, L1_ffn_wo, L1_ffn_gate_w, L1_ffn_w1, L1_ffn_w3, L1_ffn_w2), axis=-1)
    return x

_drawn_inputs = setup_inputs


def setup_inputs(seed=0):
    import zlib

    import numpy as np

    out = dict(_drawn_inputs(seed))
    spreads = {'L0_attn_b_qkv': (0.0, 0.1),
     'L0_attn_b_out': (0.0, 0.1),
     'L1_ffn_ln_w': (1.0, 0.6),
     'L1_ffn_ff_ln_w': (1.0, 0.6)}
    factors = {'L1_attn_lambda_q1': 8.0,
     'L1_attn_lambda_k1': 8.0,
     'L1_attn_lambda_q2': 64.0,
     'L1_attn_lambda_k2': 64.0,
     'L1_ffn_wq': 8.0,
     'L1_ffn_wk': 8.0,
     'L1_ffn_gate_w': 7.932,
     'L1_ffn_w1': 7.014,
     'L1_ffn_w3': 6.869,
     'L1_ffn_w2': 7.0}
    for name, (base, spread) in spreads.items():
        noise = np.random.default_rng([zlib.crc32(name.encode()), seed]).standard_normal(out[name].shape)
        drawn = base * np.exp(spread * noise) if base else spread * noise
        out[name] = jnp.asarray(drawn.astype(out[name].dtype))
    for name, factor in factors.items():
        out[name] = (out[name] * factor).astype(out[name].dtype)
    return out
```

```python
from contextlib import ExitStack

import concourse.bass as bass
from concourse import mybir

F32 = mybir.dt.float32
BF16 = mybir.dt.bfloat16
U32 = mybir.dt.uint32
ALU = mybir.AluOpType
ACT = mybir.ActivationFunctionType
AX = mybir.AxisListType

P = 128
B, S, D = 4, 512, 256
KT = D // P
NQ = S // P
NT = B * NQ
T = B * S
H = 16
QUADS = B * H // 4
HD = D // H
GD, KVH = 128, 4
EPS = 1e-5
LAMBDA_INIT = 0.8 - 0.6
E0, K0, M0, G0, SCALE0 = 32, 6, 128, 8, 2.5
E1, F1 = 8, 896
FC1 = F1 // P

Q_PART = [0, 0, 0, 1, 1, 1, 2, 2]
K_PART = [0, 1, 2, 0, 1, 2, 0, 1]


class Core:

    def __init__(self, nc, ctx):
        self.nc, self.ctx, self.sems = nc, ctx, []
        self.x = self.sb("x", [P, NT, D], F32)
        self.ident = self.sb("ident", [P, P], F32)
        self.identb = self.sb("identb", [P, P], BF16)
        self.causal = self.sb("causal", [P, P], BF16)
        self.mhalf = self.sb("mhalf", [P, NQ], F32)
        self.bank = [ctx.enter_context(nc.psum_tensor(f"bank{i}", [P, 512], F32)) for i in range(8)]

    def sb(self, name, shape, dt):
        return self.ctx.enter_context(self.nc.sbuf_tensor(name, shape, dt))

    def sem(self, name):
        self.sems.append(self.nc.alloc_semaphore(name))
        return self.sems[-1]

    def end_stage(self):
        self.nc.clear_and_free_semaphores(self.sems)
        self.nc.all_engine_barrier()
        self.sems = []


def weights(ap):
    return ap.rearrange("(k p) n -> p k n", p=P)


def hold(eng, spare):
    eng.sem_inc(spare, 1)


class Norm:

    def __init__(self, c, ctx, name):
        nc = c.nc

        def sb(n, shape):
            return ctx.enter_context(nc.sbuf_tensor(f"{name}_{n}", shape, F32))

        self.c = c
        self.st, self.mv = sb("st", [P, NQ, 6]), sb("mv", [P, NQ, 2])
        self.ve, self.r = sb("ve", [P, NQ]), sb("r", [P, NQ])
        self.stats_done, self.mean_done, self.var_done, self.root_done, self.spare = (
            c.sem(f"{name}_{n}") for n in ("stats", "mean", "var", "root", "carry"))

    def statistics(self, v, b, tile, rms=False):
        nv = self.c.nc.vector
        hold(v, self.spare)
        for q in range(NQ):
            nv.bn_stats(self.st[:, q, :], tile(q)).then_inc(self.stats_done, 1)
        v.wait_ge(self.stats_done, b * NQ + NQ)
        hold(v, self.spare)
        for q in range(NQ):
            nv.bn_aggr(self.mv[:, q, :], self.st[:, q, :]).then_inc(self.mean_done, 1)
        v.wait_ge(self.mean_done, b * NQ + NQ)
        if rms:
            nv.tensor_tensor(self.ve[:, :], self.mv[:, :, 0], self.mv[:, :, 0], ALU.mult).then_inc(self.var_done, 1)
            v.wait_ge(self.var_done, b * 2 + 1)
            nv.scalar_tensor_tensor(out=self.ve[:, :], in0=self.mv[:, :, 1], scalar=EPS, in1=self.ve[:, :],
                                    op0=ALU.add, op1=ALU.add).then_inc(self.var_done, 1)
        else:
            nv.tensor_scalar(self.ve[:, :], self.mv[:, :, 1], EPS, None, ALU.add).then_inc(self.var_done, 1)

    def root(self, g, b, rms=False):
        g.wait_ge(self.var_done, b * (1 + rms) + 1 + rms)
        g.tensor_tensor(self.r[:, :], self.ve[:, :], self.c.mhalf[:, :], ALU.pow).then_inc(self.root_done, 1)

    def wait(self, v, b):
        v.wait_ge(self.root_done, b + 1)

    def apply(self, q, out, tile, rms=False):
        nv = self.c.nc.vector
        if rms:
            return nv.tensor_scalar(out, tile, self.r[:, q:q + 1], None, ALU.mult)
        return nv.tensor_scalar(out, tile, self.mv[:, q, 0:1], self.r[:, q:q + 1], ALU.subtract, ALU.mult)


def tile_of(x, b, q):
    return x[:, bass.ds(b * NQ + q, 1), :].rearrange("p a d -> p (a d)")


def load_constants(c, a, iota):
    nc = c.nc
    x_in, mask_in, cast = c.sem("x_in"), c.sem("mask_in"), c.sem("cast")
    with ExitStack() as ctx:
        mask = ctx.enter_context(nc.sbuf_tensor("mask", [P, P], F32))
        block = nc.Block()
        with block:
            @block.sync
            def _(sp):
                sp.dma_start(c.ident[:, :], a["ident"]).then_inc(mask_in, 16)
                sp.dma_start(mask[:, :], a["causal"]).then_inc(mask_in, 16)
                sp.dma_start(iota[:, :], a["iota"].partition_broadcast(P)).then_inc(mask_in, 16)
                sp.dma_start(c.x[:, :, :], a["x"].rearrange("b (q p) d -> p (b q) d", p=P)).then_inc(x_in, 16)
                sp.wait_ge(x_in, 16)

            @block.vector
            def _(v):
                v.wait_ge(mask_in, 48)
                nc.vector.tensor_copy(c.identb[:, :], c.ident[:, :]).then_inc(cast, 1)
                nc.vector.tensor_copy(c.causal[:, :], mask[:, :]).then_inc(cast, 1)

            @block.gpsimd
            def _(g):
                g.memset(c.mhalf[:, :], -0.5)


def narrow_projection(c, name, w_qk, w_v, b_qk, b_v, lambdas, q_parts, k_parts, vals):
    nc = c.nc
    with ExitStack() as ctx:
        def sb(n, shape, dt=F32):
            return ctx.enter_context(nc.sbuf_tensor(f"{name}_{n}", shape, dt))

        def sem(n):
            return c.sem(f"{name}_{n}")

        norm = Norm(c, ctx, name)
        wqk, wv = sb("wqk", [P, KT, 512]), sb("wv", [P, KT, D])
        biasqk, biasv = sb("bqk", [P, 4]), sb("bv", [P, D])
        mul = sb("mul", [P, 2])
        h = sb("h", [P, NQ, D])
        hT = sb("hT", [P, KT, S])
        xp = sb("xp", [P, 4, S])
        r1 = sb("r1", [P, 4, S])
        parts = sb("parts", [P, 4, 3, S], BF16)
        w_in, mul_ready = sem("w_in"), sem("mul_ready")
        h_ready, tr_done, hT_ready = sem("h_ready"), sem("tr_done"), sem("hT_ready")
        qk_done, v_done, v_kept = sem("qk_done"), sem("v_done"), sem("v_kept")
        xp_ready, hi_ready, r1_ready, mid_ready, lo_ready = (
            sem(n) for n in ("xp_ready", "hi_ready", "r1_ready", "mid_ready", "lo_ready"))
        stored, parts_free = sem("stored"), sem("parts_free")
        tr, ps, pv = c.bank[0:2], c.bank[2:6], c.bank[6:8]
        n_w = 2 + 2 * (lambdas is None)
        if lambdas is not None:
            lam_in, lam_ex, lam_sem, lam_exp = sb("lam_in", [P, 4, D]), sb("lam_ex", [P, 8]), sem("lam"), sem("lam_exp")
            halves = sb("halves", [P, 2])
            n_w = 4
        block = nc.Block()
        with block:
            @block.sync
            def _(sp):
                sp.sem_inc(parts_free, 1)
                sp.dma_start(wqk[:, :, :], weights(w_qk)).then_inc(w_in, 16)
                sp.dma_start(wv[:, :, :], weights(w_v)).then_inc(w_in, 16)
                if lambdas is None:
                    sp.dma_start(biasqk[:, :], b_qk).then_inc(w_in, 16)
                    sp.dma_start(biasv[:, :], b_v.partition_broadcast(P)).then_inc(w_in, 16)
                else:
                    sp.dma_start(lam_in[:, :, :], lambdas["vectors"].partition_broadcast(P)).then_inc(w_in, 16)
                    sp.dma_start(halves[:, :], lambdas["halves"]).then_inc(w_in, 16)
                with sp.Fori(0, B) as b:
                    for cc in range(4):
                        dst = (q_parts if cc < 2 else k_parts)[:, bass.ds(b * 4 + 2 * (cc % 2), 2), :, :]
                        sp.wait_ge(lo_ready, b * 4 + cc + 1)
                        sp.dma_start(dst.rearrange("t g r s -> (g r) t s"), parts[:, cc, :, :]).then_inc(stored, 16)
                    sp.wait_ge(stored, b * 64 + 64)
                    sp.sem_inc(parts_free, 1)

            @block.vector
            def _(v):
                v.wait_ge(w_in, 16 * n_w)
                if lambdas is None:
                    nc.vector.memset(mul[:, 0:1], HD ** -0.5).then_inc(mul_ready, 1)
                    nc.vector.memset(mul[:, 1:2], 1.0).then_inc(mul_ready, 1)
                    v.wait_ge(mul_ready, 2)
                else:
                    half_scale = (HD // 2) ** -0.5
                    for i in range(2):
                        nc.vector.tensor_tensor_reduce(lam_in[:, 2 * i, :], lam_in[:, 2 * i, :], lam_in[:, 2 * i + 1, :],
                                                       1.0, 0.0, ALU.mult, ALU.add, lam_ex[:, i:i + 1]).then_inc(lam_sem, 1)
                    v.wait_ge(lam_exp, 1)
                    nc.vector.tensor_tensor(lam_ex[:, 4:5], lam_ex[:, 2:3], lam_ex[:, 3:4], ALU.subtract).then_inc(lam_sem, 1)
                    v.wait_ge(lam_sem, 3)
                    nc.vector.tensor_scalar(lam_ex[:, 5:6], lam_ex[:, 4:5], LAMBDA_INIT, None, ALU.add).then_inc(lam_sem, 1)
                    v.wait_ge(lam_sem, 4)
                    nc.vector.tensor_scalar(mul[:, 1:2], halves[:, 0:1], lam_ex[:, 5:6], halves[:, 1:2],
                                            ALU.mult, ALU.add).then_inc(mul_ready, 1)
                    nc.vector.memset(mul[:, 0:1], half_scale).then_inc(mul_ready, 1)
                    nc.vector.memset(biasqk[:, :], 0.0).then_inc(mul_ready, 1)
                    v.wait_ge(mul_ready, 3)
                with v.Fori(0, B) as b:
                    norm.statistics(v, b, lambda q: tile_of(c.x, b, q))
                    norm.wait(v, b)
                    v.wait_ge(tr_done, b * KT + 2)
                    for q in range(NQ):
                        norm.apply(q, h[:, q, :], tile_of(c.x, b, q)).then_inc(h_ready, 1)
                    for cc in range(4):
                        if cc == 0:
                            v.wait_ge(parts_free, b + 1)
                        v.wait_ge(qk_done, b * 4 + cc + 1)
                        nc.vector.tensor_scalar(xp[:, cc, :], ps[cc][:, :], biasqk[:, cc:cc + 1],
                                                mul[:, cc // 2:cc // 2 + 1], ALU.add, ALU.mult).then_inc(xp_ready, 1)
                    for q in range(NQ):
                        v.wait_ge(v_done, b * 2 + q // 2 + 3)
                        dst = vals[:, bass.ds(b * H, H), q, :]
                        src = pv[q // 2][:, (q % 2) * D:(q % 2 + 1) * D].rearrange("p (h d) -> p h d", d=HD)
                        if lambdas is None:
                            nc.vector.tensor_tensor(dst, src, biasv[:, :].rearrange("p (h d) -> p h d", d=HD),
                                                    ALU.add).then_inc(v_kept, 1)
                        else:
                            nc.vector.tensor_copy(dst, src).then_inc(v_kept, 1)
                    for cc in range(4):
                        v.wait_ge(hi_ready, b * 4 + cc + 1)
                        nc.vector.tensor_tensor(r1[:, cc, :], xp[:, cc, :], parts[:, cc, 0, :], ALU.subtract).then_inc(r1_ready, 1)
                    for cc in range(4):
                        v.wait_ge(mid_ready, b * 4 + cc + 1)
                        v.wait_ge(r1_ready, b * 4 + cc + 1)
                        nc.vector.tensor_tensor(parts[:, cc, 2, :], r1[:, cc, :], parts[:, cc, 1, :], ALU.subtract).then_inc(lo_ready, 1)

            @block.gpsimd
            def _(g):
                with g.Fori(0, B) as b:
                    norm.root(g, b)

            @block.scalar
            def _(a):
                if lambdas is not None:
                    a.wait_ge(lam_sem, 2)
                    nc.scalar.activation(lam_ex[:, 2:4], lam_ex[:, 0:2], ACT.Exp).then_inc(lam_exp, 1)
                with a.Fori(0, B) as b:
                    for k in range(KT):
                        a.wait_ge(tr_done, b * KT + k + 3)
                        if k == 0:
                            a.wait_ge(v_done, b * 2 + 2)
                        nc.scalar.copy(hT[:, k, :], tr[k][:, :]).then_inc(hT_ready, 1)
                    for cc in range(4):
                        a.wait_ge(xp_ready, b * 4 + cc + 1)
                        nc.scalar.copy(parts[:, cc, 0, :], xp[:, cc, :]).then_inc(hi_ready, 1)
                    for cc in range(4):
                        a.wait_ge(r1_ready, b * 4 + cc + 1)
                        nc.scalar.copy(parts[:, cc, 1, :], r1[:, cc, :]).then_inc(mid_ready, 1)

            @block.tensor
            def _(pe):
                pe.sem_inc(tr_done, KT)
                pe.sem_inc(v_done, 2)
                pe.wait_ge(w_in, 16 * n_w)
                with pe.Fori(0, B) as b:
                    for k in range(KT):
                        for q in range(NQ):
                            if k == 0:
                                pe.wait_ge(h_ready, b * NQ + q + 1)
                            mm = nc.tensor.transpose(tr[k][:, q * P:(q + 1) * P], h[:, q, k * P:(k + 1) * P], c.ident[:, :])
                        mm.then_inc(tr_done, 1)
                    pe.wait_ge(hT_ready, b * KT + KT)
                    for cc in range(4):
                        for k in range(KT):
                            mm = nc.tensor.matmul(ps[cc][:, :], wqk[:, k, cc * P:(cc + 1) * P], hT[:, k, :],
                                                  start=(k == 0), stop=(k == KT - 1))
                        mm.then_inc(qk_done, 1)
                    for q in range(NQ):
                        for k in range(KT):
                            mm = nc.tensor.matmul(pv[q // 2][:, (q % 2) * D:(q % 2 + 1) * D], hT[:, k, q * P:(q + 1) * P],
                                                  wv[:, k, :], start=(k == 0), stop=(k == KT - 1))
                        if q % 2:
                            mm.then_inc(v_done, 1)


def attention(c, name, q_src, k_src, vals, out, narrow, causal):
    nc = c.nc
    W = HD if narrow else GD
    dt = BF16 if narrow else F32
    kh = 4 if narrow else 1
    loads = 16 if narrow else 2
    width = [(qt + 1) * P if causal else S for qt in range(NQ)]
    STEPS = B * H
    with ExitStack() as ctx:
        def sb(n, shape, d=F32):
            return ctx.enter_context(nc.sbuf_tensor(f"{name}_{n}", shape, d))

        def sem(n):
            return c.sem(f"{name}_{n}")

        qs = [sb(f"q{s}", [P, 4, S], dt) for s in range(2)]
        ks = [sb(f"k{s}", [P, kh, S], dt) for s in range(2)]
        probs = [sb(f"probs{i}", [P, NQ, S]) for i in range(2)]
        pT = sb("pT", [P, NQ, S])
        nmax, rsum, rinv = sb("nmax", [P, 8, NQ]), sb("rsum", [P, 8, NQ]), sb("rinv", [P, 8, NQ])
        o_slot = None if narrow else [sb(f"o{i}", [P, NQ, W]) for i in range(2)]
        loaded = [sem("loaded0"), sem("loaded1")]
        scores_done, max_ready, exp_done, turned, pv_done, rinv_ready, o_ready = (
            sem(n) for n in ("scores", "max", "exp", "turned", "pv", "rinv", "o"))
        copied = [sem("copied_even"), sem("copied_odd")]
        o_free = [sem("o_free0"), sem("o_free1")]
        sbank, tbank, obank = c.bank[0:4], c.bank[4:6], c.bank[6:8]

        def wait_copy(eng, n, qt):
            eng.wait_ge(copied[qt % 2], 2 * n + (qt // 2 + 1))

        def load_quad(sp, quad, s):
            if narrow:
                for j in range(8):
                    for dst, src, part in ((qs[s], q_src, Q_PART[j]), (ks[s], k_src, K_PART[j])):
                        sp.dma_start(dst[16 * j:16 * (j + 1), :, :],
                                     src[part, bass.ds(quad, 1), :, :].rearrange("a (u d) s -> d (a u) s", d=HD)
                                     ).then_inc(loaded[s], 16)
            else:
                for dst, src in ((qs[s], q_src), (ks[s], k_src)):
                    sp.dma_start(dst[:, :, :], src[bass.ds(quad, 1), :, :, :].rearrange("a p u s -> p (a u) s")
                                 ).then_inc(loaded[s], 16)

        block = nc.Block()
        with block:
            @block.sync
            def _(sp):
                for s in range(2):
                    load_quad(sp, s, s)
                if not narrow:
                    sp.sem_inc(o_free[0], 16)
                    sp.sem_inc(o_free[1], 16)

                def store(n, j):
                    sp.wait_ge(o_ready, n + 1)
                    sp.dma_start(out[bass.ds(n, 1), :, :].rearrange("a (q p) d -> p (a q) d", p=P),
                                 o_slot[j % 2][:, :, :]).then_inc(o_free[j % 2], 16)

                with sp.Fori(1, 8) as m:
                    for j in range(8):
                        if not narrow:
                            store(8 * m + (j - 8), j)
                        if j in (2, 6):
                            s = j // 4
                            sp.wait_ge(scores_done, 32 * m + (16 * s - 16))
                            load_quad(sp, 2 * m + s, s)
                if not narrow:
                    for j in range(8):
                        store(56 + j, j)
                    for i in range(2):
                        sp.wait_ge(o_free[i], 16 * (STEPS // 2 + 1))

            @block.tensor
            def _(pe):
                def scores(m, j, qt):
                    s, u = j // 4, j % 4
                    if u == 0 and qt == 0:
                        pe.wait_ge(loaded[s], (m + 1) * 16 * loads)
                    w = width[qt]
                    mm = nc.tensor.matmul(sbank[qt][:, 0:w], qs[s][:, u, qt * P:(qt + 1) * P], ks[s][:, u % kh, 0:w],
                                          start=True, stop=not causal)
                    if causal:
                        mm = nc.tensor.matmul(sbank[qt][:, w - P:w], c.identb[:, :], c.causal[:, :], start=False, stop=True)
                    mm.then_inc(scores_done, 1)

                def values(m, j, qt):
                    n = 8 * m + j
                    wait_copy(pe, n, qt)
                    nk = width[qt] // P
                    for kt in range(nk):
                        if narrow:
                            rhs = vals[:, bass.ds(n, 1), kt, :].rearrange("p a d -> p (a d)")
                        else:
                            rhs = vals[:, bass.ds(2 * m + j // 4, 1), kt, :].rearrange("p a d -> p (a d)")
                        mm = nc.tensor.matmul(obank[j % 2][:, qt * W:(qt + 1) * W], pT[:, qt, kt * P:(kt + 1) * P], rhs,
                                              start=(kt == 0), stop=(kt == nk - 1))
                    if qt == NQ - 1:
                        mm.then_inc(pv_done, 1)

                def step(m, j, following):
                    n = 8 * m + j
                    for qt in range(NQ):
                        pe.wait_ge(exp_done, NQ * n + qt + 1)
                        if qt >= 2:
                            wait_copy(pe, n, qt - 2)
                        for kt in range(width[qt] // P):
                            mm = nc.tensor.transpose(tbank[qt % 2][:, kt * P:(kt + 1) * P],
                                                     probs[j % 2][:, qt, kt * P:(kt + 1) * P], c.ident[:, :])
                        mm.then_inc(turned, 1)
                        if following:
                            scores(*following, qt)
                        if qt:
                            values(m, j, qt - 1)
                    values(m, j, NQ - 1)

                for qt in range(NQ):
                    scores(0, 0, qt)
                with pe.Fori(0, 7) as m:
                    for j in range(8):
                        step(m, j, (m, j + 1) if j < 7 else (m + 1, 0))
                for j in range(8):
                    step(7, j, (7, j + 1) if j < 7 else None)

            @block.scalar
            def _(a):
                def step(m, j):
                    for qt in range(NQ):
                        a.wait_ge(max_ready, NQ * (8 * m + j) + qt + 1)
                        nc.scalar.activation(probs[j % 2][:, qt, 0:width[qt]], sbank[qt][:, 0:width[qt]], ACT.Exp,
                                             bias=nmax[:, j, qt:qt + 1],
                                             accum_out=rsum[:, j, qt:qt + 1]).then_inc(exp_done, 1)
                    for qt in (1, 3):
                        a.wait_ge(turned, NQ * (8 * m + j) + qt + 1)
                        nc.scalar.copy(pT[:, qt, 0:width[qt]], tbank[1][:, 0:width[qt]]).then_inc(copied[1], 1)

                with a.Fori(0, 8) as m:
                    for j in range(8):
                        step(m, j)

            @block.vector
            def _(v):
                def negated_max(m, j, qt):
                    v.wait_ge(scores_done, NQ * (8 * m + j) + qt + 1)
                    nc.vector.tensor_reduce(nmax[:, j, qt:qt + 1], sbank[qt][:, 0:width[qt]], AX.X, ALU.max,
                                            negate=True).then_inc(max_ready, 1)

                def step(m, j, following):
                    n = 8 * m + j
                    for qt in range(NQ):
                        if following:
                            negated_max(*following, qt)
                        if qt % 2 == 0:
                            v.wait_ge(turned, NQ * n + qt + 1)
                            nc.vector.tensor_copy(pT[:, qt, 0:width[qt]], tbank[0][:, 0:width[qt]]).then_inc(copied[0], 1)
                    v.wait_ge(exp_done, NQ * n + NQ)
                    nc.vector.reciprocal(rinv[:, j, :], rsum[:, j, :]).then_inc(rinv_ready, 1)
                    v.wait_ge(rinv_ready, n + 1)
                    v.wait_ge(pv_done, n + 1)
                    o = obank[j % 2][:, 0:NQ * W].rearrange("p (q w) -> p q w", w=W)
                    ri = rinv[:, j, :].unsqueeze(2).to_broadcast([P, NQ, W])
                    if narrow:
                        dst = out[:, bass.ds(n, 1), :, :].rearrange("p a q w -> p (a q) w")
                    else:
                        v.wait_ge(o_free[j % 2], 16 * (4 * m + j // 2 + 1))
                        dst = o_slot[j % 2][:, :, :]
                    nc.vector.tensor_tensor(dst, o, ri, ALU.mult).then_inc(o_ready, 1)

                for qt in range(NQ):
                    negated_max(0, 0, qt)
                with v.Fori(0, 7) as m:
                    for j in range(8):
                        step(m, j, (m, j + 1) if j < 7 else (m + 1, 0))
                for j in range(8):
                    step(7, j, (7, j + 1) if j < 7 else None)


def narrow_output(c, name, attended, w_out, bias, factor):
    nc = c.nc
    with ExitStack() as ctx:
        def sb(n, shape):
            return ctx.enter_context(nc.sbuf_tensor(f"{name}_{n}", shape, F32))

        def sem(n):
            return c.sem(f"{name}_{n}")

        norm = Norm(c, ctx, name)
        w, bias_row = sb("w", [P, KT, D]), sb("bias", [P, D])
        o, oT = sb("o", [P, NQ, D]), sb("oT", [P, KT, S])
        y, t = sb("y", [P, NQ, D]), sb("t", [P, NQ, D])
        w_in, o_ready, tr_done, oT_ready, y_done, y_ready, t_ready, x_ready, spare = (
            sem(n) for n in ("w_in", "o_ready", "tr_done", "oT_ready", "y_done", "y_ready", "t_ready", "x_ready", "spare"))
        y_free = sem("y_free")
        tr, py = c.bank[0:2], c.bank[2:4]
        n_w = 1 + (bias is not None)
        block = nc.Block()
        with block:
            @block.sync
            def _(sp):
                sp.dma_start(w[:, :, :], weights(w_out)).then_inc(w_in, 16)
                if bias is not None:
                    sp.dma_start(bias_row[:, :], bias.partition_broadcast(P)).then_inc(w_in, 16)

            @block.gpsimd
            def _(g):
                with g.Fori(0, B) as b:
                    g.wait_ge(tr_done, b * KT + KT)
                    hold(g, spare)
                    for q in range(NQ):
                        g.tensor_copy(o[:, q, :].rearrange("p (h d) -> p h d", d=HD),
                                      attended[:, bass.ds(b * H, H), q, :]).then_inc(o_ready, 1)
                    norm.root(g, b)

            @block.tensor
            def _(pe):
                pe.sem_inc(tr_done, KT)
                pe.wait_ge(w_in, 16 * n_w)
                with pe.Fori(0, B) as b:
                    for k in range(KT):
                        for q in range(NQ):
                            if k == 0:
                                pe.wait_ge(o_ready, b * NQ + q + 1)
                            mm = nc.tensor.transpose(tr[k][:, q * P:(q + 1) * P], o[:, q, k * P:(k + 1) * P], c.ident[:, :])
                        mm.then_inc(tr_done, 1)
                    pe.wait_ge(oT_ready, b * KT + KT)
                    for q in range(NQ):
                        for k in range(KT):
                            mm = nc.tensor.matmul(py[q // 2][:, (q % 2) * D:(q % 2 + 1) * D], oT[:, k, q * P:(q + 1) * P],
                                                  w[:, k, :], start=(k == 0), stop=(k == KT - 1))
                        if q % 2:
                            mm.then_inc(y_done, 1)

            @block.scalar
            def _(a):
                with a.Fori(0, B) as b:
                    for k in range(KT):
                        a.wait_ge(tr_done, b * KT + k + 3)
                        if k == 0:
                            a.wait_ge(y_free, b + 1)
                        nc.scalar.activation(oT[:, k, :], tr[k][:, :], ACT.Copy, scale=factor).then_inc(oT_ready, 1)

            @block.vector
            def _(v):
                v.sem_inc(y_free, 1)
                if bias is not None:
                    v.wait_ge(w_in, 16 * n_w)
                with v.Fori(0, B) as b:
                    for i in range(2):
                        v.wait_ge(y_done, b * 2 + i + 1)
                        src = py[i][:, :].rearrange("p (q d) -> p q d", d=D)
                        dst = y[:, 2 * i:2 * i + 2, :]
                        if bias is not None:
                            row = bias_row[:, :].unsqueeze(1).to_broadcast([P, 2, D])
                            mm = nc.vector.tensor_tensor(dst, src, row, ALU.add)
                        else:
                            mm = nc.vector.tensor_copy(dst, src)
                        mm.then_inc(y_ready, 1)
                    v.wait_ge(y_ready, b * 2 + 2)
                    v.sem_inc(y_free, 1)
                    norm.statistics(v, b, lambda q: y[:, q, :])
                    norm.wait(v, b)
                    add_normed(c, v, norm, b, lambda q: y[:, q, :], t, t_ready, x_ready)


def add_normed(c, v, norm, b, tile, t, t_ready, x_ready):
    for q in range(NQ):
        norm.apply(q, t[:, q, :], tile(q)).then_inc(t_ready, 1)
    for q in range(NQ):
        v.wait_ge(t_ready, b * NQ + q + 1)
        c.nc.vector.tensor_tensor(tile_of(c.x, b, q), tile_of(c.x, b, q), t[:, q, :], ALU.add).then_inc(x_ready, 1)


def router_input(c, name, src, rms, col_scale, w_router, bias, n_experts, hT_all, logits):
    nc = c.nc
    with ExitStack() as ctx:
        def sb(n, shape):
            return ctx.enter_context(nc.sbuf_tensor(f"{name}_{n}", shape, F32))

        def sem(n):
            return c.sem(f"{name}_{n}")

        norm = Norm(c, ctx, name)
        w = sb("w", [P, KT, n_experts])
        row = sb("row", [P, n_experts])
        col = sb("col", [P, KT])
        h, hT = sb("h", [P, NQ, D]), sb("hT", [P, KT, S])
        w_in, h_ready, tr_done, hT_ready, hT_kept, lg_done, lg_ready, spare = (
            sem(n) for n in ("w_in", "h_ready", "tr_done", "hT_ready", "hT_kept", "lg_done", "lg_ready", "spare"))
        tr, pl = c.bank[0:2], c.bank[2]
        n_w = 1 + (bias is not None) + (col_scale is not None)
        block = nc.Block()
        with block:
            @block.sync
            def _(sp):
                sp.dma_start(w[:, :, :], weights(w_router)).then_inc(w_in, 16)
                if bias is not None:
                    sp.dma_start(row[:, :], bias.partition_broadcast(P)).then_inc(w_in, 16)
                if col_scale is not None:
                    sp.dma_start(col[:, :], col_scale).then_inc(w_in, 16)

            @block.vector
            def _(v):
                v.wait_ge(w_in, 16 * n_w)
                with v.Fori(0, B) as b:
                    norm.statistics(v, b, lambda q: tile_of(src, b, q), rms)
                    norm.wait(v, b)
                    v.wait_ge(tr_done, b * KT + KT)
                    for q in range(NQ):
                        norm.apply(q, h[:, q, :], tile_of(src, b, q), rms).then_inc(h_ready, 1)
                    v.wait_ge(lg_done, b + 2)
                    dst = logits[:, bass.ds(b * NQ, NQ), :]
                    lg = pl[:, 0:NQ * n_experts].rearrange("p (q e) -> p q e", e=n_experts)
                    if bias is not None:
                        nc.vector.tensor_tensor(dst, lg, row[:, :].unsqueeze(1).to_broadcast([P, NQ, n_experts]),
                                                ALU.add).then_inc(lg_ready, 1)
                    else:
                        nc.vector.tensor_copy(dst, lg).then_inc(lg_ready, 1)

            @block.gpsimd
            def _(g):
                g.sem_inc(hT_kept, KT)
                with g.Fori(0, B) as b:
                    norm.root(g, b, rms)
                    for k in range(KT):
                        g.wait_ge(hT_ready, b * KT + k + 1)
                        hold(g, spare)
                        g.tensor_copy(hT_all[:, k, bass.ds(b * S, S)], hT[:, k, :]).then_inc(hT_kept, 1)

            @block.scalar
            def _(a):
                with a.Fori(0, B) as b:
                    for k in range(KT):
                        a.wait_ge(tr_done, b * KT + k + 3)
                        a.wait_ge(hT_kept, b * KT + k + 1)
                        a.wait_ge(lg_done, b + 1)
                        if col_scale is None:
                            nc.scalar.copy(hT[:, k, :], tr[k][:, :]).then_inc(hT_ready, 1)
                        else:
                            nc.scalar.activation(hT[:, k, :], tr[k][:, :], ACT.Copy, scale=col[:, k:k + 1]).then_inc(hT_ready, 1)

            @block.tensor
            def _(pe):
                pe.sem_inc(tr_done, KT)
                pe.sem_inc(lg_done, 1)
                pe.wait_ge(w_in, 16 * n_w)
                with pe.Fori(0, B) as b:
                    for k in range(KT):
                        for q in range(NQ):
                            if k == 0:
                                pe.wait_ge(h_ready, b * NQ + q + 1)
                            mm = nc.tensor.transpose(tr[k][:, q * P:(q + 1) * P], h[:, q, k * P:(k + 1) * P], c.ident[:, :])
                        mm.then_inc(tr_done, 1)
                    pe.wait_ge(hT_ready, b * KT + KT)
                    for q in range(NQ):
                        for k in range(KT):
                            mm = nc.tensor.matmul(pl[:, q * n_experts:(q + 1) * n_experts], hT[:, k, q * P:(q + 1) * P],
                                                  w[:, k, :], start=(k == 0), stop=(k == KT - 1))
                    mm.then_inc(lg_done, 1)


class Chain:

    def __init__(self, v, sem):
        self.v, self.sem, self.n = v, sem, 0

    def link(self, ins):
        self.n += 1
        ins.then_inc(self.sem, 1)
        self.v.wait_ge(self.sem, self.n)


def sigmoid_gates(c, name, logits, iota, gates):
    nc = c.nc
    KG, EG = 4, E0 // G0
    with ExitStack() as ctx:
        def sb(n, shape, dt=F32):
            return ctx.enter_context(nc.sbuf_tensor(f"{name}_{n}", shape, dt))

        ex, s = sb("ex", [P, NT, E0]), sb("s", [P, NT, E0])
        pairs = sb("pairs", [P, 6, NT * G0])
        gw = sb("gw", [P, NT, G0])
        top, idx, idxf = sb("top", [P, NT, 8]), sb("idx", [P, NT, 8], U32), sb("idxf", [P, NT, 8])
        eq = sb("eq", [P, NT, E0, K0])
        gmask, masked, sel = sb("gmask", [P, NT, G0]), sb("masked", [P, NT, E0]), sb("sel", [P, NT, E0])
        den = sb("den", [P, 2, NT])
        ex_ready, step = c.sem(f"{name}_ex"), c.sem(f"{name}_step")
        block = nc.Block()
        with block:
            @block.scalar
            def _(a):
                nc.scalar.activation(ex[:, :, :], logits[:, :, :], ACT.Exp, scale=-1.0).then_inc(ex_ready, 1)

            @block.vector
            def _(v):
                nv = nc.vector
                link = Chain(v, step).link

                def top8(scores):
                    for t in range(NT):
                        ins = nv.max(top[:, t, :], scores[:, t, :])
                    link(ins)
                    for t in range(NT):
                        ins = nv.max_index(idx[:, t, :], top[:, t, :], scores[:, t, :])
                    link(ins)
                    link(nv.tensor_copy(idxf[:, :, :], idx[:, :, :]))

                def among(out, n, k):
                    e = eq[:, :, 0:n, 0:k]
                    link(nv.tensor_tensor(e, idxf[:, :, 0:k].unsqueeze(2).to_broadcast([P, NT, n, k]),
                                          iota[:, 0:n].unsqueeze(1).unsqueeze(3).to_broadcast([P, NT, n, k]), ALU.is_equal))
                    link(nv.tensor_reduce(out, e, AX.X, ALU.add))

                v.wait_ge(ex_ready, 1)
                link(nv.tensor_scalar(s[:, :, :], ex[:, :, :], 1.0, None, ALU.add))
                link(nv.reciprocal(s[:, :, :], s[:, :, :]))
                sg = s[:, :, :].rearrange("p t (g e) -> p (t g) e", e=EG)
                for i, (x, y, op) in enumerate(((0, 1, ALU.max), (0, 1, ALU.min), (2, 3, ALU.max), (2, 3, ALU.min))):
                    link(nv.tensor_tensor(pairs[:, i, :], sg[:, :, x], sg[:, :, y], op))
                link(nv.tensor_tensor(pairs[:, 4, :], pairs[:, 0, :], pairs[:, 2, :], ALU.min))
                link(nv.tensor_tensor(pairs[:, 5, :], pairs[:, 1, :], pairs[:, 3, :], ALU.max))
                link(nv.tensor_tensor(pairs[:, 4, :], pairs[:, 4, :], pairs[:, 5, :], ALU.max))
                link(nv.tensor_tensor(pairs[:, 5, :], pairs[:, 0, :], pairs[:, 2, :], ALU.max))
                link(nv.tensor_tensor(gw[:, :, :].rearrange("p t g -> p (t g)"), pairs[:, 4, :], pairs[:, 5, :], ALU.add))
                top8(gw)
                among(gmask[:, :, :], G0, KG)
                link(nv.tensor_tensor(masked[:, :, :].rearrange("p t (g e) -> p (t g) e", e=EG), sg,
                                      gmask[:, :, :].rearrange("p t g -> p (t g)").unsqueeze(2).to_broadcast([P, NT * G0, EG]),
                                      ALU.mult))
                top8(masked)
                among(sel[:, :, :], E0, K0)
                link(nv.tensor_tensor(sel[:, :, :], sel[:, :, :], s[:, :, :], ALU.mult))
                link(nv.tensor_reduce(den[:, 0, :], sel[:, :, :], AX.X, ALU.add))
                link(nv.tensor_scalar(den[:, 1, :], den[:, 0, :], 1e-20, None, ALU.add))
                link(nv.reciprocal(den[:, 0, :], den[:, 1, :]))
                link(nv.tensor_tensor(gates[:, :, :], sel[:, :, :], den[:, 0, :].unsqueeze(2).to_broadcast([P, NT, E0]), ALU.mult))
                link(nv.tensor_scalar(gates[:, :, :], gates[:, :, :], SCALE0, None, ALU.mult))


def relu2_experts(c, name, hT, gates, w, acc):
    nc = c.nc
    WC = KT * M0
    PAIRS = E0 // 2
    with ExitStack() as ctx:
        def sb(n, shape):
            return ctx.enter_context(nc.sbuf_tensor(f"{name}_{n}", shape, F32))

        def sem(n):
            return c.sem(f"{name}_{n}")

        ws = [sb(f"w{s}", [P, 2, WC + D]) for s in range(2)]
        relu, act = sb("relu", [P, 2, S]), sb("act", [P, 2, S])
        loaded = [sem("loaded0"), sem("loaded1")]
        up_done, relu_ready, act_ready, y_done, acc_done, zeroed = (
            sem(n) for n in ("up", "relu", "act", "y", "acc", "zeroed"))
        ph, py = c.bank[0:2], c.bank[2:6]

        block = nc.Block()
        with block:
            @block.sync
            def _(sp):
                def load(pair, s):
                    sp.dma_start(ws[s][:, :, :], w[bass.ds(pair, 1), :, :, :].rearrange("a p i n -> p (a i) n")).then_inc(loaded[s], 16)

                load(0, 0)
                load(1, 1)
                with sp.Fori(1, PAIRS // 2) as m:
                    for s in range(2):
                        sp.wait_ge(y_done, 16 * m + (8 * s - 8))
                        load(2 * m + s, s)
                sp.wait_ge(y_done, 8 * PAIRS - 8)
                load(PAIRS, 0)

            @block.tensor
            def _(pe):
                def group(unit, g, s, load_count):
                    pe.wait_ge(loaded[s], load_count)
                    for i in range(2):
                        for k in range(KT):
                            mm = nc.tensor.matmul(ph[i][:, :], ws[s][:, i, k * M0:(k + 1) * M0], hT[:, k, bass.ds(g * S, S)],
                                                  start=(k == 0), stop=(k == KT - 1))
                        mm.then_inc(up_done, 1)
                    for i in range(2):
                        pe.wait_ge(act_ready, unit + (i + 1))
                        for q in range(NQ):
                            mm = nc.tensor.matmul(py[2 * i + q // 2][:, (q % 2) * D:(q % 2 + 1) * D],
                                                  act[:, i, q * P:(q + 1) * P], ws[s][:, i, WC:], start=True, stop=True)
                        mm.then_inc(y_done, 1)

                with pe.Fori(0, PAIRS // 2) as m:
                    for s in range(2):
                        with pe.Fori(0, B) as g:
                            group(16 * m + 8 * s + 2 * g, g, s, 16 * m + 16)
                with pe.Fori(0, B) as g:
                    group(8 * PAIRS + 2 * g, g, 0, 8 * PAIRS + 16)

            @block.scalar
            def _(a):
                with a.Fori(0, 4 * PAIRS + 4) as g:
                    for i in range(2):
                        a.wait_ge(up_done, 2 * g + (i + 1))
                        nc.scalar.activation(relu[:, i, :], ph[i][:, :], ACT.Relu).then_inc(relu_ready, 1)

            @block.vector
            def _(v):
                def group(unit, g, expert):
                    for i in range(2):
                        v.wait_ge(relu_ready, unit + (i + 1))
                        nc.vector.scalar_tensor_tensor(out=act[:, i, :], in0=ph[i][:, :], scalar=0.0, in1=relu[:, i, :],
                                                       op0=ALU.max, op1=ALU.mult).then_inc(act_ready, 1)
                    for i in range(2):
                        v.wait_ge(y_done, unit + (i + 1))
                        for q in range(NQ):
                            tile = tile_of(acc, g, q)
                            y = py[2 * i + q // 2][:, (q % 2) * D:(q % 2 + 1) * D]
                            v.wait_ge(acc_done, NQ * (unit + i) + (q + 1))
                            if expert is None:
                                nc.vector.tensor_tensor(tile, y, tile, ALU.add).then_inc(acc_done, 1)
                            else:
                                gate = gates[:, bass.ds(g * NQ + q, 1), bass.ds(expert + i, 1)].rearrange("p a e -> p (a e)")
                                nc.vector.scalar_tensor_tensor(out=tile, in0=y, scalar=gate, in1=tile,
                                                               op0=ALU.mult, op1=ALU.add).then_inc(acc_done, 1)

                v.sem_inc(acc_done, NQ)
                nc.vector.memset(acc[:, :, :], 0.0).then_inc(zeroed, 1)
                v.wait_ge(zeroed, 1)
                with v.Fori(0, PAIRS // 2) as m:
                    for s in range(2):
                        with v.Fori(0, B) as g:
                            group(16 * m + 8 * s + 2 * g, g, 4 * m + 2 * s)
                with v.Fori(0, B) as g:
                    group(8 * PAIRS + 2 * g, g, None)


def add_normed_sum(c, name, acc, plus=None):
    nc = c.nc
    with ExitStack() as ctx:
        norm = Norm(c, ctx, name)
        y = ctx.enter_context(nc.sbuf_tensor(f"{name}_y", [P, NQ, D], F32))
        t = ctx.enter_context(nc.sbuf_tensor(f"{name}_t", [P, NQ, D], F32))
        y_ready, t_ready, x_ready = (c.sem(f"{name}_{n}") for n in ("y_ready", "t_ready", "x_ready"))
        block = nc.Block()
        with block:
            @block.vector
            def _(v):
                with v.Fori(0, B) as b:
                    if plus is not None:
                        nc.vector.tensor_tensor(y[:, :, :], acc[:, bass.ds(b * NQ, NQ), :], plus[:, bass.ds(b * NQ, NQ), :],
                                                ALU.add).then_inc(y_ready, 1)
                        v.wait_ge(y_ready, b + 1)

                    def tile(q):
                        return tile_of(acc, b, q) if plus is None else y[:, q, :]

                    norm.statistics(v, b, tile)
                    norm.wait(v, b)
                    add_normed(c, v, norm, b, tile, t, t_ready, x_ready)

            @block.gpsimd
            def _(g):
                with g.Fori(0, B) as b:
                    norm.root(g, b)


def grouped_projection(c, name, a, z, vals, q_dram, k_dram):
    nc = c.nc
    NC = H + KVH
    HALF = P // 2
    with ExitStack() as ctx:
        def sb(n, shape):
            return ctx.enter_context(nc.sbuf_tensor(f"{name}_{n}", shape, F32))

        def sem(n):
            return c.sem(f"{name}_{n}")

        norm_x, norm_z = Norm(c, ctx, name + "_x"), Norm(c, ctx, name + "_z")
        wqk, wv = sb("wqk", [P, KT, NC * P]), sb("wv", [P, KT, KVH * GD])
        col, rope = sb("col", [P, KT]), sb("rope", [P, 2, 2, S])
        h, hT = sb("h", [P, NQ, D]), sb("hT", [P, KT, S])
        xc, xs = sb("xc", [P, 2, S]), sb("xs", [P, 2, S])
        rot = sb("rot", [P, NC, S])
        w_in, z_ready, h_ready, tr_done, hT_ready, v_done, v_kept, qk_done, bank_free, terms, rot_ready, stored, rot_free, spare = (
            sem(n) for n in ("w_in", "z_ready", "h_ready", "tr_done", "hT_ready", "v_done", "v_kept", "qk_done",
                             "bank_free", "terms", "rot_ready", "stored", "rot_free", "carry"))
        tr, ps, pv = c.bank[0:2], c.bank[2:6], c.bank[6:8]
        block = nc.Block()
        with block:
            @block.sync
            def _(sp):
                sp.sem_inc(rot_free, 1)
                for dst, src in ((wqk[:, :, :], weights(a["d_wqk"])), (wv[:, :, :], weights(a["d_wv"])),
                                 (col[:, :], a["d_ln"]), (rope[:, :, :, :], a["d_rope"])):
                    sp.dma_start(dst, src).then_inc(w_in, 16)
                with sp.Fori(0, B) as b:
                    for quad in range(5):
                        sp.wait_ge(rot_ready, b * NC + (4 * quad + 4 + 2))
                        if quad < 4:
                            dst = q_dram[bass.ds(4 * b + quad, 1), :, :, :].rearrange("a p u s -> p (a u) s")
                        else:
                            dst = k_dram[bass.ds(4 * b, 4), :, :, :].rearrange("g p u s -> p (g u) s")
                        sp.dma_start(dst, rot[:, 4 * quad:4 * quad + 4, :]).then_inc(stored, 16)
                    sp.wait_ge(stored, b * 80 + 80)
                    sp.sem_inc(rot_free, 1)

            @block.vector
            def _(v):
                v.wait_ge(w_in, 64)
                with v.Fori(0, B) as b:
                    norm_x.statistics(v, b, lambda q: tile_of(c.x, b, q))
                    norm_x.wait(v, b)
                    for q in range(NQ):
                        norm_x.apply(q, tile_of(z, b, q), tile_of(c.x, b, q)).then_inc(z_ready, 1)
                    v.wait_ge(z_ready, b * NQ + NQ)
                    norm_z.statistics(v, b, lambda q: tile_of(z, b, q), rms=True)
                    norm_z.wait(v, b)
                    v.wait_ge(tr_done, b * KT + KT)
                    for q in range(NQ):
                        norm_z.apply(q, h[:, q, :], tile_of(z, b, q), rms=True).then_inc(h_ready, 1)
                    for cc in range(NC):
                        src, k = ps[cc % 4], cc // H
                        v.wait_ge(qk_done, b * NC + (cc + 1 + NC))
                        v.wait_ge(rot_ready, b * NC + (cc + 1))
                        nc.vector.tensor_tensor(xc[:, cc % 2, :], src[:, :], rope[:, k, 0, :], ALU.mult).then_inc(terms, 1)
                        nc.vector.tensor_tensor(xs[0:HALF, cc % 2, :], src[HALF:P, :], rope[HALF:P, k, 1, :], ALU.mult).then_inc(terms, 1)
                        nc.vector.tensor_tensor(xs[HALF:P, cc % 2, :], src[0:HALF, :], rope[0:HALF, k, 1, :], ALU.mult).then_inc(terms, 1)

            @block.gpsimd
            def _(g):
                g.sem_inc(rot_ready, 2)
                with g.Fori(0, B) as b:
                    norm_x.root(g, b)
                    norm_z.root(g, b, rms=True)
                    for cc in range(NC):
                        g.wait_ge(terms, b * 3 * NC + 3 * (cc + 1))
                        if cc == 0:
                            g.wait_ge(rot_free, b + 1)
                        g.tensor_tensor(rot[:, cc, :], xc[:, cc % 2, :], xs[:, cc % 2, :], ALU.add).then_inc(rot_ready, 1)

            @block.scalar
            def _(s):
                s.wait_ge(w_in, 64)
                with s.Fori(0, B) as b:
                    for k in range(KT):
                        s.wait_ge(tr_done, b * KT + (k + 1 + KT))
                        s.wait_ge(qk_done, b * NC + NC)
                        nc.scalar.activation(hT[:, k, :], tr[k][:, :], ACT.Copy, scale=col[:, k:k + 1]).then_inc(hT_ready, 1)
                    for q in range(NQ):
                        s.wait_ge(v_done, b * NQ + (q + 1))
                        hold(s, spare)
                        nc.scalar.copy(vals[:, bass.ds(b * KVH, KVH), q, :],
                                       pv[q % 2][:, :].rearrange("p (g d) -> p g d", d=GD)).then_inc(v_kept, 1)

            @block.tensor
            def _(pe):
                pe.sem_inc(tr_done, KT)
                pe.sem_inc(qk_done, NC)
                pe.wait_ge(w_in, 64)
                with pe.Fori(0, B) as b:
                    for k in range(KT):
                        for q in range(NQ):
                            if k == 0:
                                pe.wait_ge(h_ready, b * NQ + (q + 1))
                            mm = nc.tensor.transpose(tr[k][:, q * P:(q + 1) * P], h[:, q, k * P:(k + 1) * P], c.ident[:, :])
                        mm.then_inc(tr_done, 1)
                    pe.wait_ge(hT_ready, b * KT + KT)
                    for q in range(NQ):
                        if q >= 2:
                            pe.wait_ge(v_kept, b * NQ + (q - 1))
                        for k in range(KT):
                            mm = nc.tensor.matmul(pv[q % 2][:, :], hT[:, k, q * P:(q + 1) * P], wv[:, k, :],
                                                  start=(k == 0), stop=(k == KT - 1))
                        mm.then_inc(v_done, 1)
                    for cc in range(NC):
                        if cc >= 4:
                            pe.wait_ge(terms, b * 3 * NC + 3 * (cc - 3))
                        for k in range(KT):
                            mm = nc.tensor.matmul(ps[cc % 4][:, :], wqk[:, k, cc * P:(cc + 1) * P], hT[:, k, :],
                                                  start=(k == 0), stop=(k == KT - 1))
                        mm.then_inc(qk_done, 1)


def grouped_output(c, name, o_dram, w_out, z):
    nc = c.nc
    with ExitStack() as ctx:
        def sb(n, shape):
            return ctx.enter_context(nc.sbuf_tensor(f"{name}_{n}", shape, F32))

        def sem(n):
            return c.sem(f"{name}_{n}")

        w = sb("w", [P, H, D])
        o = [sb(f"o{i}", [P, H, GD]) for i in range(2)]
        oT = sb("oT", [P, H, P])
        w_in, tr_done, oT_ready, y_done, z_ready = (sem(n) for n in ("w_in", "tr_done", "oT_ready", "y_done", "z_ready"))
        loaded = [sem("loaded0"), sem("loaded1")]
        tr, py = c.bank[0:4], c.bank[4:6]
        block = nc.Block()
        with block:
            @block.sync
            def _(sp):
                sp.dma_start(w[:, :, :], w_out.rearrange("(h p) n -> p h n", p=P)).then_inc(w_in, 16)
                with sp.Fori(0, B) as b:
                    for q in range(NQ):
                        sp.wait_ge(tr_done, 4 * (b * NQ + (q + 1)))
                        for i in range(4):
                            sp.dma_start(o[q % 2][:, 4 * i:4 * i + 4, :], o_dram[bass.ds(b * H + 4 * i, 4), q * P:(q + 1) * P, :].rearrange(
                                "h p d -> p h d")).then_inc(loaded[q % 2], 16)

            @block.tensor
            def _(pe):
                pe.sem_inc(tr_done, 8)
                pe.wait_ge(w_in, 16)
                with pe.Fori(0, B) as b:
                    for q in range(NQ):
                        pe.wait_ge(loaded[q % 2], 128 * b + 64 * (q // 2 + 1))
                        for h in range(H):
                            mm = nc.tensor.transpose(tr[h // 4][:, (h % 4) * P:(h % 4 + 1) * P], o[q % 2][:, h, :], c.ident[:, :])
                            if h % 4 == 3:
                                mm.then_inc(tr_done, 1)
                        pe.wait_ge(z_ready, b * NQ + (q + 1))
                        for h in range(H):
                            if h % 4 == 0:
                                pe.wait_ge(oT_ready, 4 * (b * NQ + q) + (h // 4 + 1))
                            mm = nc.tensor.matmul(py[q % 2][:, 0:D], oT[:, h, :], w[:, h, :], start=(h == 0), stop=(h == H - 1))
                        mm.then_inc(y_done, 1)

            @block.scalar
            def _(s):
                with s.Fori(0, B) as b:
                    for q in range(NQ):
                        for i in range(4):
                            s.wait_ge(tr_done, 4 * (b * NQ + q) + (i + 9))
                            nc.scalar.copy(oT[:, 4 * i:4 * i + 4, :].rearrange("p h t -> p (h t)"), tr[i][:, :]).then_inc(oT_ready, 1)

            @block.vector
            def _(v):
                v.sem_inc(z_ready, 2)
                with v.Fori(0, B) as b:
                    for q in range(NQ):
                        v.wait_ge(y_done, b * NQ + (q + 1))
                        nc.vector.tensor_tensor(tile_of(z, b, q), py[q % 2][:, 0:D], tile_of(z, b, q), ALU.add).then_inc(z_ready, 1)


def softmax_gates(c, name, logits, iota, gates):
    nc = c.nc
    K = 2
    with ExitStack() as ctx:
        def sb(n, shape, dt=F32):
            return ctx.enter_context(nc.sbuf_tensor(f"{name}_{n}", shape, dt))

        top, idx, idxf = sb("top", [P, NT, 8]), sb("idx", [P, NT, 8], U32), sb("idxf", [P, NT, 8])
        diff, ex, den, pair = sb("diff", [P, NT]), sb("ex", [P, NT]), sb("den", [P, NT]), sb("pair", [P, NT, K])
        eq = sb("eq", [P, NT, E1, K])
        diff_ready, ex_ready, step = (c.sem(f"{name}_{n}") for n in ("diff", "ex", "step"))
        block = nc.Block()
        with block:
            @block.scalar
            def _(a):
                a.wait_ge(diff_ready, 1)
                nc.scalar.activation(ex[:, :], diff[:, :], ACT.Exp).then_inc(ex_ready, 1)

            @block.vector
            def _(v):
                nv = nc.vector
                link = Chain(v, step).link
                for t in range(NT):
                    ins = nv.max(top[:, t, :], logits[:, t, :])
                link(ins)
                nv.tensor_tensor(diff[:, :], top[:, :, 1], top[:, :, 0], ALU.subtract).then_inc(diff_ready, 1)
                for t in range(NT):
                    ins = nv.max_index(idx[:, t, :], top[:, t, :], logits[:, t, :])
                link(ins)
                link(nv.tensor_copy(idxf[:, :, :], idx[:, :, :]))
                v.wait_ge(ex_ready, 1)
                link(nv.tensor_scalar(den[:, :], ex[:, :], 1.0, None, ALU.add))
                link(nv.reciprocal(pair[:, :, 0], den[:, :]))
                link(nv.tensor_tensor(pair[:, :, 1], pair[:, :, 0], ex[:, :], ALU.mult))
                link(nv.tensor_tensor(eq[:, :, :, :], idxf[:, :, 0:K].unsqueeze(2).to_broadcast([P, NT, E1, K]),
                                      iota[:, 0:E1].unsqueeze(1).unsqueeze(3).to_broadcast([P, NT, E1, K]), ALU.is_equal))
                link(nv.tensor_tensor(eq[:, :, :, :], eq[:, :, :, :], pair[:, :, :].unsqueeze(2).to_broadcast([P, NT, E1, K]), ALU.mult))
                link(nv.tensor_reduce(gates[:, :, :], eq[:, :, :, :], AX.X, ALU.add))


def swiglu_experts(c, name, hT, gates, w, acc):
    nc = c.nc
    WU, WF = KT * 2 * F1, KT * 2 * F1 + FC1 * D
    with ExitStack() as ctx:
        def sb(n, shape):
            return ctx.enter_context(nc.sbuf_tensor(f"{name}_{n}", shape, F32))

        def sem(n):
            return c.sem(f"{name}_{n}")

        ws = [sb(f"w{s}", [P, WF]) for s in range(2)]
        silu, act = sb("silu", [P, 2, S]), sb("act", [P, FC1, S])
        loaded = [sem("loaded0"), sem("loaded1")]
        up_done, silu_ready, act_ready, y_done, acc_done, zeroed = (
            sem(n) for n in ("up", "silu", "act", "y", "acc", "zeroed"))
        ph, py = c.bank[0:4], c.bank[4:6]
        block = nc.Block()
        with block:
            @block.sync
            def _(sp):
                def load(e, s):
                    sp.dma_start(ws[s][:, :], w[bass.ds(e, 1), :, :].rearrange("a p n -> p (a n)")).then_inc(loaded[s], 16)

                load(0, 0)
                load(1, 1)
                with sp.Fori(1, E1 // 2) as m:
                    for s in range(2):
                        sp.wait_ge(y_done, 8 * m + (4 * s - 4))
                        load(2 * m + s, s)

            @block.tensor
            def _(pe):
                def group(m, s, g):
                    n = 8 * m + 4 * s + g
                    up, down = ws[s][:, 0:WU].rearrange("p (k i f) -> p k i f", k=KT, i=2), ws[s][:, WU:].rearrange("p (f n) -> p f n", n=D)
                    pe.wait_ge(loaded[s], 16 * m + 16)
                    for f in range(FC1):
                        if f >= 2:
                            pe.wait_ge(act_ready, n * FC1 + (f - 1))
                        for i in range(2):
                            for k in range(KT):
                                mm = nc.tensor.matmul(ph[2 * (f % 2) + i][:, :], up[:, k, i, f * P:(f + 1) * P],
                                                      hT[:, k, bass.ds(g * S, S)], start=(k == 0), stop=(k == KT - 1))
                        mm.then_inc(up_done, 1)
                    for q in range(NQ):
                        for f in range(FC1):
                            if q == 0:
                                pe.wait_ge(act_ready, n * FC1 + (f + 1))
                            mm = nc.tensor.matmul(py[q // 2][:, (q % 2) * D:(q % 2 + 1) * D], act[:, f, q * P:(q + 1) * P],
                                                  down[:, f, :], start=(f == 0), stop=(f == FC1 - 1))
                    mm.then_inc(y_done, 1)

                with pe.Fori(0, E1 // 2) as m:
                    for s in range(2):
                        with pe.Fori(0, B) as g:
                            group(m, s, g)

            @block.scalar
            def _(a):
                with a.Fori(0, E1 * B) as n:
                    for f in range(FC1):
                        a.wait_ge(up_done, n * FC1 + (f + 1))
                        nc.scalar.activation(silu[:, f % 2, :], ph[2 * (f % 2)][:, :], ACT.Silu).then_inc(silu_ready, 1)

            @block.vector
            def _(v):
                nc.vector.memset(acc[:, :, :], 0.0).then_inc(zeroed, 1)
                v.wait_ge(zeroed, 1)
                with v.Fori(0, E1) as e:
                    with v.Fori(0, B) as g:
                        n = 4 * e + g
                        for f in range(FC1):
                            v.wait_ge(silu_ready, n * FC1 + (f + 1))
                            nc.vector.tensor_tensor(act[:, f, :], ph[2 * (f % 2) + 1][:, :], silu[:, f % 2, :], ALU.mult).then_inc(act_ready, 1)
                        v.wait_ge(y_done, n + 1)
                        for q in range(NQ):
                            gate = gates[:, bass.ds(g * NQ + q, 1), bass.ds(e, 1)].rearrange("p a e -> p (a e)")
                            nc.vector.scalar_tensor_tensor(out=tile_of(acc, g, q), in0=py[q // 2][:, (q % 2) * D:(q % 2 + 1) * D],
                                                           scalar=gate, in1=tile_of(acc, g, q), op0=ALU.mult, op1=ALU.add).then_inc(acc_done, 1)


def build(nc, a, out):
    with ExitStack() as ctx:
        c = Core(nc, ctx)
        iota = c.sb("iota", [P, E0], F32)
        load_constants(c, a, iota)
        q_parts = nc.dram_tensor("q_parts", [3, QUADS, 4 * HD, S], BF16, kind="Internal").ap()
        k_parts = nc.dram_tensor("k_parts", [3, QUADS, 4 * HD, S], BF16, kind="Internal").ap()

        with ExitStack() as stage:
            vals = stage.enter_context(nc.sbuf_tensor("a_vals", [P, B * H, NQ, HD], F32))
            attended = stage.enter_context(nc.sbuf_tensor("a_attended", [P, B * H, NQ, HD], F32))
            narrow_projection(c, "a_in", a["a_wqk"], a["a_wv"], a["a_bqk"], a["a_bv"], None, q_parts, k_parts, vals)
            attention(c, "a_att", q_parts, k_parts, vals, attended, narrow=True, causal=True)
            narrow_output(c, "a_out", attended, a["a_wout"], a["a_bout"], 1.0)
        c.end_stage()

        with ExitStack() as stage:
            def sb(n, shape):
                return stage.enter_context(nc.sbuf_tensor(n, shape, F32))

            hT, logits, gates, acc = sb("b_hT", [P, KT, T]), sb("b_lg", [P, NT, E0]), sb("b_gates", [P, NT, E0]), sb("b_acc", [P, NT, D])
            router_input(c, "b_in", c.x, False, None, a["b_wr"], a["b_br"], E0, hT, logits)
            sigmoid_gates(c, "b_gate", logits, iota, gates)
            relu2_experts(c, "b_moe", hT, gates, a["b_w"], acc)
            add_normed_sum(c, "b_out", acc)
        c.end_stage()

        with ExitStack() as stage:
            vals = stage.enter_context(nc.sbuf_tensor("c_vals", [P, B * H, NQ, HD], F32))
            attended = stage.enter_context(nc.sbuf_tensor("c_attended", [P, B * H, NQ, HD], F32))
            lambdas = {"vectors": a["c_lambdas"], "halves": a["c_halves"]}
            narrow_projection(c, "c_in", a["c_wqk"], a["c_wv"], None, None, lambdas, q_parts, k_parts, vals)
            attention(c, "c_att", q_parts, k_parts, vals, attended, narrow=True, causal=False)
            narrow_output(c, "c_out", attended, a["c_wout"], None, 1.0 - LAMBDA_INIT)
        c.end_stage()

        q_dram = nc.dram_tensor("q_dram", [QUADS, P, 4, S], F32, kind="Internal").ap()
        k_dram = nc.dram_tensor("k_dram", [QUADS, P, 1, S], F32, kind="Internal").ap()
        o_dram = nc.dram_tensor("o_dram", [B * H, S, GD], F32, kind="Internal").ap()
        z = c.sb("z", [P, NT, D], F32)
        with ExitStack() as stage:
            vals = stage.enter_context(nc.sbuf_tensor("d_vals", [P, QUADS, NQ, GD], F32))
            grouped_projection(c, "d_in", a, z, vals, q_dram, k_dram)
            attention(c, "d_att", q_dram, k_dram, vals, o_dram, narrow=False, causal=True)
            grouped_output(c, "d_out", o_dram, a["d_wo"], z)
        c.end_stage()
        with ExitStack() as stage:
            def sb(n, shape):
                return stage.enter_context(nc.sbuf_tensor(n, shape, F32))

            hT, logits, gates, acc = sb("e_hT", [P, KT, T]), sb("e_lg", [P, NT, E1]), sb("e_gates", [P, NT, E1]), sb("e_acc", [P, NT, D])
            router_input(c, "e_in", z, True, a["e_ln"], a["e_wr"], None, E1, hT, logits)
            softmax_gates(c, "e_gate", logits, iota, gates)
            swiglu_experts(c, "e_moe", hT, gates, a["e_w"], acc)
            add_normed_sum(c, "e_out", acc, z)
        c.end_stage()

        done = c.sem("done")
        with nc.Block() as block:
            @block.sync
            def _(sp):
                sp.dma_start(out.rearrange("b (q p) d -> p (b q) d", p=P), c.x[:, :, :]).then_inc(done, 16)
                sp.wait_ge(done, 16)


def laid_out(i):
    import numpy as np
    i = {k: np.asarray(v) for k, v in i.items()}
    r = np.arange(P)
    wa, wc = i["L0_attn_W_qkv"], i["L1_attn_W_attn"]
    half = HD // 2
    pair = [wc[:, j * D // 2:(j + 1) * D // 2].reshape(D, H, half) for j in range(4)]
    w1 = np.concatenate([i["L0_ffn_W1"], i["L0_ffn_Ws1"].reshape(2, M0, D)])
    w2 = np.concatenate([i["L0_ffn_W2"], i["L0_ffn_Ws2"].reshape(D, 2, M0).transpose(1, 0, 2)])
    w1 = w1.transpose(0, 2, 1).reshape(E0 + 2, KT, P, M0).transpose(0, 2, 1, 3).reshape(E0 + 2, P, KT * M0)
    b_w = np.concatenate([w1, w2.transpose(0, 2, 1)], axis=2)
    evens_first = np.concatenate([np.arange(0, GD, 2), np.arange(1, GD, 2)])
    wq = i["L1_ffn_wq"].reshape(D, H, GD)[:, :, evens_first].reshape(D, H * GD)
    wk = i["L1_ffn_wk"].reshape(D, KVH, GD)[:, :, evens_first].reshape(D, KVH * GD)
    inv_freq = np.float32(1e6) ** (-np.arange(0, GD, 2, dtype=np.float32) / np.float32(GD))
    angle = (np.arange(S, dtype=np.float32)[:, None] * inv_freq[None, :]).T.astype(np.float64)
    rope = np.stack([np.concatenate([np.cos(angle), np.cos(angle)]),
                     np.concatenate([np.sin(angle), -np.sin(angle)])], axis=1)
    rope = np.stack([rope / np.sqrt(GD), rope], axis=1).astype(np.float32)
    e_up = np.stack([i["L1_ffn_w1"], i["L1_ffn_w3"]], axis=2)
    e_up = e_up.reshape(E1, KT, P, 2 * F1).transpose(0, 2, 1, 3).reshape(E1, P, KT * 2 * F1)
    e_down = i["L1_ffn_w2"].reshape(E1, FC1, P, D).transpose(0, 2, 1, 3).reshape(E1, P, FC1 * D)
    return {
        "d_wqk": np.concatenate([wq, wk], axis=1), "d_wv": i["L1_ffn_wv"], "d_wo": i["L1_ffn_wo"],
        "d_ln": i["L1_ffn_ln_w"].reshape(KT, P).T, "d_rope": rope,
        "e_ln": i["L1_ffn_ff_ln_w"].reshape(KT, P).T, "e_wr": i["L1_ffn_gate_w"],
        "e_w": np.concatenate([e_up, e_down], axis=2),
        "x": i["L0_attn_x"],
        "ident": np.eye(P, dtype=np.float32),
        "causal": np.where(r[None, :] <= r[:, None], 0.0, -1e38).astype(np.float32),
        "iota": np.arange(E0, dtype=np.float32),
        "a_wqk": wa[:, :2 * D], "a_wv": wa[:, 2 * D:], "a_bqk": i["L0_attn_b_qkv"][:2 * D].reshape(4, P).T,
        "a_bv": i["L0_attn_b_qkv"][2 * D:], "a_wout": i["L0_attn_W_out"], "a_bout": i["L0_attn_b_out"],
        "b_wr": i["L0_ffn_Wr"].T, "b_br": i["L0_ffn_br"],
        "b_w": b_w.reshape(E0 // 2 + 1, 2, P, KT * M0 + D).transpose(0, 2, 1, 3),
        "c_wqk": np.concatenate([np.concatenate([pair[j], pair[j + 2]], axis=2).reshape(D, D) for j in range(2)], axis=1),
        "c_wv": wc[:, 2 * D:], "c_wout": i["L1_attn_W_proj"],
        "c_lambdas": np.stack([i[f"L1_attn_lambda_{n}"] for n in ("q1", "k1", "q2", "k2")]),
        "c_halves": np.stack([-(r % HD >= half).astype(np.float32), (r % HD < half).astype(np.float32)], axis=1),
    }


def kernel(**inputs):
    import numpy as _np
    import concourse.bacc as _bacc
    from concourse import mybir as _mybir
    from concourse.bass_utils import run_bass_kernel_spmd as _run

    nc = _bacc.Bacc("TRN2", target_bir_lowering=False, num_devices=1)
    arrays, args = {}, {}
    for name, a in laid_out(inputs).items():
        a = _np.ascontiguousarray(a)
        arrays[f"in_{name}"] = a
        args[name] = nc.dram_tensor(f"in_{name}", a.shape, _mybir.dt.from_np(a.dtype), kind="ExternalInput").ap()
    out = nc.dram_tensor("out", (B, S, D), F32, kind="ExternalOutput").ap()
    build(nc, args, out)
    return _run(nc, [arrays], core_ids=[0]).results[0]["out"]
```

```python
from contextlib import ExitStack

import concourse.bass as bass
from concourse import mybir

F32 = mybir.dt.float32
F32R = mybir.dt.float32r
BF16 = mybir.dt.bfloat16
U32 = mybir.dt.uint32
I32 = mybir.dt.int32
ALU = mybir.AluOpType
ACT = mybir.ActivationFunctionType
AX = mybir.AxisListType

P = 128
B, S, D = 4, 512, 256
KT = D // P
NQ = S // P
NT = B * NQ
T = B * S
H = 16
QUADS = B * H // 4
HD = D // H
GD, KVH = 128, 4
EPS = 1e-5
LAMBDA_INIT = 0.8 - 0.6
E0, K0, M0, G0, SCALE0 = 32, 6, 128, 8, 2.5
E1, F1 = 8, 896
FC1 = F1 // P
SLOTS = 256
BLOCKS = (2 * T - E1) // SLOTS + E1

Q_PART = [0, 0, 0, 1, 1, 1, 2, 2]
K_PART = [0, 1, 2, 0, 1, 2, 0, 1]


class Core:

    def __init__(self, nc, ctx):
        self.nc, self.ctx, self.sems = nc, ctx, []
        self.x = self.sb("x", [P, NT, D], F32)
        self.ident = self.sb("ident", [P, P], F32)
        self.identb = self.sb("identb", [P, P], BF16)
        self.causal = self.sb("causal", [P, P], BF16)
        self.mhalf = self.sb("mhalf", [P, NQ], F32)
        self.bank = [ctx.enter_context(nc.psum_tensor(f"bank{i}", [P, 512], F32)) for i in range(8)]

    def sb(self, name, shape, dt):
        return self.ctx.enter_context(self.nc.sbuf_tensor(name, shape, dt))

    def sem(self, name):
        self.sems.append(self.nc.alloc_semaphore(name))
        return self.sems[-1]

    def end_stage(self):
        self.nc.clear_and_free_semaphores(self.sems)
        self.nc.all_engine_barrier()
        self.sems = []


def weights(ap):
    return ap.rearrange("(k p) n -> p k n", p=P)


def hold(eng, spare):
    eng.sem_inc(spare, 1)


class Norm:

    def __init__(self, c, ctx, name):
        nc = c.nc

        def sb(n, shape):
            return ctx.enter_context(nc.sbuf_tensor(f"{name}_{n}", shape, F32))

        self.c = c
        self.st, self.mv = sb("st", [P, NQ, 6]), sb("mv", [P, NQ, 2])
        self.ve, self.r = sb("ve", [P, NQ]), sb("r", [P, NQ])
        self.stats_done, self.mean_done, self.var_done, self.root_done, self.spare = (
            c.sem(f"{name}_{n}") for n in ("stats", "mean", "var", "root", "carry"))

    def statistics(self, v, b, tile, rms=False):
        nv = self.c.nc.vector
        hold(v, self.spare)
        for q in range(NQ):
            nv.bn_stats(self.st[:, q, :], tile(q)).then_inc(self.stats_done, 1)
        v.wait_ge(self.stats_done, b * NQ + NQ)
        hold(v, self.spare)
        for q in range(NQ):
            nv.bn_aggr(self.mv[:, q, :], self.st[:, q, :]).then_inc(self.mean_done, 1)
        v.wait_ge(self.mean_done, b * NQ + NQ)
        if rms:
            nv.tensor_tensor(self.ve[:, :], self.mv[:, :, 0], self.mv[:, :, 0], ALU.mult).then_inc(self.var_done, 1)
            v.wait_ge(self.var_done, b * 2 + 1)
            nv.scalar_tensor_tensor(out=self.ve[:, :], in0=self.mv[:, :, 1], scalar=EPS, in1=self.ve[:, :],
                                    op0=ALU.add, op1=ALU.add).then_inc(self.var_done, 1)
        else:
            nv.tensor_scalar(self.ve[:, :], self.mv[:, :, 1], EPS, None, ALU.add).then_inc(self.var_done, 1)

    def root(self, g, b, rms=False):
        g.wait_ge(self.var_done, b * (1 + rms) + 1 + rms)
        g.tensor_tensor(self.r[:, :], self.ve[:, :], self.c.mhalf[:, :], ALU.pow).then_inc(self.root_done, 1)

    def wait(self, v, b):
        v.wait_ge(self.root_done, b + 1)

    def apply(self, q, out, tile, rms=False):
        nv = self.c.nc.vector
        if rms:
            return nv.tensor_scalar(out, tile, self.r[:, q:q + 1], None, ALU.mult)
        return nv.tensor_scalar(out, tile, self.mv[:, q, 0:1], self.r[:, q:q + 1], ALU.subtract, ALU.mult)


def tile_of(x, b, q):
    return x[:, bass.ds(b * NQ + q, 1), :].rearrange("p a d -> p (a d)")


def load_constants(c, a, iota, before):
    nc = c.nc
    x_in, mask_in, cast = c.sem("x_in"), c.sem("mask_in"), c.sem("cast")
    with ExitStack() as ctx:
        mask = ctx.enter_context(nc.sbuf_tensor("mask", [P, P], F32))
        block = nc.Block()
        with block:
            @block.sync
            def _(sp):
                sp.dma_start(c.ident[:, :], a["ident"]).then_inc(mask_in, 16)
                sp.dma_start(mask[:, :], a["causal"]).then_inc(mask_in, 16)
                sp.dma_start(before[:, :], a["before"]).then_inc(mask_in, 16)
                sp.dma_start(iota[:, :], a["iota"].partition_broadcast(P)).then_inc(mask_in, 16)
                sp.dma_start(c.x[:, :, :], a["x"].rearrange("b (q p) d -> p (b q) d", p=P)).then_inc(x_in, 16)
                sp.wait_ge(x_in, 16)

            @block.vector
            def _(v):
                v.wait_ge(mask_in, 64)
                nc.vector.tensor_copy(c.identb[:, :], c.ident[:, :]).then_inc(cast, 1)
                nc.vector.tensor_copy(c.causal[:, :], mask[:, :]).then_inc(cast, 1)

            @block.gpsimd
            def _(g):
                g.memset(c.mhalf[:, :], -0.5)


def narrow_projection(c, name, w_qk, w_v, b_qk, b_v, lambdas, q_parts, k_parts, vals):
    nc = c.nc
    with ExitStack() as ctx:
        def sb(n, shape, dt=F32):
            return ctx.enter_context(nc.sbuf_tensor(f"{name}_{n}", shape, dt))

        def sem(n):
            return c.sem(f"{name}_{n}")

        norm = Norm(c, ctx, name)
        wqk, wv = sb("wqk", [P, KT, 512]), sb("wv", [P, KT, D])
        biasqk, biasv = sb("bqk", [P, 4]), sb("bv", [P, D])
        mul = sb("mul", [P, 2])
        h = sb("h", [P, NQ, D])
        hT = sb("hT", [P, KT, S])
        xp = sb("xp", [P, 4, S])
        r1 = sb("r1", [P, 4, S])
        parts = sb("parts", [P, 4, 3, S], BF16)
        w_in, mul_ready = sem("w_in"), sem("mul_ready")
        h_ready, tr_done, hT_ready = sem("h_ready"), sem("tr_done"), sem("hT_ready")
        qk_done, v_done, v_kept = sem("qk_done"), sem("v_done"), sem("v_kept")
        xp_ready, hi_ready, r1_ready, mid_ready, lo_ready = (
            sem(n) for n in ("xp_ready", "hi_ready", "r1_ready", "mid_ready", "lo_ready"))
        stored, parts_free = sem("stored"), sem("parts_free")
        tr, ps, pv = c.bank[0:2], c.bank[2:6], c.bank[6:8]
        n_w = 2 + 2 * (lambdas is None)
        if lambdas is not None:
            lam_in, lam_ex, lam_sem, lam_exp = sb("lam_in", [P, 4, D]), sb("lam_ex", [P, 8]), sem("lam"), sem("lam_exp")
            halves = sb("halves", [P, 2])
            n_w = 4
        block = nc.Block()
        with block:
            @block.sync
            def _(sp):
                sp.sem_inc(parts_free, 1)
                sp.dma_start(wqk[:, :, :], weights(w_qk)).then_inc(w_in, 16)
                sp.dma_start(wv[:, :, :], weights(w_v)).then_inc(w_in, 16)
                if lambdas is None:
                    sp.dma_start(biasqk[:, :], b_qk).then_inc(w_in, 16)
                    sp.dma_start(biasv[:, :], b_v.partition_broadcast(P)).then_inc(w_in, 16)
                else:
                    sp.dma_start(lam_in[:, :, :], lambdas["vectors"].partition_broadcast(P)).then_inc(w_in, 16)
                    sp.dma_start(halves[:, :], lambdas["halves"]).then_inc(w_in, 16)
                with sp.Fori(0, B) as b:
                    for cc in range(4):
                        dst = (q_parts if cc < 2 else k_parts)[:, bass.ds(b * 4 + 2 * (cc % 2), 2), :, :]
                        sp.wait_ge(lo_ready, b * 4 + cc + 1)
                        sp.dma_start(dst.rearrange("t g r s -> (g r) t s"), parts[:, cc, :, :]).then_inc(stored, 16)
                    sp.wait_ge(stored, b * 64 + 64)
                    sp.sem_inc(parts_free, 1)

            @block.vector
            def _(v):
                v.wait_ge(w_in, 16 * n_w)
                if lambdas is None:
                    nc.vector.memset(mul[:, 0:1], HD ** -0.5).then_inc(mul_ready, 1)
                    nc.vector.memset(mul[:, 1:2], 1.0).then_inc(mul_ready, 1)
                    v.wait_ge(mul_ready, 2)
                else:
                    half_scale = (HD // 2) ** -0.5
                    for i in range(2):
                        nc.vector.tensor_tensor_reduce(lam_in[:, 2 * i, :], lam_in[:, 2 * i, :], lam_in[:, 2 * i + 1, :],
                                                       1.0, 0.0, ALU.mult, ALU.add, lam_ex[:, i:i + 1]).then_inc(lam_sem, 1)
                    v.wait_ge(lam_exp, 1)
                    nc.vector.tensor_tensor(lam_ex[:, 4:5], lam_ex[:, 2:3], lam_ex[:, 3:4], ALU.subtract).then_inc(lam_sem, 1)
                    v.wait_ge(lam_sem, 3)
                    nc.vector.tensor_scalar(lam_ex[:, 5:6], lam_ex[:, 4:5], LAMBDA_INIT, None, ALU.add).then_inc(lam_sem, 1)
                    v.wait_ge(lam_sem, 4)
                    nc.vector.tensor_scalar(mul[:, 1:2], halves[:, 0:1], lam_ex[:, 5:6], halves[:, 1:2],
                                            ALU.mult, ALU.add).then_inc(mul_ready, 1)
                    nc.vector.memset(mul[:, 0:1], half_scale).then_inc(mul_ready, 1)
                    nc.vector.memset(biasqk[:, :], 0.0).then_inc(mul_ready, 1)
                    v.wait_ge(mul_ready, 3)

                def apply(b):
                    norm.wait(v, b)
                    v.wait_ge(tr_done, b * KT + 2)
                    for q in range(NQ):
                        norm.apply(q, h[:, q, :], tile_of(c.x, b, q)).then_inc(h_ready, 1)

                def group(b, last):
                    if not last:
                        norm.statistics(v, b + 1, lambda q: tile_of(c.x, b + 1, q))
                    for cc in range(4):
                        v.wait_ge(qk_done, b * 4 + cc + 1)
                        nc.vector.tensor_scalar(xp[:, cc, :], ps[cc][:, :], biasqk[:, cc:cc + 1],
                                                mul[:, cc // 2:cc // 2 + 1], ALU.add, ALU.mult).then_inc(xp_ready, 1)
                    if not last:
                        apply(b + 1)
                    for q in range(NQ):
                        v.wait_ge(v_done, b * 2 + q // 2 + 3)
                        dst = vals[:, bass.ds(b * H, H), q, :]
                        src = pv[q // 2][:, (q % 2) * D:(q % 2 + 1) * D].rearrange("p (h d) -> p h d", d=HD)
                        if lambdas is None:
                            nc.vector.tensor_tensor(dst, src, biasv[:, :].rearrange("p (h d) -> p h d", d=HD),
                                                    ALU.add).then_inc(v_kept, 1)
                        else:
                            nc.vector.tensor_copy(dst, src).then_inc(v_kept, 1)
                    for cc in range(4):
                        v.wait_ge(hi_ready, b * 4 + cc + 1)
                        nc.vector.tensor_tensor(r1[:, cc, :], xp[:, cc, :], parts[:, cc, 0, :], ALU.subtract).then_inc(r1_ready, 1)
                    for cc in range(4):
                        v.wait_ge(mid_ready, b * 4 + cc + 1)
                        v.wait_ge(r1_ready, b * 4 + cc + 1)
                        nc.vector.tensor_tensor(parts[:, cc, 2, :], r1[:, cc, :], parts[:, cc, 1, :], ALU.subtract).then_inc(lo_ready, 1)

                norm.statistics(v, 0, lambda q: tile_of(c.x, 0, q))
                apply(0)
                with v.Fori(0, B - 1) as b:
                    group(b, False)
                group(B - 1, True)

            @block.gpsimd
            def _(g):
                with g.Fori(0, B) as b:
                    norm.root(g, b)

            @block.scalar
            def _(a):
                if lambdas is not None:
                    a.wait_ge(lam_sem, 2)
                    nc.scalar.activation(lam_ex[:, 2:4], lam_ex[:, 0:2], ACT.Exp).then_inc(lam_exp, 1)

                def keep_hT(b):
                    for k in range(KT):
                        a.wait_ge(tr_done, b * KT + k + 3)
                        if k == 0:
                            a.wait_ge(v_done, b * 2 + 2)
                        nc.scalar.copy(hT[:, k, :], tr[k][:, :]).then_inc(hT_ready, 1)

                def group(b, last):
                    for cc in range(4):
                        if cc == 0:
                            a.wait_ge(parts_free, b + 1)
                        a.wait_ge(xp_ready, b * 4 + cc + 5)
                        nc.scalar.copy(parts[:, cc, 0, :], xp[:, cc, :]).then_inc(hi_ready, 1)
                    if not last:
                        keep_hT(b + 1)
                    for cc in range(4):
                        a.wait_ge(r1_ready, b * 4 + cc + 1)
                        nc.scalar.copy(parts[:, cc, 1, :], r1[:, cc, :]).then_inc(mid_ready, 1)

                keep_hT(0)
                with a.Fori(0, B - 1) as b:
                    group(b, False)
                group(B - 1, True)

            @block.tensor
            def _(pe):
                def turn(b):
                    for k in range(KT):
                        for q in range(NQ):
                            if k == 0:
                                pe.wait_ge(h_ready, b * NQ + q + 1)
                            mm = nc.tensor.transpose(tr[k][:, q * P:(q + 1) * P], h[:, q, k * P:(k + 1) * P], c.ident[:, :])
                        mm.then_inc(tr_done, 1)

                def group(b, last):
                    pe.wait_ge(hT_ready, b * KT + KT)
                    for cc in range(4):
                        pe.wait_ge(xp_ready, b * 4 + cc + 1)
                        for k in range(KT):
                            mm = nc.tensor.matmul(ps[cc][:, :], wqk[:, k, cc * P:(cc + 1) * P], hT[:, k, :],
                                                  start=(k == 0), stop=(k == KT - 1))
                        mm.then_inc(qk_done, 1)
                    for q in range(NQ):
                        if q % 2 == 0:
                            pe.wait_ge(v_kept, b * 4 + q + 2)
                        for k in range(KT):
                            mm = nc.tensor.matmul(pv[q // 2][:, (q % 2) * D:(q % 2 + 1) * D], hT[:, k, q * P:(q + 1) * P],
                                                  wv[:, k, :], start=(k == 0), stop=(k == KT - 1))
                        if q % 2:
                            mm.then_inc(v_done, 1)
                    if not last:
                        turn(b + 1)

                pe.sem_inc(tr_done, KT)
                pe.sem_inc(v_done, 2)
                pe.sem_inc(xp_ready, 4)
                pe.sem_inc(v_kept, 4)
                pe.wait_ge(w_in, 16 * n_w)
                turn(0)
                with pe.Fori(0, B - 1) as b:
                    group(b, False)
                group(B - 1, True)


def attention(c, name, q_src, k_src, vals, out, narrow, causal):
    nc = c.nc
    W = HD if narrow else GD
    dt = BF16 if narrow else F32
    kh = 4 if narrow else 1
    loads = 16 if narrow else 2
    width = [(qt + 1) * P if causal else S for qt in range(NQ)]
    STEPS = B * H
    with ExitStack() as ctx:
        def sb(n, shape, d=F32):
            return ctx.enter_context(nc.sbuf_tensor(f"{name}_{n}", shape, d))

        def sem(n):
            return c.sem(f"{name}_{n}")

        qs = [sb(f"q{s}", [P, 4, S], dt) for s in range(2)]
        ks = [sb(f"k{s}", [P, kh, S], dt) for s in range(2)]
        probs = [sb(f"probs{i}", [P, NQ, S]) for i in range(2)]
        pT = sb("pT", [P, NQ, S])
        nmax, rsum, rinv = sb("nmax", [P, 8, NQ]), sb("rsum", [P, 8, NQ]), sb("rinv", [P, 8, NQ])
        o_slot = None if narrow else [sb(f"o{i}", [P, NQ, W]) for i in range(2)]
        loaded = [sem("loaded0"), sem("loaded1")]
        scores_done, max_ready, exp_done, turned, pv_done, rinv_ready, o_ready = (
            sem(n) for n in ("scores", "max", "exp", "turned", "pv", "rinv", "o"))
        copied = [sem("copied_even"), sem("copied_odd")]
        o_free = [sem("o_free0"), sem("o_free1")]
        sbank, tbank, obank = c.bank[0:4], c.bank[4:6], c.bank[6:8]

        def wait_copy(eng, n, qt):
            eng.wait_ge(copied[qt % 2], 2 * n + (qt // 2 + 1))

        def load_quad(sp, quad, s):
            if narrow:
                for j in range(8):
                    for dst, src, part in ((qs[s], q_src, Q_PART[j]), (ks[s], k_src, K_PART[j])):
                        sp.dma_start(dst[16 * j:16 * (j + 1), :, :],
                                     src[part, bass.ds(quad, 1), :, :].rearrange("a (u d) s -> d (a u) s", d=HD)
                                     ).then_inc(loaded[s], 16)
            else:
                for dst, src in ((qs[s], q_src), (ks[s], k_src)):
                    sp.dma_start(dst[:, :, :], src[bass.ds(quad, 1), :, :, :].rearrange("a p u s -> p (a u) s")
                                 ).then_inc(loaded[s], 16)

        block = nc.Block()
        with block:
            @block.sync
            def _(sp):
                for s in range(2):
                    load_quad(sp, s, s)
                if not narrow:
                    sp.sem_inc(o_free[0], 16)
                    sp.sem_inc(o_free[1], 16)

                def store(n, j):
                    sp.wait_ge(o_ready, n + 1)
                    sp.dma_start(out[bass.ds(n, 1), :, :].rearrange("a (q p) d -> p (a q) d", p=P),
                                 o_slot[j % 2][:, :, :]).then_inc(o_free[j % 2], 16)

                with sp.Fori(1, 8) as m:
                    for j in range(8):
                        if not narrow:
                            store(8 * m + (j - 8), j)
                        if j in (2, 6):
                            s = j // 4
                            sp.wait_ge(scores_done, 32 * m + (16 * s - 16))
                            load_quad(sp, 2 * m + s, s)
                if not narrow:
                    for j in range(8):
                        store(56 + j, j)
                    for i in range(2):
                        sp.wait_ge(o_free[i], 16 * (STEPS // 2 + 1))

            @block.tensor
            def _(pe):
                def scores(m, j, qt):
                    s, u = j // 4, j % 4
                    if u == 0 and qt == 0:
                        pe.wait_ge(loaded[s], (m + 1) * 16 * loads)
                    w = width[qt]
                    mm = nc.tensor.matmul(sbank[qt][:, 0:w], qs[s][:, u, qt * P:(qt + 1) * P], ks[s][:, u % kh, 0:w],
                                          start=True, stop=not causal)
                    if causal:
                        mm = nc.tensor.matmul(sbank[qt][:, w - P:w], c.identb[:, :], c.causal[:, :], start=False, stop=True)
                    mm.then_inc(scores_done, 1)

                def values(m, j, qt):
                    n = 8 * m + j
                    wait_copy(pe, n, qt)
                    nk = width[qt] // P
                    for kt in range(nk):
                        if narrow:
                            rhs = vals[:, bass.ds(n, 1), kt, :].rearrange("p a d -> p (a d)")
                        else:
                            rhs = vals[:, bass.ds(2 * m + j // 4, 1), kt, :].rearrange("p a d -> p (a d)")
                        mm = nc.tensor.matmul(obank[j % 2][:, qt * W:(qt + 1) * W], pT[:, qt, kt * P:(kt + 1) * P], rhs,
                                              start=(kt == 0), stop=(kt == nk - 1))
                    if qt == NQ - 1:
                        mm.then_inc(pv_done, 1)

                def step(m, j, following):
                    n = 8 * m + j
                    for qt in range(NQ):
                        pe.wait_ge(exp_done, NQ * n + qt + 1)
                        if qt >= 2:
                            wait_copy(pe, n, qt - 2)
                        for kt in range(width[qt] // P):
                            mm = nc.tensor.transpose(tbank[qt % 2][:, kt * P:(kt + 1) * P],
                                                     probs[j % 2][:, qt, kt * P:(kt + 1) * P], c.ident[:, :])
                        mm.then_inc(turned, 1)
                        if following:
                            scores(*following, qt)
                        if qt:
                            values(m, j, qt - 1)
                    values(m, j, NQ - 1)

                for qt in range(NQ):
                    scores(0, 0, qt)
                with pe.Fori(0, 7) as m:
                    for j in range(8):
                        step(m, j, (m, j + 1) if j < 7 else (m + 1, 0))
                for j in range(8):
                    step(7, j, (7, j + 1) if j < 7 else None)

            @block.scalar
            def _(a):
                def step(m, j):
                    for qt in range(NQ):
                        a.wait_ge(max_ready, NQ * (8 * m + j) + qt + 1)
                        nc.scalar.activation(probs[j % 2][:, qt, 0:width[qt]], sbank[qt][:, 0:width[qt]], ACT.Exp,
                                             bias=nmax[:, j, qt:qt + 1],
                                             accum_out=rsum[:, j, qt:qt + 1]).then_inc(exp_done, 1)
                    for qt in (1, 3):
                        a.wait_ge(turned, NQ * (8 * m + j) + qt + 1)
                        nc.scalar.copy(pT[:, qt, 0:width[qt]], tbank[1][:, 0:width[qt]]).then_inc(copied[1], 1)

                with a.Fori(0, 8) as m:
                    for j in range(8):
                        step(m, j)

            @block.vector
            def _(v):
                def negated_max(m, j, qt):
                    v.wait_ge(scores_done, NQ * (8 * m + j) + qt + 1)
                    nc.vector.tensor_reduce(nmax[:, j, qt:qt + 1], sbank[qt][:, 0:width[qt]], AX.X, ALU.max,
                                            negate=True).then_inc(max_ready, 1)

                def step(m, j, following):
                    n = 8 * m + j
                    for qt in range(NQ):
                        if following:
                            negated_max(*following, qt)
                        if qt % 2 == 0:
                            v.wait_ge(turned, NQ * n + qt + 1)
                            nc.vector.tensor_copy(pT[:, qt, 0:width[qt]], tbank[0][:, 0:width[qt]]).then_inc(copied[0], 1)
                    v.wait_ge(exp_done, NQ * n + NQ)
                    nc.vector.reciprocal(rinv[:, j, :], rsum[:, j, :]).then_inc(rinv_ready, 1)
                    v.wait_ge(rinv_ready, n + 1)
                    v.wait_ge(pv_done, n + 1)
                    o = obank[j % 2][:, 0:NQ * W].rearrange("p (q w) -> p q w", w=W)
                    ri = rinv[:, j, :].unsqueeze(2).to_broadcast([P, NQ, W])
                    if narrow:
                        dst = out[:, bass.ds(n, 1), :, :].rearrange("p a q w -> p (a q) w")
                    else:
                        v.wait_ge(o_free[j % 2], 16 * (4 * m + j // 2 + 1))
                        dst = o_slot[j % 2][:, :, :]
                    nc.vector.tensor_tensor(dst, o, ri, ALU.mult).then_inc(o_ready, 1)

                for qt in range(NQ):
                    negated_max(0, 0, qt)
                with v.Fori(0, 7) as m:
                    for j in range(8):
                        step(m, j, (m, j + 1) if j < 7 else (m + 1, 0))
                for j in range(8):
                    step(7, j, (7, j + 1) if j < 7 else None)


def narrow_attention(c, name, q_parts, k_parts, vals, out, causal):
    nc = c.nc
    LEAD = 10
    HEADS = B * H
    VW = 32

    def keys(qt):
        return (qt + 1) * P if causal else S

    def first_query(kt):
        return kt * P if causal else 0

    with ExitStack() as ctx:
        def sb(n, shape, d=F32):
            return ctx.enter_context(nc.sbuf_tensor(f"{name}_{n}", shape, d))

        def sem(n):
            return c.sem(f"{name}_{n}")

        qs = [sb(f"q{s}", [P, 4, S], BF16) for s in range(4)]
        ks = [sb(f"k{s}", [P, 4, S], BF16) for s in range(4)]
        probs = [sb(f"probs{i}", [P, NQ, S]) for i in range(2)]
        nmax = sb("nmax", [P, 8, NQ])
        rest = sb("rest", [P, 8, NQ])
        mparts = sb("mparts", [P, NQ, P], BF16)
        mT = [sb(f"mT{i}", [P, S], BF16) for i in range(2)]
        vq = [sb(f"vq{i}", [P, 4, NQ, VW]) for i in range(4)]
        pick_f = sb("pick_f", [P, 8])
        pick = sb("pick", [P, 8, P], BF16)
        oT = sb("oT", [P, S])
        rinv = sb("rinv", [P, NQ, 4])
        loaded = [sem(f"loaded{s}") for s in range(4)]
        rows_done, max_ready, split, max_turned, mT_ready = (
            sem(n) for n in ("rows", "max", "split", "max_turned", "mT"))
        cols_done, exp_done, pv_done, quad_done, oT_ready, o_turned, rinv_ready, o_ready, pick_ready = (
            sem(n) for n in ("cols", "exp", "pv", "quad", "oT", "o_turned", "rinv", "o", "pick"))
        spare, zeroed, held = sem("carry"), sem("zeroed"), sem("held")
        cbank, rbank, obank, mbank = c.bank[0:2], c.bank[2:4], c.bank[4:6], c.bank[6]

        def in_turn(b, h):
            return b + h // H, h % H

        block = nc.Block()
        with block:
            @block.sync
            def _(sp):
                def load_quad(quad, s):
                    for j in range(8):
                        for dst, src, part in ((qs[s], q_parts, Q_PART[j]), (ks[s], k_parts, K_PART[j])):
                            sp.dma_start(dst[16 * j:16 * (j + 1), :, :],
                                         src[part, bass.ds(quad, 1), :, :].rearrange("a (u d) s -> d (a u) s", d=HD)
                                         ).then_inc(loaded[s], 16)

                for s in range(4):
                    load_quad(s, s)
                with sp.Fori(1, B) as b:
                    for s in range(4):
                        sp.wait_ge(cols_done, b * (NQ * H) + (4 * NQ * (s + 1) - NQ * H))
                        load_quad(4 * b + s, s)

            @block.tensor
            def _(pe):
                def rows(b, h, qt):
                    s, u, w = h // 4, h % 4, keys(qt)
                    if u == 0 and qt == 0:
                        pe.wait_ge(loaded[s], (b + 1) * 256)
                    pe.wait_ge(max_ready, NQ * (H * b + h) + qt + 1)
                    mm = nc.tensor.matmul(rbank[qt % 2][:, 0:w], qs[s][:, u, qt * P:(qt + 1) * P], ks[s][:, u, 0:w],
                                          start=True, stop=not causal)
                    if causal:
                        mm = nc.tensor.matmul(rbank[qt % 2][:, w - P:w], c.identb[:, :], c.causal[:, :], start=False, stop=True)
                    mm.then_inc(rows_done, 1)

                def turn_maxima():
                    for qt in range(NQ):
                        mm = nc.tensor.matmul(mbank[:, qt * P:(qt + 1) * P], mparts[:, qt, :], c.identb[:, :],
                                              start=True, stop=True)
                    mm.then_inc(max_turned, 1)

                def cols(b, h, kt):
                    s, u, g, lo = h // 4, h % 4, h // 8, first_query(kt)
                    if h % 8 == 0 and kt == 0:
                        pe.wait_ge(mT_ready, 2 * b + g + 1)
                    dst = cbank[kt % 2]
                    nc.tensor.matmul(dst[:, lo:S], ks[s][:, u, kt * P:(kt + 1) * P], qs[s][:, u, lo:S], start=True, stop=False)
                    if causal:
                        nc.tensor.matmul(dst[:, lo:lo + P], c.causal[:, :], c.identb[:, :], start=False, stop=False)
                    nc.tensor.matmul(dst[:, lo:S], pick[:, h % 8, :], mT[g][:, lo:S], start=False, stop=True
                                     ).then_inc(cols_done, 1)

                def values(b, h, kt):
                    u, lo = h % 4, first_query(kt)
                    if u == 0 and kt == 0:
                        pe.wait_ge(held, 4 * b + h // 4 + 1)
                        pe.wait_ge(o_ready, 4 * b + h // 4 + 1)
                    mm = nc.tensor.matmul(obank[h // 4 % 2][VW * u:VW * (u + 1), lo:S], vq[h // 4][:, u, kt, :], probs[h % 2][:, kt, lo:S],
                                          start=(kt == 0), stop=(kt == NQ - 1))
                    if kt == NQ - 1:
                        mm.then_inc(pv_done, 1)

                def turn_quad(b, quad):
                    pe.wait_ge(oT_ready, 4 * b + quad + 1)
                    for qt in range(NQ):
                        mm = nc.tensor.transpose(obank[quad % 2][:, qt * P:(qt + 1) * P], oT[:, qt * P:(qt + 1) * P], c.ident[:, :])
                    mm.then_inc(o_turned, 1)

                def step(b, h, last):
                    for kt in range(NQ):
                        pe.wait_ge(exp_done, NQ * (H * b + h) + kt + 1)
                        if not (last and h == H - 1 and kt >= 2):
                            cols(*in_turn(b, h + (kt + 2) // NQ), (kt + 2) % NQ)
                        if not (last and h + LEAD >= H):
                            rows(*in_turn(b, h + LEAD), kt)
                        values(b, h, kt)
                        if h % 4 == 0 and h and kt == 1:
                            turn_quad(b, h // 4 - 1)
                        if h % 8 == 6 and kt == 3 and not (last and h == H - 2):
                            pe.wait_ge(split, 8 * b + 4 * (h // 8) + 8)
                            turn_maxima()
                    if h == H - 1:
                        turn_quad(b, H // 4 - 1)

                pe.sem_inc(max_ready, 2)
                pe.sem_inc(o_ready, 2)
                pe.sem_inc(max_turned, 1)
                for h in range(LEAD):
                    for qt in range(NQ):
                        rows(0, h, qt)
                pe.wait_ge(pick_ready, 2)
                pe.wait_ge(split, 4)
                turn_maxima()
                cols(0, 0, 0)
                cols(0, 0, 1)
                with pe.Fori(0, B - 1) as b:
                    for h in range(H):
                        step(b, h, False)
                for h in range(H):
                    step(B - 1, h, True)

            @block.scalar
            def _(a):
                def keep_maxima(b, g):
                    a.wait_ge(max_turned, 2 * b + g + 2)
                    nc.scalar.copy(mT[g][:, :], mbank[:, :]).then_inc(mT_ready, 1)

                def step(b, h, last):
                    for kt in range(NQ):
                        a.wait_ge(cols_done, NQ * (H * b + h) + kt + 1)
                        if kt == 0:
                            a.wait_ge(pv_done, H * b + h + 1)
                        lo = first_query(kt)
                        nc.scalar.activation(probs[h % 2][:, kt, lo:S], cbank[kt % 2][:, lo:S], ACT.Exp).then_inc(exp_done, 1)
                        if h % 8 == 7 and kt == 0 and not (last and h == H - 1):
                            keep_maxima(*((b, 1) if h < 8 else (b + 1, 0)))

                a.sem_inc(pv_done, 2)
                keep_maxima(0, 0)
                with a.Fori(0, B - 1) as b:
                    for h in range(H):
                        step(b, h, False)
                for h in range(H):
                    step(B - 1, h, True)

            @block.gpsimd
            def _(g):
                g.memset(mparts[:, :, :], 0.0).then_inc(zeroed, 1)
                for i in range(4):
                    g.memset(vq[i][:, :, :, :], 1.0).then_inc(zeroed, 1)
                g.wait_ge(zeroed, 5)

                def part(i):
                    return mparts[:, :, 8 * i:8 * i + 8].rearrange("p q j -> p j q")

                def split_maxima(n):
                    g.wait_ge(max_ready, n * (8 * NQ) + (8 * NQ + 2))
                    g.wait_ge(max_turned, n + 1)
                    hold(g, spare)
                    g.tensor_copy(part(0), nmax[:, :, :]).then_inc(split, 1)
                    g.wait_ge(split, n * 4 + 1)
                    g.tensor_tensor(rest[:, :, :], nmax[:, :, :], part(0), ALU.subtract).then_inc(split, 1)
                    g.wait_ge(split, n * 4 + 2)
                    hold(g, spare)
                    g.tensor_copy(part(1), rest[:, :, :]).then_inc(split, 1)
                    g.wait_ge(split, n * 4 + 3)
                    g.tensor_tensor(part(2), rest[:, :, :], part(1), ALU.subtract).then_inc(split, 1)

                def hold_values(b, quad):
                    g.wait_ge(pv_done, H * b + (1 if quad < 2 else 4))
                    hold(g, spare)
                    g.tensor_copy(vq[quad][:, :, :, 0:HD], vals[:, bass.ds(H * b + 4 * quad, 4), :, :]).then_inc(held, 1)

                with g.Fori(0, B) as b:
                    for half in range(2):
                        split_maxima(2 * b + half)
                        hold_values(b, 2 * half)
                        hold_values(b, 2 * half + 1)

            @block.vector
            def _(v):
                def maxima(b, h, qt, first=False):
                    if h % 8 == 0 and qt == 0 and not first:
                        v.wait_ge(split, 8 * b + 4 * (h // 8) - 2)
                    v.wait_ge(rows_done, NQ * (H * b + h) + qt + 1)
                    nc.vector.tensor_reduce(nmax[:, h % 8, qt:qt + 1], rbank[qt % 2][:, 0:keys(qt)], AX.X, ALU.max,
                                            negate=True).then_inc(max_ready, 1)

                def keep_quad(b, quad):
                    v.wait_ge(pv_done, H * b + 4 * quad + 6)
                    nc.vector.tensor_copy(oT[:, :], obank[quad % 2][:, :]).then_inc(oT_ready, 1)

                def divide_quad(b, quad):
                    v.wait_ge(o_turned, 4 * b + quad + 1)
                    o = obank[quad % 2][:, :].rearrange("p (q u w) -> p q u w", q=NQ, w=VW)
                    nc.vector.reciprocal(rinv[:, :, :], o[:, :, :, HD]).then_inc(rinv_ready, 1)
                    v.wait_ge(rinv_ready, 4 * b + quad + 1)
                    dst = out[:, bass.ds(NQ * b, NQ), 4 * HD * quad:4 * HD * (quad + 1)].rearrange("p q (u w) -> p q u w", w=HD)
                    nc.vector.tensor_tensor(dst,
                                            o[:, :, :, 0:HD], rinv[:, :, :].unsqueeze(3).to_broadcast([P, NQ, 4, HD]),
                                            ALU.mult).then_inc(o_ready, 1)

                def step(b, h, last):
                    quad = h // 4 - 1 if h % 4 == 0 else -1
                    if quad >= 0:
                        keep_quad(b, quad)
                    for qt in range(NQ):
                        if not (last and h + LEAD >= H):
                            maxima(*in_turn(b, h + LEAD), qt)
                        if quad >= 0 and qt == 2:
                            divide_quad(b, quad)
                    if h == H - 1:
                        keep_quad(b, H // 4 - 1)
                        divide_quad(b, H // 4 - 1)

                nc.vector.tensor_reduce(pick_f[:, :], c.ident[:, 0:24].rearrange("p (t j) -> p j t", t=3), AX.X,
                                        ALU.add).then_inc(pick_ready, 1)
                v.wait_ge(pick_ready, 1)
                nc.vector.tensor_copy(pick[:, :, :], pick_f[:, :].unsqueeze(2).to_broadcast([P, 8, P])).then_inc(pick_ready, 1)
                for h in range(LEAD):
                    for qt in range(NQ):
                        maxima(0, h, qt, h == 0)
                with v.Fori(0, B - 1) as b:
                    for h in range(H):
                        step(b, h, False)
                for h in range(H):
                    step(B - 1, h, True)


def narrow_output(c, name, attended, w_out, bias, factor):
    nc = c.nc
    with ExitStack() as ctx:
        def sb(n, shape):
            return ctx.enter_context(nc.sbuf_tensor(f"{name}_{n}", shape, F32))

        def sem(n):
            return c.sem(f"{name}_{n}")

        norm = Norm(c, ctx, name)
        w, bias_row = sb("w", [P, KT, D]), sb("bias", [P, D])
        o, oT = sb("o", [P, NQ, D]), sb("oT", [P, KT, S])
        y, t = sb("y", [P, NQ, D]), sb("t", [P, NQ, D])
        w_in, o_ready, tr_done, oT_ready, y_done, y_ready, t_ready, x_ready, spare = (
            sem(n) for n in ("w_in", "o_ready", "tr_done", "oT_ready", "y_done", "y_ready", "t_ready", "x_ready", "spare"))
        tr, py = c.bank[0:2], c.bank[2:4]
        n_w = 1 + (bias is not None)
        block = nc.Block()
        with block:
            @block.sync
            def _(sp):
                sp.dma_start(w[:, :, :], weights(w_out)).then_inc(w_in, 16)
                if bias is not None:
                    sp.dma_start(bias_row[:, :], bias.partition_broadcast(P)).then_inc(w_in, 16)

            @block.gpsimd
            def _(g):
                def keep_o(b):
                    g.wait_ge(tr_done, b * KT + KT)
                    hold(g, spare)
                    g.tensor_copy(o[:, :, :], attended[:, bass.ds(b * NQ, NQ), :]).then_inc(o_ready, 1)

                keep_o(0)
                with g.Fori(0, B - 1) as b:
                    keep_o(b + 1)
                    norm.root(g, b)
                norm.root(g, B - 1)

            @block.tensor
            def _(pe):
                def turn(b):
                    pe.wait_ge(o_ready, b + 1)
                    for k in range(KT):
                        for q in range(NQ):
                            mm = nc.tensor.transpose(tr[k][:, q * P:(q + 1) * P], o[:, q, k * P:(k + 1) * P], c.ident[:, :])
                        mm.then_inc(tr_done, 1)

                def group(b, last):
                    pe.wait_ge(oT_ready, b * KT + KT)
                    pe.wait_ge(y_ready, b * 2 + 2)
                    for q in range(NQ):
                        for k in range(KT):
                            mm = nc.tensor.matmul(py[q // 2][:, (q % 2) * D:(q % 2 + 1) * D], oT[:, k, q * P:(q + 1) * P],
                                                  w[:, k, :], start=(k == 0), stop=(k == KT - 1))
                        if q % 2:
                            mm.then_inc(y_done, 1)
                    if not last:
                        turn(b + 1)

                pe.sem_inc(tr_done, KT)
                pe.sem_inc(y_done, 2)
                pe.sem_inc(y_ready, 2)
                pe.wait_ge(w_in, 16 * n_w)
                turn(0)
                with pe.Fori(0, B - 1) as b:
                    group(b, False)
                group(B - 1, True)

            @block.scalar
            def _(a):
                with a.Fori(0, B) as b:
                    for k in range(KT):
                        a.wait_ge(tr_done, b * KT + k + 3)
                        if k == 0:
                            a.wait_ge(y_done, b * 2 + 2)
                        nc.scalar.activation(oT[:, k, :], tr[k][:, :], ACT.Copy, scale=factor).then_inc(oT_ready, 1)

            @block.vector
            def _(v):
                if bias is not None:
                    v.wait_ge(w_in, 16 * n_w)
                with v.Fori(0, B) as b:
                    for i in range(2):
                        v.wait_ge(y_done, b * 2 + i + 3)
                        src = py[i][:, :].rearrange("p (q d) -> p q d", d=D)
                        dst = y[:, 2 * i:2 * i + 2, :]
                        if bias is not None:
                            row = bias_row[:, :].unsqueeze(1).to_broadcast([P, 2, D])
                            mm = nc.vector.tensor_tensor(dst, src, row, ALU.add)
                        else:
                            mm = nc.vector.tensor_copy(dst, src)
                        mm.then_inc(y_ready, 1)
                    v.wait_ge(y_ready, b * 2 + 4)
                    norm.statistics(v, b, lambda q: y[:, q, :])
                    norm.wait(v, b)
                    add_normed(c, v, norm, b, lambda q: y[:, q, :], t, t_ready, x_ready)


def add_normed(c, v, norm, b, tile, t, t_ready, x_ready):
    for q in range(NQ):
        norm.apply(q, t[:, q, :], tile(q)).then_inc(t_ready, 1)
    for q in range(NQ):
        v.wait_ge(t_ready, b * NQ + q + 1)
        c.nc.vector.tensor_tensor(tile_of(c.x, b, q), tile_of(c.x, b, q), t[:, q, :], ALU.add).then_inc(x_ready, 1)


def router_input(c, name, src, rms, col_scale, w_router, bias, n_experts, hT_all, h_all, logits,
                 h_slots=None):
    nc = c.nc
    with ExitStack() as ctx:
        def sb(n, shape):
            return ctx.enter_context(nc.sbuf_tensor(f"{name}_{n}", shape, F32))

        def sem(n):
            return c.sem(f"{name}_{n}")

        norm = Norm(c, ctx, name)
        w = sb("w", [P, KT, n_experts])
        row = sb("row", [P, n_experts])
        col = sb("col", [P, KT])
        h, hT = sb("h", [P, NQ, D]), sb("hT", [P, KT, S])
        w_in, h_ready, tr_done, hT_ready, kept, lg_done, lg_ready, spare = (
            sem(n) for n in ("w_in", "h_ready", "tr_done", "hT_ready", "kept", "lg_done", "lg_ready", "spare"))
        zero = sb("zero", [P, 8, D])
        zero_ready, zeroed = sem("zero_ready"), sem("zeroed")
        kept_per = KT if h_all is None else 1
        tr, pl = c.bank[0:2], c.bank[2]
        n_w = 1 + (bias is not None) + (col_scale is not None)
        block = nc.Block()
        with block:
            @block.sync
            def _(sp):
                sp.dma_start(w[:, :, :], weights(w_router)).then_inc(w_in, 16)
                if bias is not None:
                    sp.dma_start(row[:, :], bias.partition_broadcast(P)).then_inc(w_in, 16)
                if col_scale is not None:
                    sp.dma_start(col[:, :], col_scale).then_inc(w_in, 16)
                if h_slots is not None:
                    sp.wait_ge(zero_ready, 1)
                    tiles = BLOCKS * SLOTS // P
                    for i in range(0, tiles, 8):
                        n = min(8, tiles - i)
                        sp.dma_start(h_slots[i * P:(i + n) * P, :].rearrange("(i p) d -> p i d", p=P), zero[:, 0:n, :]).then_inc(zeroed, 16)
                    sp.wait_ge(zeroed, 16 * -(-tiles // 8))

            @block.vector
            def _(v):
                if h_slots is not None:
                    nc.vector.memset(zero[:, :, :], 0.0).then_inc(zero_ready, 1)
                v.wait_ge(w_in, 16 * n_w)
                with v.Fori(0, B) as b:
                    norm.statistics(v, b, lambda q: tile_of(src, b, q), rms)
                    norm.wait(v, b)
                    v.wait_ge(tr_done, b * KT + KT)
                    if h_all is not None:
                        v.wait_ge(kept, b + 1)
                    for q in range(NQ):
                        norm.apply(q, h[:, q, :], tile_of(src, b, q), rms).then_inc(h_ready, 1)
                    v.wait_ge(lg_done, b + 2)
                    dst = logits[:, bass.ds(b * NQ, NQ), :]
                    lg = pl[:, 0:NQ * n_experts].rearrange("p (q e) -> p q e", e=n_experts)
                    if bias is not None:
                        nc.vector.tensor_tensor(dst, lg, row[:, :].unsqueeze(1).to_broadcast([P, NQ, n_experts]),
                                                ALU.add).then_inc(lg_ready, 1)
                    else:
                        nc.vector.tensor_copy(dst, lg).then_inc(lg_ready, 1)

            @block.gpsimd
            def _(g):
                g.sem_inc(kept, kept_per)
                with g.Fori(0, B) as b:
                    norm.root(g, b, rms)
                    if h_all is not None:
                        g.wait_ge(h_ready, b * NQ + NQ)
                        hold(g, spare)
                        g.tensor_copy(h_all[:, bass.ds(b * NQ, NQ), :], h[:, :, :]).then_inc(kept, 1)
                    for k in range(KT if h_all is None else 0):
                        g.wait_ge(hT_ready, b * KT + k + 1)
                        hold(g, spare)
                        g.tensor_copy(hT_all[:, k, bass.ds(b * S, S)], hT[:, k, :]).then_inc(kept, 1)

            @block.scalar
            def _(a):
                with a.Fori(0, B) as b:
                    for k in range(KT):
                        a.wait_ge(tr_done, b * KT + k + 3)
                        if h_all is None:
                            a.wait_ge(kept, b * KT + k + 1)
                        a.wait_ge(lg_done, b + 1)
                        if col_scale is None:
                            nc.scalar.copy(hT[:, k, :], tr[k][:, :]).then_inc(hT_ready, 1)
                        else:
                            nc.scalar.activation(hT[:, k, :], tr[k][:, :], ACT.Copy, scale=col[:, k:k + 1]).then_inc(hT_ready, 1)

            @block.tensor
            def _(pe):
                pe.sem_inc(tr_done, KT)
                pe.sem_inc(lg_done, 1)
                pe.wait_ge(w_in, 16 * n_w)
                with pe.Fori(0, B) as b:
                    for k in range(KT):
                        for q in range(NQ):
                            if k == 0:
                                pe.wait_ge(h_ready, b * NQ + q + 1)
                            mm = nc.tensor.transpose(tr[k][:, q * P:(q + 1) * P], h[:, q, k * P:(k + 1) * P], c.ident[:, :])
                        mm.then_inc(tr_done, 1)
                    pe.wait_ge(hT_ready, b * KT + KT)
                    for q in range(NQ):
                        for k in range(KT):
                            mm = nc.tensor.matmul(pl[:, q * n_experts:(q + 1) * n_experts], hT[:, k, q * P:(q + 1) * P],
                                                  w[:, k, :], start=(k == 0), stop=(k == KT - 1))
                    mm.then_inc(lg_done, 1)


class Chain:

    def __init__(self, v, sem):
        self.v, self.sem, self.n = v, sem, 0

    def link(self, ins):
        self.n += 1
        ins.then_inc(self.sem, 1)
        self.v.wait_ge(self.sem, self.n)


def sigmoid_gates(c, name, logits, iota, gates):
    nc = c.nc
    KG, EG = 4, E0 // G0
    with ExitStack() as ctx:
        def sb(n, shape, dt=F32):
            return ctx.enter_context(nc.sbuf_tensor(f"{name}_{n}", shape, dt))

        ex, s = sb("ex", [P, NT, E0]), sb("s", [P, NT, E0])
        pairs = sb("pairs", [P, 6, NT * G0])
        gw = sb("gw", [P, NT, G0])
        top, idx, idxf = sb("top", [P, NT, 8]), sb("idx", [P, NT, 8], U32), sb("idxf", [P, NT, 8])
        eq = sb("eq", [P, NT, E0, K0])
        gmask, masked, sel = sb("gmask", [P, NT, G0]), sb("masked", [P, NT, E0]), sb("sel", [P, NT, E0])
        den = sb("den", [P, 2, NT])
        ex_ready, step = c.sem(f"{name}_ex"), c.sem(f"{name}_step")
        block = nc.Block()
        with block:
            @block.scalar
            def _(a):
                nc.scalar.activation(ex[:, :, :], logits[:, :, :], ACT.Exp, scale=-1.0).then_inc(ex_ready, 1)

            @block.vector
            def _(v):
                nv = nc.vector
                link = Chain(v, step).link

                def top8(scores):
                    for t in range(NT):
                        ins = nv.max(top[:, t, :], scores[:, t, :])
                    link(ins)
                    for t in range(NT):
                        ins = nv.max_index(idx[:, t, :], top[:, t, :], scores[:, t, :])
                    link(ins)
                    link(nv.tensor_copy(idxf[:, :, :], idx[:, :, :]))

                def among(out, n, k):
                    e = eq[:, :, 0:n, 0:k]
                    link(nv.tensor_tensor(e, idxf[:, :, 0:k].unsqueeze(2).to_broadcast([P, NT, n, k]),
                                          iota[:, 0:n].unsqueeze(1).unsqueeze(3).to_broadcast([P, NT, n, k]), ALU.is_equal))
                    link(nv.tensor_reduce(out, e, AX.X, ALU.add))

                v.wait_ge(ex_ready, 1)
                link(nv.tensor_scalar(s[:, :, :], ex[:, :, :], 1.0, None, ALU.add))
                link(nv.reciprocal(s[:, :, :], s[:, :, :]))
                sg = s[:, :, :].rearrange("p t (g e) -> p (t g) e", e=EG)
                for i, (x, y, op) in enumerate(((0, 1, ALU.max), (0, 1, ALU.min), (2, 3, ALU.max), (2, 3, ALU.min))):
                    link(nv.tensor_tensor(pairs[:, i, :], sg[:, :, x], sg[:, :, y], op))
                link(nv.tensor_tensor(pairs[:, 4, :], pairs[:, 0, :], pairs[:, 2, :], ALU.min))
                link(nv.tensor_tensor(pairs[:, 5, :], pairs[:, 1, :], pairs[:, 3, :], ALU.max))
                link(nv.tensor_tensor(pairs[:, 4, :], pairs[:, 4, :], pairs[:, 5, :], ALU.max))
                link(nv.tensor_tensor(pairs[:, 5, :], pairs[:, 0, :], pairs[:, 2, :], ALU.max))
                link(nv.tensor_tensor(gw[:, :, :].rearrange("p t g -> p (t g)"), pairs[:, 4, :], pairs[:, 5, :], ALU.add))
                top8(gw)
                among(gmask[:, :, :], G0, KG)
                link(nv.tensor_tensor(masked[:, :, :].rearrange("p t (g e) -> p (t g) e", e=EG), sg,
                                      gmask[:, :, :].rearrange("p t g -> p (t g)").unsqueeze(2).to_broadcast([P, NT * G0, EG]),
                                      ALU.mult))
                top8(masked)
                among(sel[:, :, :], E0, K0)
                link(nv.tensor_tensor(sel[:, :, :], sel[:, :, :], s[:, :, :], ALU.mult))
                link(nv.tensor_reduce(den[:, 0, :], sel[:, :, :], AX.X, ALU.add))
                link(nv.tensor_scalar(den[:, 1, :], den[:, 0, :], 1e-20, None, ALU.add))
                link(nv.reciprocal(den[:, 0, :], den[:, 1, :]))
                link(nv.tensor_tensor(gates[:, :, :], sel[:, :, :], den[:, 0, :].unsqueeze(2).to_broadcast([P, NT, E0]), ALU.mult))
                link(nv.tensor_scalar(gates[:, :, :], gates[:, :, :], SCALE0, None, ALU.mult))


def relu2_experts(c, name, hT, gates, w, acc):
    nc = c.nc
    WC = KT * M0
    PAIRS = E0 // 2
    PRODUCTS = [(0, 0), (0, 1), (1, 0)]
    with ExitStack() as ctx:
        def sb(n, shape, dt=F32):
            return ctx.enter_context(nc.sbuf_tensor(f"{name}_{n}", shape, dt))

        def sem(n):
            return c.sem(f"{name}_{n}")

        ws = [sb(f"w{s}", [P, 2, WC + D]) for s in range(2)]
        wp = [[sb(f"w{s}_{part}", [P, 2, WC + D], F32R) for part in ("high", "low")] for s in range(2)]
        hp = [sb(f"h_{part}", [P, KT, T], F32R) for part in ("high", "low")]
        relu, act = sb("relu", [P, 4, S]), sb("act", [P, 4, S])
        ap = [sb(f"act_{part}", [P, 4, S], F32R) for part in ("high", "low")]
        loaded = [sem("loaded0"), sem("loaded1")]
        h_high, h_low, w_high, w_low, up_done, relu_ready, act_ready, act_high, act_low, y_done, acc_done, zeroed = (
            sem(n) for n in ("h_high", "h_low", "w_high", "w_low", "up", "relu", "act", "act_high", "act_low", "y", "acc", "zeroed"))
        ph, py = c.bank[0:4], c.bank[4:8]

        def ahead(p, u):
            return p + (u + 2) // 8, (u + 2) % 8

        block = nc.Block()
        with block:
            @block.sync
            def _(sp):
                def load(pair, s):
                    sp.dma_start(ws[s][:, :, :], w[bass.ds(pair, 1), :, :, :].rearrange("a p i n -> p (a i) n")).then_inc(loaded[s], 16)

                load(0, 0)
                load(1, 1)
                with sp.Fori(1, PAIRS // 2) as m:
                    for s in range(2):
                        sp.wait_ge(w_low, 2 * m + (s - 1))
                        load(2 * m + s, s)
                sp.wait_ge(w_low, PAIRS - 1)
                load(PAIRS, 0)

            @block.tensor
            def _(pe):
                def up(p, u, s):
                    g, i = u // 2, u % 2
                    if u == 0:
                        pe.wait_ge(w_low, p + 1)
                    n = 0
                    for k in range(KT):
                        for x, y in PRODUCTS:
                            mm = nc.tensor.matmul(ph[u % 4][:, :], wp[s][x][:, i, k * M0:(k + 1) * M0], hp[y][:, k, g * S:(g + 1) * S],
                                                  start=(n == 0), stop=(n == 3 * KT - 1))
                            n += 1
                    mm.then_inc(up_done, 1)

                def down(p, u, s):
                    i = u % 2
                    pe.wait_ge(act_low, 8 * p + u + 1)
                    pe.wait_ge(acc_done, NQ * (8 * p + u + 1))
                    for q in range(NQ):
                        for n, (x, y) in enumerate(PRODUCTS):
                            mm = nc.tensor.matmul(py[2 * i + q // 2][:, (q % 2) * D:(q % 2 + 1) * D],
                                                  ap[x][:, u % 4, q * P:(q + 1) * P], wp[s][y][:, i, WC:], start=(n == 0), stop=(n == 2))
                    mm.then_inc(y_done, 1)

                pe.wait_ge(h_low, 2 * B)
                up(0, 0, 0)
                up(0, 1, 0)
                with pe.Fori(0, PAIRS // 2) as m:
                    for s in range(2):
                        for u in range(8):
                            q, v = ahead(2 * m + s, u)
                            up(q, v, s if u < 6 else 1 - s)
                            down(2 * m + s, u, s)
                for u in range(8):
                    if u < 6:
                        up(PAIRS, u + 2, 0)
                    down(PAIRS, u, 0)

            @block.scalar
            def _(a):
                def split_weights(p, s, count, first=False):
                    a.wait_ge(loaded[s], 16 * count)
                    if not first:
                        a.wait_ge(y_done, 8 * p - 7)
                    nc.scalar.copy(wp[s][0][:, :, :], ws[s][:, :, :]).then_inc(w_high, 1)

                def unit(p, u):
                    a.wait_ge(up_done, 8 * p + u + 1)
                    nc.scalar.activation(relu[:, u % 4, :], ph[u % 4][:, :], ACT.Relu).then_inc(relu_ready, 1)
                    a.wait_ge(act_ready, 8 * p + u + 1)
                    nc.scalar.copy(ap[0][:, u % 4, :], act[:, u % 4, :]).then_inc(act_high, 1)

                split_weights(0, 0, 1, True)
                for g in range(B):
                    for k in range(KT):
                        nc.scalar.copy(hp[0][:, k, g * S:(g + 1) * S], hT[:, k, g * S:(g + 1) * S]).then_inc(h_high, 1)
                with a.Fori(0, PAIRS // 2) as m:
                    for s in range(2):
                        for u in range(8):
                            unit(2 * m + s, u)
                            if u == 4:
                                split_weights(2 * m + s + 1, 1 - s, m + 1 + s)
                for u in range(8):
                    unit(PAIRS, u)

            @block.gpsimd
            def _(g):
                def low_weights(p, s):
                    g.wait_ge(w_high, p + 1)
                    g.tensor_tensor(wp[s][1][:, :, :], ws[s][:, :, :], wp[s][0][:, :, :], ALU.subtract).then_inc(w_low, 1)

                def unit(p, u):
                    g.wait_ge(act_high, 8 * p + u + 1)
                    g.tensor_tensor(ap[1][:, u % 4, :], act[:, u % 4, :], ap[0][:, u % 4, :], ALU.subtract).then_inc(act_low, 1)

                low_weights(0, 0)
                with g.Fori(0, PAIRS // 2) as m:
                    for s in range(2):
                        for u in range(8):
                            unit(2 * m + s, u)
                            if u == 4:
                                low_weights(2 * m + s + 1, 1 - s)
                for u in range(8):
                    unit(PAIRS, u)

            @block.vector
            def _(v):
                def square(p, u):
                    v.wait_ge(relu_ready, 8 * p + u + 1)
                    nc.vector.scalar_tensor_tensor(out=act[:, u % 4, :], in0=ph[u % 4][:, :], scalar=0.0, in1=relu[:, u % 4, :],
                                                   op0=ALU.max, op1=ALU.mult).then_inc(act_ready, 1)

                def add(p, u, shared):
                    g, i = u // 2, u % 2
                    v.wait_ge(y_done, 8 * p + u + 1)
                    for q in range(NQ):
                        tile = acc[:, NQ * g + q, :]
                        y = py[2 * i + q // 2][:, (q % 2) * D:(q % 2 + 1) * D]
                        v.wait_ge(acc_done, NQ * (8 * p + u) + (NQ + q + 1))
                        if shared:
                            nc.vector.tensor_tensor(tile, y, tile, ALU.add).then_inc(acc_done, 1)
                        else:
                            gate = gates[:, NQ * g + q, bass.ds(2 * p + i, 1)]
                            nc.vector.scalar_tensor_tensor(out=tile, in0=y, scalar=gate, in1=tile,
                                                           op0=ALU.mult, op1=ALU.add).then_inc(acc_done, 1)

                v.sem_inc(acc_done, 2 * NQ)
                for g in range(B):
                    for k in range(KT):
                        v.wait_ge(h_high, 2 * g + k + 1)
                        nc.vector.tensor_tensor(hp[1][:, k, g * S:(g + 1) * S], hT[:, k, g * S:(g + 1) * S],
                                                hp[0][:, k, g * S:(g + 1) * S], ALU.subtract).then_inc(h_low, 1)
                nc.vector.memset(acc[:, :, :], 0.0).then_inc(zeroed, 1)
                v.wait_ge(zeroed, 1)
                square(0, 0)
                square(0, 1)
                with v.Fori(0, PAIRS // 2) as m:
                    for s in range(2):
                        for u in range(8):
                            square(*ahead(2 * m + s, u))
                            add(2 * m + s, u, False)
                for u in range(8):
                    if u < 6:
                        square(PAIRS, u + 2)
                    add(PAIRS, u, True)


def add_normed_sum(c, name, acc, plus=None):
    nc = c.nc
    with ExitStack() as ctx:
        norm = Norm(c, ctx, name)
        y = ctx.enter_context(nc.sbuf_tensor(f"{name}_y", [P, NQ, D], F32))
        t = ctx.enter_context(nc.sbuf_tensor(f"{name}_t", [P, NQ, D], F32))
        y_ready, t_ready, x_ready = (c.sem(f"{name}_{n}") for n in ("y_ready", "t_ready", "x_ready"))
        block = nc.Block()
        with block:
            @block.vector
            def _(v):
                with v.Fori(0, B) as b:
                    if plus is not None:
                        nc.vector.tensor_tensor(y[:, :, :], acc[:, bass.ds(b * NQ, NQ), :], plus[:, bass.ds(b * NQ, NQ), :],
                                                ALU.add).then_inc(y_ready, 1)
                        v.wait_ge(y_ready, b + 1)

                    def tile(q):
                        return tile_of(acc, b, q) if plus is None else y[:, q, :]

                    norm.statistics(v, b, tile)
                    norm.wait(v, b)
                    add_normed(c, v, norm, b, tile, t, t_ready, x_ready)

            @block.gpsimd
            def _(g):
                with g.Fori(0, B) as b:
                    norm.root(g, b)


def grouped_projection(c, name, a, z, vals, q_dram, k_dram):
    nc = c.nc
    NC = H + KVH
    HALF = P // 2
    with ExitStack() as ctx:
        def sb(n, shape):
            return ctx.enter_context(nc.sbuf_tensor(f"{name}_{n}", shape, F32))

        def sem(n):
            return c.sem(f"{name}_{n}")

        norm_x, norm_z = Norm(c, ctx, name + "_x"), Norm(c, ctx, name + "_z")
        wqk, wv = sb("wqk", [P, KT, NC * P]), sb("wv", [P, KT, KVH * GD])
        col, rope = sb("col", [P, KT]), sb("rope", [P, 2, 2, S])
        h, hT = sb("h", [P, NQ, D]), sb("hT", [P, KT, S])
        xc, xs = sb("xc", [P, 2, S]), sb("xs", [P, 2, S])
        rot = sb("rot", [P, NC, S])
        w_in, z_ready, h_ready, tr_done, hT_ready, v_done, v_kept, qk_done, bank_free, terms, rot_ready, stored, rot_free, spare = (
            sem(n) for n in ("w_in", "z_ready", "h_ready", "tr_done", "hT_ready", "v_done", "v_kept", "qk_done",
                             "bank_free", "terms", "rot_ready", "stored", "rot_free", "carry"))
        tr, ps, pv = c.bank[0:2], c.bank[2:6], c.bank[6:8]
        block = nc.Block()
        with block:
            @block.sync
            def _(sp):
                sp.sem_inc(rot_free, 1)
                for dst, src in ((wqk[:, :, :], weights(a["d_wqk"])), (wv[:, :, :], weights(a["d_wv"])),
                                 (col[:, :], a["d_ln"]), (rope[:, :, :, :], a["d_rope"])):
                    sp.dma_start(dst, src).then_inc(w_in, 16)
                with sp.Fori(0, B) as b:
                    for quad in range(5):
                        sp.wait_ge(rot_ready, b * NC + (4 * quad + 4 + 2))
                        if quad < 4:
                            dst = q_dram[bass.ds(4 * b + quad, 1), :, :, :].rearrange("a p u s -> p (a u) s")
                        else:
                            dst = k_dram[bass.ds(4 * b, 4), :, :, :].rearrange("g p u s -> p (g u) s")
                        sp.dma_start(dst, rot[:, 4 * quad:4 * quad + 4, :]).then_inc(stored, 16)
                    sp.wait_ge(stored, b * 80 + 80)
                    sp.sem_inc(rot_free, 1)

            @block.vector
            def _(v):
                v.wait_ge(w_in, 64)
                with v.Fori(0, B) as b:
                    norm_x.statistics(v, b, lambda q: tile_of(c.x, b, q))
                    norm_x.wait(v, b)
                    for q in range(NQ):
                        norm_x.apply(q, tile_of(z, b, q), tile_of(c.x, b, q)).then_inc(z_ready, 1)
                    v.wait_ge(z_ready, b * NQ + NQ)
                    norm_z.statistics(v, b, lambda q: tile_of(z, b, q), rms=True)
                    norm_z.wait(v, b)
                    v.wait_ge(tr_done, b * KT + KT)
                    for q in range(NQ):
                        norm_z.apply(q, h[:, q, :], tile_of(z, b, q), rms=True).then_inc(h_ready, 1)
                    for cc in range(NC):
                        src, k = ps[cc % 4], cc // H
                        v.wait_ge(qk_done, b * NC + (cc + 1 + NC))
                        v.wait_ge(rot_ready, b * NC + (cc + 1))
                        nc.vector.tensor_tensor(xc[:, cc % 2, :], src[:, :], rope[:, k, 0, :], ALU.mult).then_inc(terms, 1)
                        nc.vector.tensor_tensor(xs[0:HALF, cc % 2, :], src[HALF:P, :], rope[HALF:P, k, 1, :], ALU.mult).then_inc(terms, 1)
                        nc.vector.tensor_tensor(xs[HALF:P, cc % 2, :], src[0:HALF, :], rope[0:HALF, k, 1, :], ALU.mult).then_inc(terms, 1)

            @block.gpsimd
            def _(g):
                g.sem_inc(rot_ready, 2)
                with g.Fori(0, B) as b:
                    norm_x.root(g, b)
                    norm_z.root(g, b, rms=True)
                    for cc in range(NC):
                        g.wait_ge(terms, b * 3 * NC + 3 * (cc + 1))
                        if cc == 0:
                            g.wait_ge(rot_free, b + 1)
                        g.tensor_tensor(rot[:, cc, :], xc[:, cc % 2, :], xs[:, cc % 2, :], ALU.add).then_inc(rot_ready, 1)

            @block.scalar
            def _(s):
                s.wait_ge(w_in, 64)
                with s.Fori(0, B) as b:
                    for k in range(KT):
                        s.wait_ge(tr_done, b * KT + (k + 1 + KT))
                        s.wait_ge(qk_done, b * NC + NC)
                        nc.scalar.activation(hT[:, k, :], tr[k][:, :], ACT.Copy, scale=col[:, k:k + 1]).then_inc(hT_ready, 1)
                    for q in range(NQ):
                        s.wait_ge(v_done, b * NQ + (q + 1))
                        hold(s, spare)
                        nc.scalar.copy(vals[:, bass.ds(b * KVH, KVH), q, :],
                                       pv[q % 2][:, :].rearrange("p (g d) -> p g d", d=GD)).then_inc(v_kept, 1)

            @block.tensor
            def _(pe):
                pe.sem_inc(tr_done, KT)
                pe.sem_inc(qk_done, NC)
                pe.wait_ge(w_in, 64)
                with pe.Fori(0, B) as b:
                    for k in range(KT):
                        for q in range(NQ):
                            if k == 0:
                                pe.wait_ge(h_ready, b * NQ + (q + 1))
                            mm = nc.tensor.transpose(tr[k][:, q * P:(q + 1) * P], h[:, q, k * P:(k + 1) * P], c.ident[:, :])
                        mm.then_inc(tr_done, 1)
                    pe.wait_ge(hT_ready, b * KT + KT)
                    for q in range(NQ):
                        if q >= 2:
                            pe.wait_ge(v_kept, b * NQ + (q - 1))
                        for k in range(KT):
                            mm = nc.tensor.matmul(pv[q % 2][:, :], hT[:, k, q * P:(q + 1) * P], wv[:, k, :],
                                                  start=(k == 0), stop=(k == KT - 1))
                        mm.then_inc(v_done, 1)
                    for cc in range(NC):
                        if cc >= 4:
                            pe.wait_ge(terms, b * 3 * NC + 3 * (cc - 3))
                        for k in range(KT):
                            mm = nc.tensor.matmul(ps[cc % 4][:, :], wqk[:, k, cc * P:(cc + 1) * P], hT[:, k, :],
                                                  start=(k == 0), stop=(k == KT - 1))
                        mm.then_inc(qk_done, 1)


def grouped_output(c, name, o_dram, w_out, z):
    nc = c.nc
    with ExitStack() as ctx:
        def sb(n, shape):
            return ctx.enter_context(nc.sbuf_tensor(f"{name}_{n}", shape, F32))

        def sem(n):
            return c.sem(f"{name}_{n}")

        w = sb("w", [P, H, D])
        o = [sb(f"o{i}", [P, H, GD]) for i in range(2)]
        oT = sb("oT", [P, H, P])
        w_in, tr_done, oT_ready, y_done, z_ready = (sem(n) for n in ("w_in", "tr_done", "oT_ready", "y_done", "z_ready"))
        loaded = [sem("loaded0"), sem("loaded1")]
        tr, py = c.bank[0:4], c.bank[4:6]
        block = nc.Block()
        with block:
            @block.sync
            def _(sp):
                sp.dma_start(w[:, :, :], w_out.rearrange("(h p) n -> p h n", p=P)).then_inc(w_in, 16)
                with sp.Fori(0, B) as b:
                    for q in range(NQ):
                        sp.wait_ge(tr_done, 4 * (b * NQ + (q + 1)))
                        for i in range(4):
                            sp.dma_start(o[q % 2][:, 4 * i:4 * i + 4, :], o_dram[bass.ds(b * H + 4 * i, 4), q * P:(q + 1) * P, :].rearrange(
                                "h p d -> p h d")).then_inc(loaded[q % 2], 16)

            @block.tensor
            def _(pe):
                pe.sem_inc(tr_done, 8)
                pe.wait_ge(w_in, 16)
                with pe.Fori(0, B) as b:
                    for q in range(NQ):
                        pe.wait_ge(loaded[q % 2], 128 * b + 64 * (q // 2 + 1))
                        for h in range(H):
                            mm = nc.tensor.transpose(tr[h // 4][:, (h % 4) * P:(h % 4 + 1) * P], o[q % 2][:, h, :], c.ident[:, :])
                            if h % 4 == 3:
                                mm.then_inc(tr_done, 1)
                        pe.wait_ge(z_ready, b * NQ + (q + 1))
                        for h in range(H):
                            if h % 4 == 0:
                                pe.wait_ge(oT_ready, 4 * (b * NQ + q) + (h // 4 + 1))
                            mm = nc.tensor.matmul(py[q % 2][:, 0:D], oT[:, h, :], w[:, h, :], start=(h == 0), stop=(h == H - 1))
                        mm.then_inc(y_done, 1)

            @block.scalar
            def _(s):
                with s.Fori(0, B) as b:
                    for q in range(NQ):
                        for i in range(4):
                            s.wait_ge(tr_done, 4 * (b * NQ + q) + (i + 9))
                            nc.scalar.copy(oT[:, 4 * i:4 * i + 4, :].rearrange("p h t -> p (h t)"), tr[i][:, :]).then_inc(oT_ready, 1)

            @block.vector
            def _(v):
                v.sem_inc(z_ready, 2)
                with v.Fori(0, B) as b:
                    for q in range(NQ):
                        v.wait_ge(y_done, b * NQ + (q + 1))
                        nc.vector.tensor_tensor(tile_of(z, b, q), py[q % 2][:, 0:D], tile_of(z, b, q), ALU.add).then_inc(z_ready, 1)


def two_highest(c, name, logits, iota, eq, pair):
    nc = c.nc
    K = 2
    with ExitStack() as ctx:
        def sb(n, shape, dt=F32):
            return ctx.enter_context(nc.sbuf_tensor(f"{name}_{n}", shape, dt))

        top, idx, idxf = sb("top", [P, NT, 8]), sb("idx", [P, NT, 8], U32), sb("idxf", [P, NT, 8])
        diff, ex, den = sb("diff", [P, NT]), sb("ex", [P, NT]), sb("den", [P, NT])
        diff_ready, ex_ready, step = (c.sem(f"{name}_{n}") for n in ("diff", "ex", "step"))
        block = nc.Block()
        with block:
            @block.scalar
            def _(a):
                a.wait_ge(diff_ready, 1)
                nc.scalar.activation(ex[:, :], diff[:, :], ACT.Exp).then_inc(ex_ready, 1)

            @block.vector
            def _(v):
                nv = nc.vector
                link = Chain(v, step).link
                for t in range(NT):
                    ins = nv.max(top[:, t, :], logits[:, t, :])
                link(ins)
                nv.tensor_tensor(diff[:, :], top[:, :, 1], top[:, :, 0], ALU.subtract).then_inc(diff_ready, 1)
                for t in range(NT):
                    ins = nv.max_index(idx[:, t, :], top[:, t, :], logits[:, t, :])
                link(ins)
                link(nv.tensor_copy(idxf[:, :, :], idx[:, :, :]))
                link(nv.tensor_tensor(eq[:, :, :, :], idxf[:, :, 0:K].unsqueeze(2).to_broadcast([P, NT, E1, K]),
                                      iota[:, 0:E1].unsqueeze(1).unsqueeze(3).to_broadcast([P, NT, E1, K]), ALU.is_equal))
                v.wait_ge(ex_ready, 1)
                link(nv.tensor_scalar(den[:, :], ex[:, :], 1.0, None, ALU.add))
                link(nv.reciprocal(pair[:, :, 0], den[:, :]))
                link(nv.tensor_tensor(pair[:, :, 1], pair[:, :, 0], ex[:, :], ALU.mult))




def routed_slots(c, name, eq, before, iota, pos, block_expert):
    nc = c.nc
    with ExitStack() as ctx:
        def sb(n, shape, dt=F32):
            return ctx.enter_context(nc.sbuf_tensor(f"{name}_{n}", shape, dt))

        ones, chosen = sb("ones", [P, P]), sb("chosen", [P, NT, E1])
        total = sb("total", [P, NT, E1])
        cum = [sb("cum0", [P, NT, E1]), sb("cum1", [P, NT, E1])]
        above, thr = sb("above", [P, E1, 8]), sb("thr", [P, 8])
        nb, off = sb("nb", [P, E1]), [sb("off0", [P, E1]), sb("off1", [P, E1])]
        base, prod, posf = sb("base", [P, NT, E1]), sb("prod", [P, NT, E1]), sb("posf", [P, 2, NT])
        cmp, eb = sb("cmp", [P, BLOCKS, E1]), sb("eb", [P, BLOCKS])
        step, counted, ones_ready, chosen_ready = (c.sem(f"{name}_{n}") for n in ("step", "counted", "ones", "chosen"))
        rank, tile_total = c.bank[0], c.bank[1]
        block = nc.Block()
        with block:
            @block.gpsimd
            def _(g):
                g.memset(ones[:, :], 1.0).then_inc(ones_ready, 1)

            @block.tensor
            def _(pe):
                pe.wait_ge(ones_ready, 1)
                pe.wait_ge(chosen_ready, 1)
                flat = chosen[:, :, :].rearrange("p t e -> p (t e)")
                nc.tensor.matmul(rank[:, 0:NT * E1], before[:, :], flat, start=True, stop=True)
                nc.tensor.matmul(tile_total[:, 0:NT * E1], ones[:, :], flat, start=True, stop=True).then_inc(counted, 1)

            @block.vector
            def _(v):
                nv = nc.vector
                link = Chain(v, step).link
                nv.tensor_reduce(chosen[:, :, :], eq[:, :, :, :], AX.X, ALU.add).then_inc(chosen_ready, 1)
                link(nv.tensor_scalar(thr[:, :], iota[:, 0:8], float(SLOTS), None, ALU.mult))
                v.wait_ge(counted, 1)
                link(nv.tensor_copy(total[:, :, :].rearrange("p t e -> p (t e)"), tile_total[:, 0:NT * E1]))
                src = total
                for i, d in enumerate((1, 2, 4, 8)):
                    dst = cum[i % 2]
                    link(nv.tensor_copy(dst[:, 0:d, :], src[:, 0:d, :]))
                    link(nv.tensor_tensor(dst[:, d:, :], src[:, d:, :], src[:, 0:NT - d, :], ALU.add))
                    src = dst
                count = src[:, NT - 1, :]
                link(nv.tensor_tensor(above[:, :, :], count.unsqueeze(2).to_broadcast([P, E1, 8]),
                                      thr[:, :].unsqueeze(1).to_broadcast([P, E1, 8]), ALU.is_gt))
                link(nv.tensor_reduce(nb[:, :], above[:, :, :], AX.X, ALU.add))
                blocks = nb
                for i, d in enumerate((1, 2, 4)):
                    dst = off[i % 2]
                    link(nv.tensor_copy(dst[:, 0:d], blocks[:, 0:d]))
                    link(nv.tensor_tensor(dst[:, d:], blocks[:, d:], blocks[:, 0:E1 - d], ALU.add))
                    blocks = dst
                first = off[1]
                link(nv.tensor_tensor(first[:, :], blocks[:, :], nb[:, :], ALU.subtract))
                link(nv.tensor_tensor(base[:, :, :], src[:, :, :], total[:, :, :], ALU.subtract))
                link(nv.tensor_tensor(base[:, :, :].rearrange("p t e -> p (t e)"), rank[:, 0:NT * E1],
                                      base[:, :, :].rearrange("p t e -> p (t e)"), ALU.add))
                link(nv.tensor_scalar(off[0][:, :], first[:, :], float(SLOTS), None, ALU.mult))
                link(nv.tensor_tensor(base[:, :, :], base[:, :, :], off[0][:, :].unsqueeze(1).to_broadcast([P, NT, E1]), ALU.add))
                for k in range(2):
                    link(nv.tensor_tensor(prod[:, :, :], base[:, :, :], eq[:, :, :, k], ALU.mult))
                    link(nv.tensor_reduce(posf[:, k, :], prod[:, :, :], AX.X, ALU.add))
                    link(nv.tensor_copy(pos[k][:, :], posf[:, k, :]))
                link(nv.tensor_tensor(cmp[:, :, :], first[:, :].unsqueeze(1).to_broadcast([P, BLOCKS, E1]),
                                      iota[:, 0:BLOCKS].unsqueeze(2).to_broadcast([P, BLOCKS, E1]), ALU.is_le))
                link(nv.tensor_reduce(eb[:, :], cmp[:, :, :], AX.X, ALU.add))
                link(nv.tensor_scalar(eb[:, :], eb[:, :], -1.0, None, ALU.add))
                link(nv.tensor_copy(block_expert[:, :], eb[:, :]))


def scatter_rows(c, name, h, pos, h_slots):
    nc = c.nc
    done = c.sem(f"{name}_done")
    block = nc.Block()
    with block:
        @block.gpsimd
        def _(g):
            for t in range(NT):
                for k in range(2):
                    g.indirect_dma_start(h_slots[:, :], bass.IndirectOffsetOnAxis(ap=pos[k][:, t:t + 1], axis=0),
                                         h[:, t, :], None).then_inc(done, 16)
            g.wait_ge(done, 16 * 2 * NT)


def swiglu_blocks(c, name, h_slots, y_slots, w, col_scale, block_expert):
    nc = c.nc
    WU, WF = KT * 2 * F1, KT * 2 * F1 + FC1 * D
    NI = SLOTS // P
    LAST = BLOCKS - 1
    assert BLOCKS % 2 == 1
    with ExitStack() as ctx:
        def sb(n, shape):
            return ctx.enter_context(nc.sbuf_tensor(f"{name}_{n}", shape, F32))

        def sem(n):
            return c.sem(f"{name}_{n}")

        ws = [sb(f"w{s}", [P, WF]) for s in range(2)]
        hs = [sb(f"h{s}", [P, NI, D]) for s in range(2)]
        hT = [sb(f"hT{s}", [P, KT, SLOTS]) for s in range(2)]
        ys = [sb(f"y{s}", [P, NI, D]) for s in range(2)]
        col = sb("col", [P, KT])
        silu, act = sb("silu", [P, 4, SLOTS]), sb("act", [P, FC1, SLOTS])
        w_in, h_in, y_free = ([sem(f"{n}{s}") for s in range(2)] for n in ("w_in", "h_in", "y_free"))
        col_in, tr_done, hT_ready, up_done, silu_ready, act_ready, y_done, y_ready = (
            sem(n) for n in ("col_in", "tr", "hT", "up", "silu", "act", "y_done", "y_ready"))
        ph, py, tr = c.bank[0:4], c.bank[4:6], c.bank[6]
        block = nc.Block()
        with block:
            @block.sync
            def _(sp):
                def load(j, s):
                    expert = sp.value_load(block_expert[0:1, bass.ds(j, 1)], min_val=0, max_val=E1 - 1)
                    sp.dma_start(hs[s][:, :, :], h_slots[bass.ds(j * SLOTS, SLOTS), :].rearrange("(i p) d -> p i d", p=P)).then_inc(h_in[s], 16)
                    sp.dma_start(ws[s][:, :], w[bass.ds(expert, 1), :, :].rearrange("a p n -> p (a n)")).then_inc(w_in[s], 16)

                def store(j, s):
                    sp.wait_ge(y_ready, j + 1)
                    sp.dma_start(y_slots[bass.ds(j * SLOTS, SLOTS), :].rearrange("(i p) d -> p i d", p=P), ys[s][:, :, :]).then_inc(y_free[s], 16)

                for s in range(2):
                    sp.sem_inc(y_free[s], 16)
                sp.dma_start(col[:, :], col_scale).then_inc(col_in, 16)
                load(0, 0)
                load(1, 1)
                with sp.Fori(1, BLOCKS // 2) as m:
                    for s in range(2):
                        sp.wait_ge(y_done, 2 * m + (s - 1))
                        load(2 * m + s, s)
                        store(2 * m + (s - 2), s)
                sp.wait_ge(y_done, LAST - 1)
                load(LAST, 0)
                for j in range(LAST - 2, LAST + 1):
                    store(j, j % 2)
                sp.wait_ge(y_free[0], 16 * (BLOCKS // 2 + 2))
                sp.wait_ge(y_free[1], 16 * (BLOCKS // 2 + 1))

            @block.tensor
            def _(pe):
                def turn(m, s):
                    pe.wait_ge(h_in[s], 16 * m + 16)
                    for k in range(KT):
                        for i in range(NI):
                            mm = nc.tensor.transpose(tr[:, k * SLOTS + i * P:k * SLOTS + (i + 1) * P], hs[s][:, i, k * P:(k + 1) * P], c.ident[:, :])
                    mm.then_inc(tr_done, 1)

                def experts(m, s, following):
                    j = 2 * m + s
                    up, down = ws[s][:, 0:WU].rearrange("p (k i f) -> p k i f", k=KT, i=2), ws[s][:, WU:].rearrange("p (f n) -> p f n", n=D)
                    pe.wait_ge(hT_ready, 2 * j + 2)
                    pe.wait_ge(w_in[s], 16 * m + 16)
                    for f in range(FC1):
                        if f >= 4:
                            pe.wait_ge(act_ready, FC1 * j + (f - 3))
                        for i in range(2):
                            for k in range(KT):
                                mm = nc.tensor.matmul(ph[f % 4][:, i * SLOTS:(i + 1) * SLOTS], up[:, k, i, f * P:(f + 1) * P],
                                                      hT[s][:, k, :], start=(k == 0), stop=(k == KT - 1))
                        mm.then_inc(up_done, 1)
                    if following:
                        turn(*following)
                    for i in range(NI):
                        for f in range(FC1):
                            if i == 0:
                                pe.wait_ge(act_ready, FC1 * j + (f + 1))
                            mm = nc.tensor.matmul(py[s][:, i * D:(i + 1) * D], act[:, f, i * P:(i + 1) * P], down[:, f, :],
                                                  start=(f == 0), stop=(f == FC1 - 1))
                    mm.then_inc(y_done, 1)

                turn(0, 0)
                with pe.Fori(0, BLOCKS // 2) as m:
                    experts(m, 0, (m, 1))
                    experts(m, 1, (m + 1, 0))
                experts(LAST // 2, 0, None)

            @block.scalar
            def _(a):
                def keep_hT(j, s):
                    a.wait_ge(tr_done, j + 1)
                    for k in range(KT):
                        nc.scalar.activation(hT[s][:, k, :], tr[:, k * SLOTS:(k + 1) * SLOTS], ACT.Copy, scale=col[:, k:k + 1]).then_inc(hT_ready, 1)

                def silus(j):
                    for f in range(FC1):
                        a.wait_ge(up_done, FC1 * j + (f + 1))
                        nc.scalar.activation(silu[:, f % 4, :], ph[f % 4][:, 0:SLOTS], ACT.Silu).then_inc(silu_ready, 1)

                a.wait_ge(col_in, 16)
                keep_hT(0, 0)
                with a.Fori(0, BLOCKS // 2) as m:
                    for s in range(2):
                        silus(2 * m + s)
                        keep_hT(2 * m + s + 1, 1 - s)
                silus(LAST)

            @block.vector
            def _(v):
                def experts(m, s):
                    j = 2 * m + s
                    for f in range(FC1):
                        v.wait_ge(silu_ready, FC1 * j + (f + 1))
                        nc.vector.tensor_tensor(act[:, f, :], ph[f % 4][:, SLOTS:], silu[:, f % 4, :], ALU.mult).then_inc(act_ready, 1)
                    v.wait_ge(y_done, j + 1)
                    v.wait_ge(y_free[s], 16 * m + 16)
                    nc.vector.tensor_copy(ys[s][:, :, :].rearrange("p i d -> p (i d)"), py[s][:, :]).then_inc(y_ready, 1)

                with v.Fori(0, BLOCKS // 2) as m:
                    for s in range(2):
                        experts(m, s)
                experts(LAST // 2, 0)


def combine(c, name, y_slots, pos, pair, z):
    nc = c.nc
    with ExitStack() as ctx:
        def sb(n, shape):
            return ctx.enter_context(nc.sbuf_tensor(f"{name}_{n}", shape, F32))

        norm = Norm(c, ctx, name)
        got = [sb(f"got{k}", [P, NT, D]) for k in range(2)]
        y, t = sb("y", [P, NQ, D]), sb("t", [P, NQ, D])
        in_ = [c.sem(f"{name}_in{b}") for b in range(B)]
        y_ready, t_ready, x_ready = (c.sem(f"{name}_{n}") for n in ("y_ready", "t_ready", "x_ready"))
        block = nc.Block()
        with block:
            @block.gpsimd
            def _(g):
                for i in range(NT):
                    for k in range(2):
                        g.indirect_dma_start(got[k][:, i, :], None, y_slots[:, :],
                                             bass.IndirectOffsetOnAxis(ap=pos[k][:, i:i + 1], axis=0)).then_inc(in_[i // NQ], 16)
                for b in range(B):
                    norm.root(g, b)

            @block.vector
            def _(v):
                for b in range(B):
                    v.wait_ge(in_[b], 16 * 2 * NQ)
                    for q in range(NQ):
                        i = b * NQ + q
                        nc.vector.scalar_tensor_tensor(out=y[:, q, :], in0=got[0][:, i, :], scalar=pair[:, i, 0:1], in1=z[:, i, :],
                                                       op0=ALU.mult, op1=ALU.add).then_inc(y_ready, 1)
                    for q in range(NQ):
                        i = b * NQ + q
                        v.wait_ge(y_ready, 2 * NQ * b + q + 1)
                        nc.vector.scalar_tensor_tensor(out=y[:, q, :], in0=got[1][:, i, :], scalar=pair[:, i, 1:2], in1=y[:, q, :],
                                                       op0=ALU.mult, op1=ALU.add).then_inc(y_ready, 1)
                    v.wait_ge(y_ready, 2 * NQ * (b + 1))
                    norm.statistics(v, b, lambda q: y[:, q, :])
                    norm.wait(v, b)
                    add_normed(c, v, norm, b, lambda q: y[:, q, :], t, t_ready, x_ready)


def build(nc, a, out):
    with ExitStack() as ctx:
        c = Core(nc, ctx)
        iota = c.sb("iota", [P, E0], F32)
        before = c.sb("before", [P, P], F32)
        load_constants(c, a, iota, before)
        q_parts = nc.dram_tensor("q_parts", [3, QUADS, 4 * HD, S], BF16, kind="Internal").ap()
        k_parts = nc.dram_tensor("k_parts", [3, QUADS, 4 * HD, S], BF16, kind="Internal").ap()

        with ExitStack() as stage:
            vals = stage.enter_context(nc.sbuf_tensor("a_vals", [P, B * H, NQ, HD], F32))
            attended = stage.enter_context(nc.sbuf_tensor("a_attended", [P, NT, D], F32))
            narrow_projection(c, "a_in", a["a_wqk"], a["a_wv"], a["a_bqk"], a["a_bv"], None, q_parts, k_parts, vals)
            narrow_attention(c, "a_att", q_parts, k_parts, vals, attended, causal=True)
            narrow_output(c, "a_out", attended, a["a_wout"], a["a_bout"], 1.0)
        c.end_stage()

        with ExitStack() as stage:
            def sb(n, shape):
                return stage.enter_context(nc.sbuf_tensor(n, shape, F32))

            hT, logits, gates, acc = sb("b_hT", [P, KT, T]), sb("b_lg", [P, NT, E0]), sb("b_gates", [P, NT, E0]), sb("b_acc", [P, NT, D])
            router_input(c, "b_in", c.x, False, None, a["b_wr"], a["b_br"], E0, hT, None, logits)
            sigmoid_gates(c, "b_gate", logits, iota, gates)
            relu2_experts(c, "b_moe", hT, gates, a["b_w"], acc)
            add_normed_sum(c, "b_out", acc)
        c.end_stage()

        with ExitStack() as stage:
            vals = stage.enter_context(nc.sbuf_tensor("c_vals", [P, B * H, NQ, HD], F32))
            attended = stage.enter_context(nc.sbuf_tensor("c_attended", [P, NT, D], F32))
            lambdas = {"vectors": a["c_lambdas"], "halves": a["c_halves"]}
            narrow_projection(c, "c_in", a["c_wqk"], a["c_wv"], None, None, lambdas, q_parts, k_parts, vals)
            narrow_attention(c, "c_att", q_parts, k_parts, vals, attended, causal=False)
            narrow_output(c, "c_out", attended, a["c_wout"], None, 1.0 - LAMBDA_INIT)
        c.end_stage()

        q_dram = nc.dram_tensor("q_dram", [QUADS, P, 4, S], F32, kind="Internal").ap()
        k_dram = nc.dram_tensor("k_dram", [QUADS, P, 1, S], F32, kind="Internal").ap()
        o_dram = nc.dram_tensor("o_dram", [B * H, S, GD], F32, kind="Internal").ap()
        z = c.sb("z", [P, NT, D], F32)
        with ExitStack() as stage:
            vals = stage.enter_context(nc.sbuf_tensor("d_vals", [P, QUADS, NQ, GD], F32))
            grouped_projection(c, "d_in", a, z, vals, q_dram, k_dram)
            attention(c, "d_att", q_dram, k_dram, vals, o_dram, narrow=False, causal=True)
            grouped_output(c, "d_out", o_dram, a["d_wo"], z)
        c.end_stage()
        with ExitStack() as stage:
            def sb(n, shape):
                return stage.enter_context(nc.sbuf_tensor(n, shape, F32))

            h_slots = nc.dram_tensor("h_slots", [BLOCKS * SLOTS, D], F32, kind="Internal").ap()
            y_slots = nc.dram_tensor("y_slots", [BLOCKS * SLOTS, D], F32, kind="Internal").ap()
            eq, pair = sb("e_eq", [P, NT, E1, 2]), sb("e_pair", [P, NT, 2])
            pos = [stage.enter_context(nc.sbuf_tensor(f"e_pos{k}", [P, NT], U32)) for k in range(2)]
            block_expert = stage.enter_context(nc.sbuf_tensor("e_block_expert", [P, BLOCKS], I32))
            with ExitStack() as routing:
                h = routing.enter_context(nc.sbuf_tensor("e_h", [P, NT, D], F32))
                logits = routing.enter_context(nc.sbuf_tensor("e_lg", [P, NT, E1], F32))
                router_input(c, "e_in", z, True, a["e_ln"], a["e_wr"], None, E1, None, h, logits, h_slots)
                two_highest(c, "e_gate", logits, iota, eq, pair)
                routed_slots(c, "e_slots", eq, before, iota, pos, block_expert)
                scatter_rows(c, "e_scatter", h, pos, h_slots)
            swiglu_blocks(c, "e_moe", h_slots, y_slots, a["e_w"], a["e_ln"], block_expert)
            combine(c, "e_out", y_slots, pos, pair, z)
        c.end_stage()

        done = c.sem("done")
        with nc.Block() as block:
            @block.sync
            def _(sp):
                sp.dma_start(out.rearrange("b (q p) d -> p (b q) d", p=P), c.x[:, :, :]).then_inc(done, 16)
                sp.wait_ge(done, 16)


def laid_out(i):
    import numpy as np
    i = {k: np.asarray(v) for k, v in i.items()}
    r = np.arange(P)
    wa, wc = i["L0_attn_W_qkv"], i["L1_attn_W_attn"]
    half = HD // 2
    pair = [wc[:, j * D // 2:(j + 1) * D // 2].reshape(D, H, half) for j in range(4)]
    w1 = np.concatenate([i["L0_ffn_W1"], i["L0_ffn_Ws1"].reshape(2, M0, D)])
    w2 = np.concatenate([i["L0_ffn_W2"], i["L0_ffn_Ws2"].reshape(D, 2, M0).transpose(1, 0, 2)])
    w1 = w1.transpose(0, 2, 1).reshape(E0 + 2, KT, P, M0).transpose(0, 2, 1, 3).reshape(E0 + 2, P, KT * M0)
    b_w = np.concatenate([w1, w2.transpose(0, 2, 1)], axis=2)
    evens_first = np.concatenate([np.arange(0, GD, 2), np.arange(1, GD, 2)])
    wq = i["L1_ffn_wq"].reshape(D, H, GD)[:, :, evens_first].reshape(D, H * GD)
    wk = i["L1_ffn_wk"].reshape(D, KVH, GD)[:, :, evens_first].reshape(D, KVH * GD)
    inv_freq = np.float32(1e6) ** (-np.arange(0, GD, 2, dtype=np.float32) / np.float32(GD))
    angle = (np.arange(S, dtype=np.float32)[:, None] * inv_freq[None, :]).T.astype(np.float64)
    rope = np.stack([np.concatenate([np.cos(angle), np.cos(angle)]),
                     np.concatenate([np.sin(angle), -np.sin(angle)])], axis=1)
    rope = np.stack([rope / np.sqrt(GD), rope], axis=1).astype(np.float32)
    e_up = np.stack([i["L1_ffn_w1"], i["L1_ffn_w3"]], axis=2)
    e_up = e_up.reshape(E1, KT, P, 2 * F1).transpose(0, 2, 1, 3).reshape(E1, P, KT * 2 * F1)
    e_down = i["L1_ffn_w2"].reshape(E1, FC1, P, D).transpose(0, 2, 1, 3).reshape(E1, P, FC1 * D)
    return {
        "d_wqk": np.concatenate([wq, wk], axis=1), "d_wv": i["L1_ffn_wv"], "d_wo": i["L1_ffn_wo"],
        "d_ln": i["L1_ffn_ln_w"].reshape(KT, P).T, "d_rope": rope,
        "e_ln": i["L1_ffn_ff_ln_w"].reshape(KT, P).T, "e_wr": i["L1_ffn_gate_w"],
        "e_w": np.concatenate([e_up, e_down], axis=2),
        "x": i["L0_attn_x"],
        "ident": np.eye(P, dtype=np.float32),
        "causal": np.where(r[None, :] <= r[:, None], 0.0, -1e38).astype(np.float32),
        "before": (r[:, None] < r[None, :]).astype(np.float32),
        "iota": np.arange(E0, dtype=np.float32),
        "a_wqk": wa[:, :2 * D], "a_wv": wa[:, 2 * D:], "a_bqk": i["L0_attn_b_qkv"][:2 * D].reshape(4, P).T,
        "a_bv": i["L0_attn_b_qkv"][2 * D:], "a_wout": i["L0_attn_W_out"], "a_bout": i["L0_attn_b_out"],
        "b_wr": i["L0_ffn_Wr"].T, "b_br": i["L0_ffn_br"],
        "b_w": b_w.reshape(E0 // 2 + 1, 2, P, KT * M0 + D).transpose(0, 2, 1, 3),
        "c_wqk": np.concatenate([np.concatenate([pair[j], pair[j + 2]], axis=2).reshape(D, D) for j in range(2)], axis=1),
        "c_wv": wc[:, 2 * D:], "c_wout": i["L1_attn_W_proj"],
        "c_lambdas": np.stack([i[f"L1_attn_lambda_{n}"] for n in ("q1", "k1", "q2", "k2")]),
        "c_halves": np.stack([-(r % HD >= half).astype(np.float32), (r % HD < half).astype(np.float32)], axis=1),
    }


def kernel(**inputs):
    import numpy as _np
    import concourse.bacc as _bacc
    from concourse import mybir as _mybir
    from concourse.bass_utils import run_bass_kernel_spmd as _run

    nc = _bacc.Bacc("TRN2", target_bir_lowering=False, num_devices=1)
    arrays, args = {}, {}
    for name, a in laid_out(inputs).items():
        a = _np.ascontiguousarray(a)
        arrays[f"in_{name}"] = a
        args[name] = nc.dram_tensor(f"in_{name}", a.shape, _mybir.dt.from_np(a.dtype), kind="ExternalInput").ap()
    out = nc.dram_tensor("out", (B, S, D), F32, kind="ExternalOutput").ap()
    build(nc, args, out)
    return _run(nc, [arrays], core_ids=[0]).results[0]["out"]
```

```python
from contextlib import ExitStack

import concourse.bass as bass
from concourse import mybir

F32 = mybir.dt.float32
F32R = mybir.dt.float32r
BF16 = mybir.dt.bfloat16
U32 = mybir.dt.uint32
I32 = mybir.dt.int32
ALU = mybir.AluOpType
ACT = mybir.ActivationFunctionType
AX = mybir.AxisListType

P = 128
B, S, D = 4, 512, 256
KT = D // P
NQ = S // P
NT = B * NQ
T = B * S
H = 16
QUADS = B * H // 4
HD = D // H
GD, KVH = 128, 4
EPS = 1e-5
LAMBDA_INIT = 0.8 - 0.6
E0, K0, M0, G0, SCALE0 = 32, 6, 128, 8, 2.5
E1, F1 = 8, 896
FC1 = F1 // P
SLOTS = 256
BLOCKS = (2 * T - E1) // SLOTS + E1

Q_PART = [0, 0, 0, 1, 1, 1, 2, 2]
K_PART = [0, 1, 2, 0, 1, 2, 0, 1]


class Core:

    def __init__(self, nc, ctx):
        self.nc, self.ctx, self.sems = nc, ctx, []
        self.x = self.sb("x", [P, NT, D], F32)
        self.ident = self.sb("ident", [P, P], F32)
        self.identb = self.sb("identb", [P, P], BF16)
        self.causal = self.sb("causal", [P, P], BF16)
        self.mhalf = self.sb("mhalf", [P, NQ], F32)
        self.bank = [ctx.enter_context(nc.psum_tensor(f"bank{i}", [P, 512], F32)) for i in range(8)]

    def sb(self, name, shape, dt):
        return self.ctx.enter_context(self.nc.sbuf_tensor(name, shape, dt))

    def sem(self, name):
        self.sems.append(self.nc.alloc_semaphore(name))
        return self.sems[-1]

    def end_stage(self):
        self.nc.clear_and_free_semaphores(self.sems)
        self.nc.all_engine_barrier()
        self.sems = []


def weights(ap):
    return ap.rearrange("(k p) n -> p k n", p=P)


def hold(eng, spare):
    eng.sem_inc(spare, 1)


class Norm:

    def __init__(self, c, ctx, name):
        nc = c.nc

        def sb(n, shape):
            return ctx.enter_context(nc.sbuf_tensor(f"{name}_{n}", shape, F32))

        self.c = c
        self.st, self.mv = sb("st", [P, NQ, 6]), sb("mv", [P, NQ, 2])
        self.ve, self.r = sb("ve", [P, NQ]), sb("r", [P, NQ])
        self.stats_done, self.mean_done, self.var_done, self.root_done, self.spare = (
            c.sem(f"{name}_{n}") for n in ("stats", "mean", "var", "root", "carry"))

    def statistics(self, v, b, tile, rms=False):
        nv = self.c.nc.vector
        hold(v, self.spare)
        for q in range(NQ):
            nv.bn_stats(self.st[:, q, :], tile(q)).then_inc(self.stats_done, 1)
        v.wait_ge(self.stats_done, b * NQ + NQ)
        hold(v, self.spare)
        for q in range(NQ):
            nv.bn_aggr(self.mv[:, q, :], self.st[:, q, :]).then_inc(self.mean_done, 1)
        v.wait_ge(self.mean_done, b * NQ + NQ)
        if rms:
            nv.tensor_tensor(self.ve[:, :], self.mv[:, :, 0], self.mv[:, :, 0], ALU.mult).then_inc(self.var_done, 1)
            v.wait_ge(self.var_done, b * 2 + 1)
            nv.scalar_tensor_tensor(out=self.ve[:, :], in0=self.mv[:, :, 1], scalar=EPS, in1=self.ve[:, :],
                                    op0=ALU.add, op1=ALU.add).then_inc(self.var_done, 1)
        else:
            nv.tensor_scalar(self.ve[:, :], self.mv[:, :, 1], EPS, None, ALU.add).then_inc(self.var_done, 1)

    def root(self, g, b, rms=False):
        g.wait_ge(self.var_done, b * (1 + rms) + 1 + rms)
        g.tensor_tensor(self.r[:, :], self.ve[:, :], self.c.mhalf[:, :], ALU.pow).then_inc(self.root_done, 1)

    def wait(self, v, b):
        v.wait_ge(self.root_done, b + 1)

    def apply(self, q, out, tile, rms=False):
        nv = self.c.nc.vector
        if rms:
            return nv.tensor_scalar(out, tile, self.r[:, q:q + 1], None, ALU.mult)
        return nv.tensor_scalar(out, tile, self.mv[:, q, 0:1], self.r[:, q:q + 1], ALU.subtract, ALU.mult)


def tile_of(x, b, q):
    return x[:, bass.ds(b * NQ + q, 1), :].rearrange("p a d -> p (a d)")


def load_constants(c, a, iota, before):
    nc = c.nc
    x_in, mask_in, cast = c.sem("x_in"), c.sem("mask_in"), c.sem("cast")
    with ExitStack() as ctx:
        mask = ctx.enter_context(nc.sbuf_tensor("mask", [P, P], F32))
        block = nc.Block()
        with block:
            @block.sync
            def _(sp):
                sp.dma_start(c.ident[:, :], a["ident"]).then_inc(mask_in, 16)
                sp.dma_start(mask[:, :], a["causal"]).then_inc(mask_in, 16)
                sp.dma_start(before[:, :], a["before"]).then_inc(mask_in, 16)
                sp.dma_start(iota[:, :], a["iota"].partition_broadcast(P)).then_inc(mask_in, 16)
                sp.dma_start(c.x[:, :, :], a["x"].rearrange("b (q p) d -> p (b q) d", p=P)).then_inc(x_in, 16)
                sp.wait_ge(x_in, 16)

            @block.vector
            def _(v):
                v.wait_ge(mask_in, 64)
                nc.vector.tensor_copy(c.identb[:, :], c.ident[:, :]).then_inc(cast, 1)
                nc.vector.tensor_copy(c.causal[:, :], mask[:, :]).then_inc(cast, 1)

            @block.gpsimd
            def _(g):
                g.memset(c.mhalf[:, :], -0.5)


def narrow_projection(c, name, w_qk, w_v, b_qk, b_v, lambdas, q_parts, k_parts, vals):
    nc = c.nc
    with ExitStack() as ctx:
        def sb(n, shape, dt=F32):
            return ctx.enter_context(nc.sbuf_tensor(f"{name}_{n}", shape, dt))

        def sem(n):
            return c.sem(f"{name}_{n}")

        norm = Norm(c, ctx, name)
        wqk, wv = sb("wqk", [P, KT, 512]), sb("wv", [P, KT, D])
        biasqk, biasv = sb("bqk", [P, 4]), sb("bv", [P, D])
        mul = sb("mul", [P, 2])
        h = sb("h", [P, NQ, D])
        hT = sb("hT", [P, KT, S])
        xp = sb("xp", [P, 4, S])
        r1 = sb("r1", [P, 4, S])
        parts = sb("parts", [P, 4, 3, S], BF16)
        w_in, mul_ready = sem("w_in"), sem("mul_ready")
        h_ready, tr_done, hT_ready = sem("h_ready"), sem("tr_done"), sem("hT_ready")
        qk_done, v_done, v_kept = sem("qk_done"), sem("v_done"), sem("v_kept")
        xp_ready, hi_ready, r1_ready, mid_ready, lo_ready = (
            sem(n) for n in ("xp_ready", "hi_ready", "r1_ready", "mid_ready", "lo_ready"))
        stored, parts_free = sem("stored"), sem("parts_free")
        tr, ps, pv = c.bank[0:2], c.bank[2:6], c.bank[6:8]
        n_w = 2 + 2 * (lambdas is None)
        if lambdas is not None:
            lam_in, lam_ex, lam_sem, lam_exp = sb("lam_in", [P, 4, D]), sb("lam_ex", [P, 8]), sem("lam"), sem("lam_exp")
            halves = sb("halves", [P, 2])
            n_w = 4
        block = nc.Block()
        with block:
            @block.sync
            def _(sp):
                sp.sem_inc(parts_free, 1)
                sp.dma_start(wqk[:, :, :], weights(w_qk)).then_inc(w_in, 16)
                sp.dma_start(wv[:, :, :], weights(w_v)).then_inc(w_in, 16)
                if lambdas is None:
                    sp.dma_start(biasqk[:, :], b_qk).then_inc(w_in, 16)
                    sp.dma_start(biasv[:, :], b_v.partition_broadcast(P)).then_inc(w_in, 16)
                else:
                    sp.dma_start(lam_in[:, :, :], lambdas["vectors"].partition_broadcast(P)).then_inc(w_in, 16)
                    sp.dma_start(halves[:, :], lambdas["halves"]).then_inc(w_in, 16)
                with sp.Fori(0, B) as b:
                    for cc in range(4):
                        dst = (q_parts if cc < 2 else k_parts)[:, bass.ds(b * 4 + 2 * (cc % 2), 2), :, :]
                        sp.wait_ge(lo_ready, b * 4 + cc + 1)
                        sp.dma_start(dst.rearrange("t g r s -> (g r) t s"), parts[:, cc, :, :]).then_inc(stored, 16)
                    sp.wait_ge(stored, b * 64 + 64)
                    sp.sem_inc(parts_free, 1)

            @block.vector
            def _(v):
                def apply(b):
                    norm.wait(v, b)
                    v.wait_ge(tr_done, b * KT + 2)
                    for q in range(NQ):
                        norm.apply(q, h[:, q, :], tile_of(c.x, b, q)).then_inc(h_ready, 1)

                norm.statistics(v, 0, lambda q: tile_of(c.x, 0, q))
                apply(0)
                v.wait_ge(w_in, 16 * n_w)
                if lambdas is None:
                    nc.vector.memset(mul[:, 0:1], HD ** -0.5).then_inc(mul_ready, 1)
                    nc.vector.memset(mul[:, 1:2], 1.0).then_inc(mul_ready, 1)
                    v.wait_ge(mul_ready, 2)
                else:
                    half_scale = (HD // 2) ** -0.5
                    for i in range(2):
                        nc.vector.tensor_tensor_reduce(lam_in[:, 2 * i, :], lam_in[:, 2 * i, :], lam_in[:, 2 * i + 1, :],
                                                       1.0, 0.0, ALU.mult, ALU.add, lam_ex[:, i:i + 1]).then_inc(lam_sem, 1)
                    v.wait_ge(lam_exp, 1)
                    nc.vector.tensor_tensor(lam_ex[:, 4:5], lam_ex[:, 2:3], lam_ex[:, 3:4], ALU.subtract).then_inc(lam_sem, 1)
                    v.wait_ge(lam_sem, 3)
                    nc.vector.tensor_scalar(lam_ex[:, 5:6], lam_ex[:, 4:5], LAMBDA_INIT, None, ALU.add).then_inc(lam_sem, 1)
                    v.wait_ge(lam_sem, 4)
                    nc.vector.tensor_scalar(mul[:, 1:2], halves[:, 0:1], lam_ex[:, 5:6], halves[:, 1:2],
                                            ALU.mult, ALU.add).then_inc(mul_ready, 1)
                    nc.vector.memset(mul[:, 0:1], half_scale).then_inc(mul_ready, 1)
                    nc.vector.memset(biasqk[:, :], 0.0).then_inc(mul_ready, 1)
                    v.wait_ge(mul_ready, 3)
                def group(b, last):
                    if not last:
                        norm.statistics(v, b + 1, lambda q: tile_of(c.x, b + 1, q))
                    for cc in range(4):
                        v.wait_ge(qk_done, b * 4 + cc + 1)
                        nc.vector.tensor_scalar(xp[:, cc, :], ps[cc][:, :], biasqk[:, cc:cc + 1],
                                                mul[:, cc // 2:cc // 2 + 1], ALU.add, ALU.mult).then_inc(xp_ready, 1)
                    if not last:
                        apply(b + 1)
                    for q in range(NQ):
                        v.wait_ge(v_done, b * 2 + q // 2 + 3)
                        dst = vals[:, bass.ds(b * H, H), q, :]
                        src = pv[q // 2][:, (q % 2) * D:(q % 2 + 1) * D].rearrange("p (h d) -> p h d", d=HD)
                        if lambdas is None:
                            nc.vector.tensor_tensor(dst, src, biasv[:, :].rearrange("p (h d) -> p h d", d=HD),
                                                    ALU.add).then_inc(v_kept, 1)
                        else:
                            nc.vector.tensor_copy(dst, src).then_inc(v_kept, 1)
                    for cc in range(4):
                        v.wait_ge(hi_ready, b * 4 + cc + 1)
                        nc.vector.tensor_tensor(r1[:, cc, :], xp[:, cc, :], parts[:, cc, 0, :], ALU.subtract).then_inc(r1_ready, 1)
                    for cc in range(4):
                        v.wait_ge(mid_ready, b * 4 + cc + 1)
                        v.wait_ge(r1_ready, b * 4 + cc + 1)
                        nc.vector.tensor_tensor(parts[:, cc, 2, :], r1[:, cc, :], parts[:, cc, 1, :], ALU.subtract).then_inc(lo_ready, 1)

                with v.Fori(0, B - 1) as b:
                    group(b, False)
                group(B - 1, True)

            @block.gpsimd
            def _(g):
                with g.Fori(0, B) as b:
                    norm.root(g, b)

            @block.scalar
            def _(a):
                if lambdas is not None:
                    a.wait_ge(lam_sem, 2)
                    nc.scalar.activation(lam_ex[:, 2:4], lam_ex[:, 0:2], ACT.Exp).then_inc(lam_exp, 1)

                def keep_hT(b):
                    for k in range(KT):
                        a.wait_ge(tr_done, b * KT + k + 3)
                        if k == 0:
                            a.wait_ge(v_done, b * 2 + 2)
                        nc.scalar.copy(hT[:, k, :], tr[k][:, :]).then_inc(hT_ready, 1)

                def group(b, last):
                    for cc in range(4):
                        if cc == 0:
                            a.wait_ge(parts_free, b + 1)
                        a.wait_ge(xp_ready, b * 4 + cc + 5)
                        nc.scalar.copy(parts[:, cc, 0, :], xp[:, cc, :]).then_inc(hi_ready, 1)
                    if not last:
                        keep_hT(b + 1)
                    for cc in range(4):
                        a.wait_ge(r1_ready, b * 4 + cc + 1)
                        nc.scalar.copy(parts[:, cc, 1, :], r1[:, cc, :]).then_inc(mid_ready, 1)

                keep_hT(0)
                with a.Fori(0, B - 1) as b:
                    group(b, False)
                group(B - 1, True)

            @block.tensor
            def _(pe):
                def turn(b):
                    for k in range(KT):
                        for q in range(NQ):
                            if k == 0:
                                pe.wait_ge(h_ready, b * NQ + q + 1)
                            mm = nc.tensor.transpose(tr[k][:, q * P:(q + 1) * P], h[:, q, k * P:(k + 1) * P], c.ident[:, :])
                        mm.then_inc(tr_done, 1)

                def group(b, last):
                    pe.wait_ge(hT_ready, b * KT + KT)
                    for cc in range(4):
                        pe.wait_ge(xp_ready, b * 4 + cc + 1)
                        for k in range(KT):
                            mm = nc.tensor.matmul(ps[cc][:, :], wqk[:, k, cc * P:(cc + 1) * P], hT[:, k, :],
                                                  start=(k == 0), stop=(k == KT - 1))
                        mm.then_inc(qk_done, 1)
                    for q in range(NQ):
                        if q % 2 == 0:
                            pe.wait_ge(v_kept, b * 4 + q + 2)
                        for k in range(KT):
                            mm = nc.tensor.matmul(pv[q // 2][:, (q % 2) * D:(q % 2 + 1) * D], hT[:, k, q * P:(q + 1) * P],
                                                  wv[:, k, :], start=(k == 0), stop=(k == KT - 1))
                        if q % 2:
                            mm.then_inc(v_done, 1)
                    if not last:
                        turn(b + 1)

                pe.sem_inc(tr_done, KT)
                pe.sem_inc(v_done, 2)
                pe.sem_inc(xp_ready, 4)
                pe.sem_inc(v_kept, 4)
                turn(0)
                pe.wait_ge(w_in, 16 * n_w)
                with pe.Fori(0, B - 1) as b:
                    group(b, False)
                group(B - 1, True)


def grouped_attention(c, name, q_src, k_src, vals, out):
    nc = c.nc
    width = [(qt + 1) * P for qt in range(NQ)]
    STEPS = B * H
    PRODUCTS = [(0, 0), (0, 1), (1, 0)]
    with ExitStack() as ctx:
        def sb(n, shape, d=F32):
            return ctx.enter_context(nc.sbuf_tensor(f"{name}_{n}", shape, d))

        def sem(n):
            return c.sem(f"{name}_{n}")

        qs = [sb(f"q{s}", [P, 4, S]) for s in range(2)]
        ks = [sb(f"k{s}", [P, 1, S]) for s in range(2)]
        probs = [sb(f"probs{i}", [P, NQ, S]) for i in range(2)]
        pT = [[sb(f"pT{i}_{part}", [P, NQ, S], F32R) for part in ("high", "low")] for i in range(2)]
        vq = [[sb(f"v{i}_{part}", [P, NQ, GD], F32R) for part in ("high", "low")] for i in range(2)]
        nmax, rsum, rinv = sb("nmax", [P, 8, NQ]), sb("rsum", [P, 8, NQ]), sb("rinv", [P, 8, NQ])
        o_slot = [sb(f"o{i}", [P, S]) for i in range(2)]
        loaded = [sem("loaded0"), sem("loaded1")]
        o_free = [sem("o_free0"), sem("o_free1")]
        scores_done, max_ready, exp_done, scaled, turned, high_ready, low_ready, v_high, v_low, pv_done, o_ready, rinv_ready, last_scaled, spare = (
            sem(n) for n in ("scores", "max", "exp", "scaled", "turned", "high", "low", "v_high", "v_low", "pv", "o", "rinv", "last_scaled", "carry"))
        stile, ttile = ([c.bank[3 * i + k][:, 0:width[qt]] for qt, k in enumerate((0, 1, 0, 2))] for i in range(2))
        obank = c.bank[6:8]

        def back(m, j, d):
            return m + (j - d) // 8, (j - d) % 8

        def by_key(t, qt):
            return t[:, 0:qt + 1, qt * P:(qt + 1) * P]

        def turned_tile(qt):
            return ttile[qt].rearrange("p (k q) -> p k q", q=P)

        block = nc.Block()
        with block:
            @block.sync
            def _(sp):
                def load_quad(quad, s):
                    for dst, src in ((qs[s], q_src), (ks[s], k_src)):
                        sp.dma_start(dst[:, :, :], src[bass.ds(quad, 1), :, :, :].rearrange("a p u s -> p (a u) s")
                                     ).then_inc(loaded[s], 16)

                def store(n, j):
                    sp.wait_ge(o_ready, n + 3)
                    sp.dma_start(out[bass.ds(n, 1), :, :].rearrange("a p s -> p (a s)"), o_slot[j % 2][:, :]).then_inc(o_free[j % 2], 16)

                for s in range(2):
                    load_quad(s, s)
                    sp.sem_inc(o_free[s], 16)
                with sp.Fori(1, 8) as m:
                    for j in range(8):
                        store(8 * m + (j - 8), j)
                        if j in (2, 6):
                            s = j // 4
                            sp.wait_ge(scores_done, 32 * m + (16 * s - 16))
                            load_quad(2 * m + s, s)
                for j in range(8):
                    store(56 + j, j)
                for i in range(2):
                    sp.wait_ge(o_free[i], 16 * (STEPS // 2 + 1))

            @block.tensor
            def _(pe):
                def scores(m, j, qt, first=False):
                    s, u, w = j // 4, j % 4, width[qt]
                    if u == 0 and qt == 0:
                        pe.wait_ge(loaded[s], (m + 1) * 32)
                    if qt == 0 and not first:
                        pe.wait_ge(exp_done, NQ * (8 * m + j) - 1)
                    if qt == 2:
                        pe.wait_ge(exp_done, NQ * (8 * m + j) + 1)
                    nc.tensor.matmul(stile[qt], qs[s][:, u, qt * P:(qt + 1) * P], ks[s][:, 0, 0:w], start=True, stop=False)
                    nc.tensor.matmul(stile[qt][:, w - P:w], c.identb[:, :], c.causal[:, :], start=False, stop=True).then_inc(scores_done, 1)

                def values(m, j, kt):
                    n, s = 8 * m + j, j // 4
                    if kt == 0:
                        pe.wait_ge(low_ready, NQ * n + NQ + 4)
                        pe.wait_ge(o_ready, n + 1)
                        if j % 4 == 0:
                            pe.wait_ge(v_low, 2 * m + s + 1)
                    for i, (x, y) in enumerate(PRODUCTS):
                        mm = nc.tensor.matmul(obank[j % 2][:, kt * P:S], vq[s][x][:, kt, :], pT[j % 2][y][:, kt, kt * P:S],
                                              start=(kt == 0 and i == 0), stop=(kt == NQ - 1 and i == 2))
                    if kt == NQ - 1:
                        mm.then_inc(pv_done, 1)

                def step(m, j, following, before):
                    n = 8 * m + j
                    for qt in range(NQ):
                        if qt < NQ - 1:
                            pe.wait_ge(scaled, (NQ - 1) * n + qt + 1)
                        else:
                            pe.wait_ge(last_scaled, n + 1)
                        pe.wait_ge(low_ready, NQ * n + (3, 2, 5, 4)[qt])
                        for kt in range(qt + 1):
                            mm = nc.tensor.transpose(ttile[qt][:, kt * P:(kt + 1) * P],
                                                     probs[j % 2][:, qt, kt * P:(kt + 1) * P], c.ident[:, :])
                        mm.then_inc(turned, 1)
                        if following:
                            scores(*following, qt)
                        if before and qt:
                            values(*before, qt - 1)
                    if before:
                        values(*before, NQ - 1)

                pe.sem_inc(low_ready, NQ)
                pe.sem_inc(o_ready, 2)
                for qt in range(NQ):
                    scores(0, 0, qt, True)
                for j in range(8):
                    step(0, j, back(0, j, -1), (0, j - 1) if j else None)
                with pe.Fori(1, 7) as m:
                    for j in range(8):
                        step(m, j, back(m, j, -1), back(m, j, 1))
                for j in range(8):
                    step(7, j, (7, j + 1) if j < 7 else None, back(7, j, 1))
                for kt in range(NQ):
                    values(7, 7, kt)

            @block.scalar
            def _(a):
                def exponentials(m, j, qt):
                    a.wait_ge(max_ready, NQ * (8 * m + j) + qt + 1)
                    nc.scalar.activation(probs[j % 2][:, qt, 0:width[qt]], stile[qt], ACT.Exp,
                                         bias=nmax[:, j, qt:qt + 1], accum_out=rsum[:, j, qt:qt + 1]).then_inc(exp_done, 1)

                def keep(m, j):
                    a.wait_ge(pv_done, 8 * m + j + 1)
                    a.wait_ge(o_free[j % 2], 16 * (4 * m + j // 2 + 1))
                    nc.scalar.copy(o_slot[j % 2][:, :], obank[j % 2][:, :]).then_inc(o_ready, 1)

                def high_values(quad, s, used):
                    if used is not None:
                        a.wait_ge(pv_done, used)
                    hold(a, spare)
                    nc.scalar.copy(vq[s][0][:, :, :], vals[:, bass.ds(quad, 1), :, :].rearrange("p a k d -> p (a k) d")).then_inc(v_high, 1)

                def step(m, j, first, last):
                    n = 8 * m + j
                    for qt in range(NQ):
                        a.wait_ge(turned, NQ * n + qt + 1)
                        nc.scalar.copy(by_key(pT[j % 2][0], qt), turned_tile(qt)).then_inc(high_ready, 1)
                        if qt == 0:
                            a.wait_ge(rinv_ready, NQ * n + NQ)
                            tile = probs[j % 2][:, NQ - 1, :]
                            nc.scalar.activation(tile, tile, ACT.Copy, scale=rinv[:, j, NQ - 1:NQ]).then_inc(last_scaled, 1)
                        if not (last and j == 7):
                            exponentials(*back(m, j, -1), qt)
                        if qt == 0 and not (first and j < 2):
                            keep(*back(m, j, 2))
                    if j == 1:
                        high_values(2 * m + 1, 1, None if first else 8 * m)
                    if j == 5 and not last:
                        high_values(2 * m + 2, 0, 8 * m + 4)

                high_values(0, 0, None)
                for qt in range(NQ):
                    exponentials(0, 0, qt)
                for j in range(8):
                    step(0, j, True, False)
                with a.Fori(1, 7) as m:
                    for j in range(8):
                        step(m, j, False, False)
                for j in range(8):
                    step(7, j, False, True)
                keep(7, 6)
                keep(7, 7)

            @block.gpsimd
            def _(g):
                with g.Fori(0, STEPS // 8) as m:
                    for j in range(8):
                        for qt in range(NQ - 1):
                            g.wait_ge(rinv_ready, NQ * (8 * m + j) + qt + 1)
                            hold(g, spare)
                            tile = probs[j % 2][:, qt, 0:width[qt]]
                            g.tensor_scalar(tile, tile, rinv[:, j, qt:qt + 1], None, ALU.mult).then_inc(scaled, 1)

            @block.vector
            def _(v):
                def negated_max(m, j, qt):
                    v.wait_ge(scores_done, NQ * (8 * m + j) + qt + 1)
                    nc.vector.tensor_reduce(nmax[:, j, qt:qt + 1], stile[qt], AX.X, ALU.max,
                                            negate=True).then_inc(max_ready, 1)

                def reciprocal(m, j, qt):
                    v.wait_ge(exp_done, NQ * (8 * m + j) + qt + 1)
                    nc.vector.reciprocal(rinv[:, j, qt:qt + 1], rsum[:, j, qt:qt + 1]).then_inc(rinv_ready, 1)

                def low_values(quad, s):
                    v.wait_ge(v_high, quad + 1)
                    nc.vector.tensor_tensor(vq[s][1][:, :, :], vals[:, bass.ds(quad, 1), :, :].rearrange("p a k d -> p (a k) d"),
                                            vq[s][0][:, :, :], ALU.subtract).then_inc(v_low, 1)

                def step(m, j, first, last):
                    for qt in range(NQ):
                        if not (last and j == 7):
                            negated_max(*back(m, j, -1), qt)
                        v.wait_ge(high_ready, NQ * (8 * m + j) + qt + 1)
                        nc.vector.tensor_tensor(by_key(pT[j % 2][1], qt), turned_tile(qt), by_key(pT[j % 2][0], qt),
                                                ALU.subtract).then_inc(low_ready, 1)
                        if not (last and j == 7):
                            reciprocal(*back(m, j, -1), qt)
                    if j == 1:
                        low_values(2 * m + 1, 1)
                    if j == 5 and not last:
                        low_values(2 * m + 2, 0)

                for qt in range(NQ):
                    negated_max(0, 0, qt)
                for qt in range(NQ):
                    reciprocal(0, 0, qt)
                low_values(0, 0)
                for j in range(8):
                    step(0, j, True, False)
                with v.Fori(1, 7) as m:
                    for j in range(8):
                        step(m, j, False, False)
                for j in range(8):
                    step(7, j, False, True)


def narrow_attention(c, name, q_parts, k_parts, vals, out, causal):
    nc = c.nc
    LEAD = 10
    HEADS = B * H
    VW = 32

    def keys(qt):
        return (qt + 1) * P if causal else S

    def first_query(kt):
        return kt * P if causal else 0

    with ExitStack() as ctx:
        def sb(n, shape, d=F32):
            return ctx.enter_context(nc.sbuf_tensor(f"{name}_{n}", shape, d))

        def sem(n):
            return c.sem(f"{name}_{n}")

        qs = [sb(f"q{s}", [P, 4, S], BF16) for s in range(4)]
        ks = [sb(f"k{s}", [P, 4, S], BF16) for s in range(4)]
        probs = [sb(f"probs{i}", [P, NQ, S]) for i in range(2)]
        nmax = sb("nmax", [P, 8, NQ])
        rest = sb("rest", [P, 8, NQ])
        mparts = sb("mparts", [P, NQ, P], BF16)
        mT = [sb(f"mT{i}", [P, S], BF16) for i in range(2)]
        vq = [sb(f"vq{i}", [P, 4, NQ, VW]) for i in range(4)]
        pick_f = sb("pick_f", [P, 8])
        pick = sb("pick", [P, 8, P], BF16)
        oT = sb("oT", [P, S])
        rinv = sb("rinv", [P, NQ, 4])
        loaded = [sem(f"loaded{s}") for s in range(4)]
        rows_done, max_ready, split, max_turned, mT_ready = (
            sem(n) for n in ("rows", "max", "split", "max_turned", "mT"))
        cols_done, exp_done, pv_done, quad_done, oT_ready, o_turned, rinv_ready, o_ready, pick_ready = (
            sem(n) for n in ("cols", "exp", "pv", "quad", "oT", "o_turned", "rinv", "o", "pick"))
        spare, zeroed, held = sem("carry"), sem("zeroed"), sem("held")
        cbank, rbank, obank, mbank = c.bank[0:2], c.bank[2:4], c.bank[4:6], c.bank[6]

        def in_turn(b, h):
            return b + h // H, h % H

        block = nc.Block()
        with block:
            @block.sync
            def _(sp):
                def load_quad(quad, s):
                    for j in range(8):
                        for dst, src, part in ((qs[s], q_parts, Q_PART[j]), (ks[s], k_parts, K_PART[j])):
                            sp.dma_start(dst[16 * j:16 * (j + 1), :, :],
                                         src[part, bass.ds(quad, 1), :, :].rearrange("a (u d) s -> d (a u) s", d=HD)
                                         ).then_inc(loaded[s], 16)

                for s in range(4):
                    load_quad(s, s)
                with sp.Fori(1, B) as b:
                    for s in range(4):
                        sp.wait_ge(cols_done, b * (NQ * H) + (4 * NQ * (s + 1) - NQ * H))
                        load_quad(4 * b + s, s)

            @block.tensor
            def _(pe):
                def rows(b, h, qt):
                    s, u, w = h // 4, h % 4, keys(qt)
                    if u == 0 and qt == 0:
                        pe.wait_ge(loaded[s], (b + 1) * 256)
                    pe.wait_ge(max_ready, NQ * (H * b + h) + qt + 1)
                    mm = nc.tensor.matmul(rbank[qt % 2][:, 0:w], qs[s][:, u, qt * P:(qt + 1) * P], ks[s][:, u, 0:w],
                                          start=True, stop=not causal)
                    if causal:
                        mm = nc.tensor.matmul(rbank[qt % 2][:, w - P:w], c.identb[:, :], c.causal[:, :], start=False, stop=True)
                    mm.then_inc(rows_done, 1)

                def turn_maxima():
                    for qt in range(NQ):
                        mm = nc.tensor.matmul(mbank[:, qt * P:(qt + 1) * P], mparts[:, qt, :], c.identb[:, :],
                                              start=True, stop=True)
                    mm.then_inc(max_turned, 1)

                def cols(b, h, kt):
                    s, u, g, lo = h // 4, h % 4, h // 8, first_query(kt)
                    if h % 8 == 0 and kt == 0:
                        pe.wait_ge(mT_ready, 2 * b + g + 1)
                    dst = cbank[kt % 2]
                    nc.tensor.matmul(dst[:, lo:S], ks[s][:, u, kt * P:(kt + 1) * P], qs[s][:, u, lo:S], start=True, stop=False)
                    if causal:
                        nc.tensor.matmul(dst[:, lo:lo + P], c.causal[:, :], c.identb[:, :], start=False, stop=False)
                    nc.tensor.matmul(dst[:, lo:S], pick[:, h % 8, :], mT[g][:, lo:S], start=False, stop=True
                                     ).then_inc(cols_done, 1)

                def values(b, h, kt):
                    u, lo = h % 4, first_query(kt)
                    if u == 0 and kt == 0:
                        pe.wait_ge(held, 4 * b + h // 4 + 1)
                        pe.wait_ge(o_ready, 4 * b + h // 4 + 1)
                    mm = nc.tensor.matmul(obank[h // 4 % 2][VW * u:VW * (u + 1), lo:S], vq[h // 4][:, u, kt, :], probs[h % 2][:, kt, lo:S],
                                          start=(kt == 0), stop=(kt == NQ - 1))
                    if kt == NQ - 1:
                        mm.then_inc(pv_done, 1)

                def turn_quad(b, quad):
                    pe.wait_ge(oT_ready, 4 * b + quad + 1)
                    for qt in range(NQ):
                        mm = nc.tensor.transpose(obank[quad % 2][:, qt * P:(qt + 1) * P], oT[:, qt * P:(qt + 1) * P], c.ident[:, :])
                    mm.then_inc(o_turned, 1)

                def step(b, h, last):
                    for kt in range(NQ):
                        pe.wait_ge(exp_done, NQ * (H * b + h) + kt + 1)
                        if not (last and h == H - 1 and kt >= 2):
                            cols(*in_turn(b, h + (kt + 2) // NQ), (kt + 2) % NQ)
                        if not (last and h + LEAD >= H):
                            rows(*in_turn(b, h + LEAD), kt)
                        values(b, h, kt)
                        if h % 4 == 0 and h and kt == 1:
                            turn_quad(b, h // 4 - 1)
                        if h % 8 == 6 and kt == 3 and not (last and h == H - 2):
                            pe.wait_ge(split, 8 * b + 4 * (h // 8) + 8)
                            turn_maxima()
                    if h == H - 1:
                        turn_quad(b, H // 4 - 1)

                pe.sem_inc(max_ready, 2)
                pe.sem_inc(o_ready, 2)
                pe.sem_inc(max_turned, 1)
                for h in range(LEAD):
                    for qt in range(NQ):
                        rows(0, h, qt)
                pe.wait_ge(pick_ready, 2)
                pe.wait_ge(split, 4)
                turn_maxima()
                cols(0, 0, 0)
                cols(0, 0, 1)
                with pe.Fori(0, B - 1) as b:
                    for h in range(H):
                        step(b, h, False)
                for h in range(H):
                    step(B - 1, h, True)

            @block.scalar
            def _(a):
                def keep_maxima(b, g):
                    a.wait_ge(max_turned, 2 * b + g + 2)
                    nc.scalar.copy(mT[g][:, :], mbank[:, :]).then_inc(mT_ready, 1)

                def step(b, h, last):
                    for kt in range(NQ):
                        a.wait_ge(cols_done, NQ * (H * b + h) + kt + 1)
                        if kt == 0:
                            a.wait_ge(pv_done, H * b + h + 1)
                        lo = first_query(kt)
                        nc.scalar.activation(probs[h % 2][:, kt, lo:S], cbank[kt % 2][:, lo:S], ACT.Exp).then_inc(exp_done, 1)
                        if h % 8 == 7 and kt == 0 and not (last and h == H - 1):
                            keep_maxima(*((b, 1) if h < 8 else (b + 1, 0)))

                a.sem_inc(pv_done, 2)
                keep_maxima(0, 0)
                with a.Fori(0, B - 1) as b:
                    for h in range(H):
                        step(b, h, False)
                for h in range(H):
                    step(B - 1, h, True)

            @block.gpsimd
            def _(g):
                g.memset(mparts[:, :, :], 0.0).then_inc(zeroed, 1)
                for i in range(4):
                    g.memset(vq[i][:, :, :, :], 1.0).then_inc(zeroed, 1)
                g.wait_ge(zeroed, 5)

                def part(i):
                    return mparts[:, :, 8 * i:8 * i + 8].rearrange("p q j -> p j q")

                def split_maxima(n):
                    g.wait_ge(max_ready, n * (8 * NQ) + (8 * NQ + 2))
                    g.wait_ge(max_turned, n + 1)
                    hold(g, spare)
                    g.tensor_copy(part(0), nmax[:, :, :]).then_inc(split, 1)
                    g.wait_ge(split, n * 4 + 1)
                    g.tensor_tensor(rest[:, :, :], nmax[:, :, :], part(0), ALU.subtract).then_inc(split, 1)
                    g.wait_ge(split, n * 4 + 2)
                    hold(g, spare)
                    g.tensor_copy(part(1), rest[:, :, :]).then_inc(split, 1)
                    g.wait_ge(split, n * 4 + 3)
                    g.tensor_tensor(part(2), rest[:, :, :], part(1), ALU.subtract).then_inc(split, 1)

                def hold_values(b, quad):
                    g.wait_ge(pv_done, H * b + (1 if quad < 2 else 4))
                    hold(g, spare)
                    g.tensor_copy(vq[quad][:, :, :, 0:HD], vals[:, bass.ds(H * b + 4 * quad, 4), :, :]).then_inc(held, 1)

                with g.Fori(0, B) as b:
                    for half in range(2):
                        split_maxima(2 * b + half)
                        hold_values(b, 2 * half)
                        hold_values(b, 2 * half + 1)

            @block.vector
            def _(v):
                def maxima(b, h, qt, first=False):
                    if h % 8 == 0 and qt == 0 and not first:
                        v.wait_ge(split, 8 * b + 4 * (h // 8) - 2)
                    v.wait_ge(rows_done, NQ * (H * b + h) + qt + 1)
                    nc.vector.tensor_reduce(nmax[:, h % 8, qt:qt + 1], rbank[qt % 2][:, 0:keys(qt)], AX.X, ALU.max,
                                            negate=True).then_inc(max_ready, 1)

                def keep_quad(b, quad):
                    v.wait_ge(pv_done, H * b + 4 * quad + 6)
                    nc.vector.tensor_copy(oT[:, :], obank[quad % 2][:, :]).then_inc(oT_ready, 1)

                def divide_quad(b, quad):
                    v.wait_ge(o_turned, 4 * b + quad + 1)
                    o = obank[quad % 2][:, :].rearrange("p (q u w) -> p q u w", q=NQ, w=VW)
                    nc.vector.reciprocal(rinv[:, :, :], o[:, :, :, HD]).then_inc(rinv_ready, 1)
                    v.wait_ge(rinv_ready, 4 * b + quad + 1)
                    dst = out[:, bass.ds(NQ * b, NQ), 4 * HD * quad:4 * HD * (quad + 1)].rearrange("p q (u w) -> p q u w", w=HD)
                    nc.vector.tensor_tensor(dst,
                                            o[:, :, :, 0:HD], rinv[:, :, :].unsqueeze(3).to_broadcast([P, NQ, 4, HD]),
                                            ALU.mult).then_inc(o_ready, 1)

                def step(b, h, last):
                    quad = h // 4 - 1 if h % 4 == 0 else -1
                    if quad >= 0:
                        keep_quad(b, quad)
                    for qt in range(NQ):
                        if not (last and h + LEAD >= H):
                            maxima(*in_turn(b, h + LEAD), qt)
                        if quad >= 0 and qt == 2:
                            divide_quad(b, quad)
                    if h == H - 1:
                        keep_quad(b, H // 4 - 1)
                        divide_quad(b, H // 4 - 1)

                nc.vector.tensor_reduce(pick_f[:, :], c.ident[:, 0:24].rearrange("p (t j) -> p j t", t=3), AX.X,
                                        ALU.add).then_inc(pick_ready, 1)
                v.wait_ge(pick_ready, 1)
                nc.vector.tensor_copy(pick[:, :, :], pick_f[:, :].unsqueeze(2).to_broadcast([P, 8, P])).then_inc(pick_ready, 1)
                for h in range(LEAD):
                    for qt in range(NQ):
                        maxima(0, h, qt, h == 0)
                with v.Fori(0, B - 1) as b:
                    for h in range(H):
                        step(b, h, False)
                for h in range(H):
                    step(B - 1, h, True)


def narrow_output(c, name, attended, w_out, bias, factor):
    nc = c.nc
    with ExitStack() as ctx:
        def sb(n, shape):
            return ctx.enter_context(nc.sbuf_tensor(f"{name}_{n}", shape, F32))

        def sem(n):
            return c.sem(f"{name}_{n}")

        norm = Norm(c, ctx, name)
        w, bias_row = sb("w", [P, KT, D]), sb("bias", [P, D])
        o, oT = sb("o", [P, NQ, D]), sb("oT", [P, KT, S])
        y, t = sb("y", [P, NQ, D]), sb("t", [P, NQ, D])
        w_in, o_ready, tr_done, oT_ready, y_done, y_ready, t_ready, x_ready, spare = (
            sem(n) for n in ("w_in", "o_ready", "tr_done", "oT_ready", "y_done", "y_ready", "t_ready", "x_ready", "spare"))
        tr, py = c.bank[0:2], c.bank[2:4]
        n_w = 1 + (bias is not None)
        block = nc.Block()
        with block:
            @block.sync
            def _(sp):
                sp.dma_start(w[:, :, :], weights(w_out)).then_inc(w_in, 16)
                if bias is not None:
                    sp.dma_start(bias_row[:, :], bias.partition_broadcast(P)).then_inc(w_in, 16)

            @block.gpsimd
            def _(g):
                def keep_o(b):
                    g.wait_ge(tr_done, b * KT + KT)
                    hold(g, spare)
                    g.tensor_copy(o[:, :, :], attended[:, bass.ds(b * NQ, NQ), :]).then_inc(o_ready, 1)

                keep_o(0)
                with g.Fori(0, B - 1) as b:
                    keep_o(b + 1)
                    norm.root(g, b)
                norm.root(g, B - 1)

            @block.tensor
            def _(pe):
                def turn(b):
                    pe.wait_ge(o_ready, b + 1)
                    for k in range(KT):
                        for q in range(NQ):
                            mm = nc.tensor.transpose(tr[k][:, q * P:(q + 1) * P], o[:, q, k * P:(k + 1) * P], c.ident[:, :])
                        mm.then_inc(tr_done, 1)

                def group(b, last):
                    pe.wait_ge(oT_ready, b * KT + KT)
                    pe.wait_ge(y_ready, b * 2 + 2)
                    for q in range(NQ):
                        for k in range(KT):
                            mm = nc.tensor.matmul(py[q // 2][:, (q % 2) * D:(q % 2 + 1) * D], oT[:, k, q * P:(q + 1) * P],
                                                  w[:, k, :], start=(k == 0), stop=(k == KT - 1))
                        if q % 2:
                            mm.then_inc(y_done, 1)
                    if not last:
                        turn(b + 1)

                pe.sem_inc(tr_done, KT)
                pe.sem_inc(y_done, 2)
                pe.sem_inc(y_ready, 2)
                pe.wait_ge(w_in, 16 * n_w)
                turn(0)
                with pe.Fori(0, B - 1) as b:
                    group(b, False)
                group(B - 1, True)

            @block.scalar
            def _(a):
                with a.Fori(0, B) as b:
                    for k in range(KT):
                        a.wait_ge(tr_done, b * KT + k + 3)
                        if k == 0:
                            a.wait_ge(y_done, b * 2 + 2)
                        nc.scalar.activation(oT[:, k, :], tr[k][:, :], ACT.Copy, scale=factor).then_inc(oT_ready, 1)

            @block.vector
            def _(v):
                if bias is not None:
                    v.wait_ge(w_in, 16 * n_w)
                with v.Fori(0, B) as b:
                    for i in range(2):
                        v.wait_ge(y_done, b * 2 + i + 3)
                        src = py[i][:, :].rearrange("p (q d) -> p q d", d=D)
                        dst = y[:, 2 * i:2 * i + 2, :]
                        if bias is not None:
                            row = bias_row[:, :].unsqueeze(1).to_broadcast([P, 2, D])
                            mm = nc.vector.tensor_tensor(dst, src, row, ALU.add)
                        else:
                            mm = nc.vector.tensor_copy(dst, src)
                        mm.then_inc(y_ready, 1)
                    v.wait_ge(y_ready, b * 2 + 4)
                    norm.statistics(v, b, lambda q: y[:, q, :])
                    norm.wait(v, b)
                    add_normed(c, v, norm, b, lambda q: y[:, q, :], t, t_ready, x_ready)


def add_normed(c, v, norm, b, tile, t, t_ready, x_ready):
    for q in range(NQ):
        norm.apply(q, t[:, q, :], tile(q)).then_inc(t_ready, 1)
    for q in range(NQ):
        v.wait_ge(t_ready, b * NQ + q + 1)
        c.nc.vector.tensor_tensor(tile_of(c.x, b, q), tile_of(c.x, b, q), t[:, q, :], ALU.add).then_inc(x_ready, 1)


def router_input(c, name, src, rms, col_scale, w_router, bias, n_experts, hT_all, h_all, logits,
                 h_slots=None):
    nc = c.nc
    with ExitStack() as ctx:
        def sb(n, shape):
            return ctx.enter_context(nc.sbuf_tensor(f"{name}_{n}", shape, F32))

        def sem(n):
            return c.sem(f"{name}_{n}")

        norm = Norm(c, ctx, name)
        w = sb("w", [P, KT, n_experts])
        row = sb("row", [P, n_experts])
        col = sb("col", [P, KT])
        h, hT = sb("h", [P, NQ, D]), sb("hT", [P, KT, S])
        w_in, h_ready, tr_done, hT_ready, kept, lg_done, lg_ready, spare = (
            sem(n) for n in ("w_in", "h_ready", "tr_done", "hT_ready", "kept", "lg_done", "lg_ready", "spare"))
        zero = sb("zero", [P, 8, D])
        zero_ready, zeroed = sem("zero_ready"), sem("zeroed")
        kept_per = KT if h_all is None else 1
        tr, pl = c.bank[0:2], c.bank[2]
        n_w = 1 + (bias is not None) + (col_scale is not None)
        block = nc.Block()
        with block:
            @block.sync
            def _(sp):
                sp.dma_start(w[:, :, :], weights(w_router)).then_inc(w_in, 16)
                if bias is not None:
                    sp.dma_start(row[:, :], bias.partition_broadcast(P)).then_inc(w_in, 16)
                if col_scale is not None:
                    sp.dma_start(col[:, :], col_scale).then_inc(w_in, 16)
                if h_slots is not None:
                    sp.wait_ge(zero_ready, 1)
                    tiles = BLOCKS * SLOTS // P
                    for i in range(0, tiles, 8):
                        n = min(8, tiles - i)
                        sp.dma_start(h_slots[i * P:(i + n) * P, :].rearrange("(i p) d -> p i d", p=P), zero[:, 0:n, :]).then_inc(zeroed, 16)
                    sp.wait_ge(zeroed, 16 * -(-tiles // 8))

            @block.vector
            def _(v):
                if h_slots is not None:
                    nc.vector.memset(zero[:, :, :], 0.0).then_inc(zero_ready, 1)

                def keep_h(b):
                    norm.statistics(v, b, lambda q: tile_of(src, b, q), rms)
                    norm.wait(v, b)
                    v.wait_ge(tr_done, b * KT + KT)
                    if h_all is not None:
                        v.wait_ge(kept, b + 1)
                    for q in range(NQ):
                        norm.apply(q, h[:, q, :], tile_of(src, b, q), rms).then_inc(h_ready, 1)

                def keep_logits(b):
                    v.wait_ge(lg_done, b + 1)
                    dst = logits[:, bass.ds(b * NQ, NQ), :]
                    lg = pl[:, 0:NQ * n_experts].rearrange("p (q e) -> p q e", e=n_experts)
                    if bias is not None:
                        nc.vector.tensor_tensor(dst, lg, row[:, :].unsqueeze(1).to_broadcast([P, NQ, n_experts]),
                                                ALU.add).then_inc(lg_ready, 1)
                    else:
                        nc.vector.tensor_copy(dst, lg).then_inc(lg_ready, 1)

                keep_h(0)
                v.wait_ge(w_in, 16 * n_w)
                with v.Fori(0, B - 1) as b:
                    keep_h(b + 1)
                    keep_logits(b)
                keep_logits(B - 1)

            @block.gpsimd
            def _(g):
                g.sem_inc(kept, kept_per)

                def keep(b):
                    if h_all is not None:
                        g.wait_ge(h_ready, b * NQ + NQ)
                        hold(g, spare)
                        g.tensor_copy(h_all[:, bass.ds(b * NQ, NQ), :], h[:, :, :]).then_inc(kept, 1)
                    for k in range(KT if h_all is None else 0):
                        g.wait_ge(hT_ready, b * KT + k + 1)
                        hold(g, spare)
                        g.tensor_copy(hT_all[:, k, bass.ds(b * S, S)], hT[:, k, :]).then_inc(kept, 1)

                norm.root(g, 0, rms)
                with g.Fori(0, B - 1) as b:
                    norm.root(g, b + 1, rms)
                    keep(b)
                keep(B - 1)

            @block.scalar
            def _(a):
                if col_scale is not None:
                    a.wait_ge(w_in, 16 * n_w)
                with a.Fori(0, B) as b:
                    for k in range(KT):
                        a.wait_ge(tr_done, b * KT + k + 3)
                        if h_all is None:
                            a.wait_ge(kept, b * KT + k + 1)
                        if col_scale is None:
                            nc.scalar.copy(hT[:, k, :], tr[k][:, :]).then_inc(hT_ready, 1)
                        else:
                            nc.scalar.activation(hT[:, k, :], tr[k][:, :], ACT.Copy, scale=col[:, k:k + 1]).then_inc(hT_ready, 1)

            @block.tensor
            def _(pe):
                pe.sem_inc(tr_done, KT)
                pe.sem_inc(lg_ready, 1)

                def turn(b):
                    for k in range(KT):
                        for q in range(NQ):
                            if k == 0:
                                pe.wait_ge(h_ready, b * NQ + q + 1)
                            mm = nc.tensor.transpose(tr[k][:, q * P:(q + 1) * P], h[:, q, k * P:(k + 1) * P], c.ident[:, :])
                        mm.then_inc(tr_done, 1)

                def router(b):
                    pe.wait_ge(hT_ready, b * KT + KT)
                    pe.wait_ge(lg_ready, b + 1)
                    for q in range(NQ):
                        for k in range(KT):
                            mm = nc.tensor.matmul(pl[:, q * n_experts:(q + 1) * n_experts], hT[:, k, q * P:(q + 1) * P],
                                                  w[:, k, :], start=(k == 0), stop=(k == KT - 1))
                    mm.then_inc(lg_done, 1)

                turn(0)
                pe.wait_ge(w_in, 16 * n_w)
                with pe.Fori(0, B - 1) as b:
                    router(b)
                    turn(b + 1)
                router(B - 1)


class Chain:

    def __init__(self, v, sem):
        self.v, self.sem, self.n = v, sem, 0

    def link(self, ins):
        self.n += 1
        ins.then_inc(self.sem, 1)
        self.v.wait_ge(self.sem, self.n)


def sigmoid_gates(c, name, logits, iota, gates):
    nc = c.nc
    KG, EG = 4, E0 // G0
    with ExitStack() as ctx:
        def sb(n, shape, dt=F32):
            return ctx.enter_context(nc.sbuf_tensor(f"{name}_{n}", shape, dt))

        ex, s = sb("ex", [P, NT, E0]), sb("s", [P, NT, E0])
        pairs = sb("pairs", [P, 6, NT * G0])
        gw = sb("gw", [P, NT, G0])
        top, idx, idxf = sb("top", [P, NT, 8]), sb("idx", [P, NT, 8], U32), sb("idxf", [P, NT, 8])
        eq = sb("eq", [P, NT, E0, K0])
        gmask, masked, sel = sb("gmask", [P, NT, G0]), sb("masked", [P, NT, E0]), sb("sel", [P, NT, E0])
        den = sb("den", [P, 2, NT])
        ex_ready, step = c.sem(f"{name}_ex"), c.sem(f"{name}_step")
        block = nc.Block()
        with block:
            @block.scalar
            def _(a):
                nc.scalar.activation(ex[:, :, :], logits[:, :, :], ACT.Exp, scale=-1.0).then_inc(ex_ready, 1)

            @block.vector
            def _(v):
                nv = nc.vector
                link = Chain(v, step).link

                def top8(scores):
                    for t in range(NT):
                        ins = nv.max(top[:, t, :], scores[:, t, :])
                    link(ins)
                    for t in range(NT):
                        ins = nv.max_index(idx[:, t, :], top[:, t, :], scores[:, t, :])
                    link(ins)
                    link(nv.tensor_copy(idxf[:, :, :], idx[:, :, :]))

                def among(out, n, k):
                    e = eq[:, :, 0:n, 0:k]
                    link(nv.tensor_tensor(e, idxf[:, :, 0:k].unsqueeze(2).to_broadcast([P, NT, n, k]),
                                          iota[:, 0:n].unsqueeze(1).unsqueeze(3).to_broadcast([P, NT, n, k]), ALU.is_equal))
                    link(nv.tensor_reduce(out, e, AX.X, ALU.add))

                v.wait_ge(ex_ready, 1)
                link(nv.tensor_scalar(s[:, :, :], ex[:, :, :], 1.0, None, ALU.add))
                link(nv.reciprocal(s[:, :, :], s[:, :, :]))
                sg = s[:, :, :].rearrange("p t (g e) -> p (t g) e", e=EG)
                for i, (x, y, op) in enumerate(((0, 1, ALU.max), (0, 1, ALU.min), (2, 3, ALU.max), (2, 3, ALU.min))):
                    link(nv.tensor_tensor(pairs[:, i, :], sg[:, :, x], sg[:, :, y], op))
                link(nv.tensor_tensor(pairs[:, 4, :], pairs[:, 0, :], pairs[:, 2, :], ALU.min))
                link(nv.tensor_tensor(pairs[:, 5, :], pairs[:, 1, :], pairs[:, 3, :], ALU.max))
                link(nv.tensor_tensor(pairs[:, 4, :], pairs[:, 4, :], pairs[:, 5, :], ALU.max))
                link(nv.tensor_tensor(pairs[:, 5, :], pairs[:, 0, :], pairs[:, 2, :], ALU.max))
                link(nv.tensor_tensor(gw[:, :, :].rearrange("p t g -> p (t g)"), pairs[:, 4, :], pairs[:, 5, :], ALU.add))
                top8(gw)
                among(gmask[:, :, :], G0, KG)
                link(nv.tensor_tensor(masked[:, :, :].rearrange("p t (g e) -> p (t g) e", e=EG), sg,
                                      gmask[:, :, :].rearrange("p t g -> p (t g)").unsqueeze(2).to_broadcast([P, NT * G0, EG]),
                                      ALU.mult))
                top8(masked)
                among(sel[:, :, :], E0, K0)
                link(nv.tensor_tensor(sel[:, :, :], sel[:, :, :], s[:, :, :], ALU.mult))
                link(nv.tensor_reduce(den[:, 0, :], sel[:, :, :], AX.X, ALU.add))
                link(nv.tensor_scalar(den[:, 1, :], den[:, 0, :], 1e-20, None, ALU.add))
                link(nv.reciprocal(den[:, 0, :], den[:, 1, :]))
                link(nv.tensor_tensor(gates[:, :, :], sel[:, :, :], den[:, 0, :].unsqueeze(2).to_broadcast([P, NT, E0]), ALU.mult))
                link(nv.tensor_scalar(gates[:, :, :], gates[:, :, :], SCALE0, None, ALU.mult))


def relu2_experts(c, name, hT, gates, w, acc):
    nc = c.nc
    WC = KT * M0
    PAIRS = E0 // 2
    PRODUCTS = [(0, 0), (0, 1), (1, 0)]
    with ExitStack() as ctx:
        def sb(n, shape, dt=F32):
            return ctx.enter_context(nc.sbuf_tensor(f"{name}_{n}", shape, dt))

        def sem(n):
            return c.sem(f"{name}_{n}")

        ws = [sb(f"w{s}", [P, 2, WC + D]) for s in range(2)]
        wp = [[sb(f"w{s}_{part}", [P, 2, WC + D], F32R) for part in ("high", "low")] for s in range(2)]
        hp = [sb(f"h_{part}", [P, KT, T], F32R) for part in ("high", "low")]
        relu, act = sb("relu", [P, 4, S]), sb("act", [P, 4, S])
        ap = [sb(f"act_{part}", [P, 4, S], F32R) for part in ("high", "low")]
        loaded = [sem("loaded0"), sem("loaded1")]
        h_high, h_low, w_high, w_low, up_done, relu_ready, act_ready, act_high, act_low, y_done, acc_done, zeroed = (
            sem(n) for n in ("h_high", "h_low", "w_high", "w_low", "up", "relu", "act", "act_high", "act_low", "y", "acc", "zeroed"))
        ph, py = c.bank[0:4], c.bank[4:8]

        def ahead(p, u):
            return p + (u + 2) // 8, (u + 2) % 8

        block = nc.Block()
        with block:
            @block.sync
            def _(sp):
                def load(pair, s):
                    sp.dma_start(ws[s][:, :, :], w[bass.ds(pair, 1), :, :, :].rearrange("a p i n -> p (a i) n")).then_inc(loaded[s], 16)

                load(0, 0)
                load(1, 1)
                with sp.Fori(1, PAIRS // 2) as m:
                    for s in range(2):
                        sp.wait_ge(w_low, 2 * m + (s - 1))
                        load(2 * m + s, s)
                sp.wait_ge(w_low, PAIRS - 1)
                load(PAIRS, 0)

            @block.tensor
            def _(pe):
                def up(p, u, s):
                    g, i = u // 2, u % 2
                    if u == 0:
                        pe.wait_ge(w_low, p + 1)
                    n = 0
                    for k in range(KT):
                        for x, y in PRODUCTS:
                            mm = nc.tensor.matmul(ph[u % 4][:, :], wp[s][x][:, i, k * M0:(k + 1) * M0], hp[y][:, k, g * S:(g + 1) * S],
                                                  start=(n == 0), stop=(n == 3 * KT - 1))
                            n += 1
                    mm.then_inc(up_done, 1)

                def down(p, u, s):
                    i = u % 2
                    pe.wait_ge(act_low, 8 * p + u + 1)
                    pe.wait_ge(acc_done, NQ * (8 * p + u + 1))
                    for q in range(NQ):
                        for n, (x, y) in enumerate(PRODUCTS):
                            mm = nc.tensor.matmul(py[2 * i + q // 2][:, (q % 2) * D:(q % 2 + 1) * D],
                                                  ap[x][:, u % 4, q * P:(q + 1) * P], wp[s][y][:, i, WC:], start=(n == 0), stop=(n == 2))
                    mm.then_inc(y_done, 1)

                pe.wait_ge(h_low, 2 * B)
                up(0, 0, 0)
                up(0, 1, 0)
                with pe.Fori(0, PAIRS // 2) as m:
                    for s in range(2):
                        for u in range(8):
                            q, v = ahead(2 * m + s, u)
                            up(q, v, s if u < 6 else 1 - s)
                            down(2 * m + s, u, s)
                for u in range(8):
                    if u < 6:
                        up(PAIRS, u + 2, 0)
                    down(PAIRS, u, 0)

            @block.scalar
            def _(a):
                def split_weights(p, s, count, first=False):
                    a.wait_ge(loaded[s], 16 * count)
                    if not first:
                        a.wait_ge(y_done, 8 * p - 7)
                    nc.scalar.copy(wp[s][0][:, :, :], ws[s][:, :, :]).then_inc(w_high, 1)

                def unit(p, u):
                    a.wait_ge(up_done, 8 * p + u + 1)
                    nc.scalar.activation(relu[:, u % 4, :], ph[u % 4][:, :], ACT.Relu).then_inc(relu_ready, 1)
                    a.wait_ge(act_ready, 8 * p + u + 1)
                    nc.scalar.copy(ap[0][:, u % 4, :], act[:, u % 4, :]).then_inc(act_high, 1)

                split_weights(0, 0, 1, True)
                for g in range(B):
                    for k in range(KT):
                        nc.scalar.copy(hp[0][:, k, g * S:(g + 1) * S], hT[:, k, g * S:(g + 1) * S]).then_inc(h_high, 1)
                with a.Fori(0, PAIRS // 2) as m:
                    for s in range(2):
                        for u in range(8):
                            unit(2 * m + s, u)
                            if u == 4:
                                split_weights(2 * m + s + 1, 1 - s, m + 1 + s)
                for u in range(8):
                    unit(PAIRS, u)

            @block.gpsimd
            def _(g):
                def low_weights(p, s):
                    g.wait_ge(w_high, p + 1)
                    g.tensor_tensor(wp[s][1][:, :, :], ws[s][:, :, :], wp[s][0][:, :, :], ALU.subtract).then_inc(w_low, 1)

                def unit(p, u):
                    g.wait_ge(act_high, 8 * p + u + 1)
                    g.tensor_tensor(ap[1][:, u % 4, :], act[:, u % 4, :], ap[0][:, u % 4, :], ALU.subtract).then_inc(act_low, 1)

                low_weights(0, 0)
                with g.Fori(0, PAIRS // 2) as m:
                    for s in range(2):
                        for u in range(8):
                            unit(2 * m + s, u)
                            if u == 4:
                                low_weights(2 * m + s + 1, 1 - s)
                for u in range(8):
                    unit(PAIRS, u)

            @block.vector
            def _(v):
                def square(p, u):
                    v.wait_ge(relu_ready, 8 * p + u + 1)
                    nc.vector.scalar_tensor_tensor(out=act[:, u % 4, :], in0=ph[u % 4][:, :], scalar=0.0, in1=relu[:, u % 4, :],
                                                   op0=ALU.max, op1=ALU.mult).then_inc(act_ready, 1)

                def add(p, u, shared):
                    g, i = u // 2, u % 2
                    v.wait_ge(y_done, 8 * p + u + 1)
                    for q in range(NQ):
                        tile = acc[:, NQ * g + q, :]
                        y = py[2 * i + q // 2][:, (q % 2) * D:(q % 2 + 1) * D]
                        v.wait_ge(acc_done, NQ * (8 * p + u) + (NQ + q + 1))
                        if shared:
                            nc.vector.tensor_tensor(tile, y, tile, ALU.add).then_inc(acc_done, 1)
                        else:
                            gate = gates[:, NQ * g + q, bass.ds(2 * p + i, 1)]
                            nc.vector.scalar_tensor_tensor(out=tile, in0=y, scalar=gate, in1=tile,
                                                           op0=ALU.mult, op1=ALU.add).then_inc(acc_done, 1)

                v.sem_inc(acc_done, 2 * NQ)
                for g in range(B):
                    for k in range(KT):
                        v.wait_ge(h_high, 2 * g + k + 1)
                        nc.vector.tensor_tensor(hp[1][:, k, g * S:(g + 1) * S], hT[:, k, g * S:(g + 1) * S],
                                                hp[0][:, k, g * S:(g + 1) * S], ALU.subtract).then_inc(h_low, 1)
                nc.vector.memset(acc[:, :, :], 0.0).then_inc(zeroed, 1)
                v.wait_ge(zeroed, 1)
                square(0, 0)
                square(0, 1)
                with v.Fori(0, PAIRS // 2) as m:
                    for s in range(2):
                        for u in range(8):
                            square(*ahead(2 * m + s, u))
                            add(2 * m + s, u, False)
                for u in range(8):
                    if u < 6:
                        square(PAIRS, u + 2)
                    add(PAIRS, u, True)


def add_normed_sum(c, name, acc, plus=None):
    nc = c.nc
    with ExitStack() as ctx:
        norm = Norm(c, ctx, name)
        y = ctx.enter_context(nc.sbuf_tensor(f"{name}_y", [P, NQ, D], F32))
        t = ctx.enter_context(nc.sbuf_tensor(f"{name}_t", [P, NQ, D], F32))
        y_ready, t_ready, x_ready = (c.sem(f"{name}_{n}") for n in ("y_ready", "t_ready", "x_ready"))
        block = nc.Block()
        with block:
            @block.vector
            def _(v):
                with v.Fori(0, B) as b:
                    if plus is not None:
                        nc.vector.tensor_tensor(y[:, :, :], acc[:, bass.ds(b * NQ, NQ), :], plus[:, bass.ds(b * NQ, NQ), :],
                                                ALU.add).then_inc(y_ready, 1)
                        v.wait_ge(y_ready, b + 1)

                    def tile(q):
                        return tile_of(acc, b, q) if plus is None else y[:, q, :]

                    norm.statistics(v, b, tile)
                    norm.wait(v, b)
                    add_normed(c, v, norm, b, tile, t, t_ready, x_ready)

            @block.gpsimd
            def _(g):
                with g.Fori(0, B) as b:
                    norm.root(g, b)


def grouped_projection(c, name, a, z, vals, q_dram, k_dram):
    nc = c.nc
    NC = H + KVH
    HALF = P // 2
    with ExitStack() as ctx:
        def sb(n, shape, dt=F32):
            return ctx.enter_context(nc.sbuf_tensor(f"{name}_{n}", shape, dt))

        def sem(n):
            return c.sem(f"{name}_{n}")

        PRODUCTS = [(0, 0), (0, 1), (1, 0)]
        norm_x, norm_z = Norm(c, ctx, name + "_x"), Norm(c, ctx, name + "_z")
        wqk = [sb(f"wqk_{part}", [P, KT, NC * P], F32R) for part in ("high", "low")]
        wv = [sb(f"wv_{part}", [P, KT, KVH * GD], F32R) for part in ("high", "low")]
        col, rope = sb("col", [P, KT]), sb("rope", [P, 2, 2, S])
        h = sb("h", [P, NQ, D])
        hT = [sb(f"hT_{part}", [P, KT, S], F32R) for part in ("high", "low")]
        xw = sb("xw", [P, 4, S])
        xc, xs = sb("xc", [P, 2, S]), sb("xs", [P, 2, S])
        rot = sb("rot", [P, NC, S])
        raw_qk = rot[:, 0:10, :].rearrange("p c s -> p (c s)").rearrange("p (k n) -> p k n", k=KT)
        raw_v = rot[:, 10:12, :]
        CW = NC * P // 2
        halves = [slice(i * CW, (i + 1) * CW) for i in range(2)]
        w_high, w_low, hT_high = sem("w_high"), sem("w_low"), sem("hT_high")
        qk_in, rope_in = [sem("qk_in0"), sem("qk_in1")], sem("rope_in")
        w_in, z_ready, h_ready, tr_done, hT_ready, v_done, v_kept, qk_done, swapped, terms, rot_ready, spare = (
            sem(n) for n in ("w_in", "z_ready", "h_ready", "tr_done", "hT_ready", "v_done", "v_kept", "qk_done",
                             "swapped", "terms", "rot_ready", "carry"))
        stored = [sem(f"stored{quad}") for quad in range(5)]
        tr, ps, pv = c.bank[0:2], c.bank[2:6], c.bank[6:8]
        block = nc.Block()
        with block:
            @block.sync
            def _(sp):
                for quad in range(5):
                    sp.sem_inc(stored[quad], 16)
                for dst, src in ((raw_v, weights(a["d_wv"])), (col[:, :], a["d_ln"])):
                    sp.dma_start(dst, src).then_inc(w_in, 16)
                for i in range(2):
                    sp.dma_start(raw_qk[:, :, halves[i]], weights(a["d_wqk"])[:, :, halves[i]]).then_inc(qk_in[i], 16)
                sp.dma_start(rope[:, :, :, :], a["d_rope"]).then_inc(rope_in, 16)
                with sp.Fori(0, B) as b:
                    for quad in range(5):
                        sp.wait_ge(rot_ready, b * NC + (4 * quad + 4 + 2))
                        if quad < 4:
                            dst = q_dram[bass.ds(4 * b + quad, 1), :, :, :].rearrange("a p u s -> p (a u) s")
                        else:
                            dst = k_dram[bass.ds(4 * b, 4), :, :, :].rearrange("g p u s -> p (g u) s")
                        sp.dma_start(dst, rot[:, 4 * quad:4 * quad + 4, :]).then_inc(stored[quad], 16)
                for quad in range(5):
                    sp.wait_ge(stored[quad], 16 * B + 16)

            @block.vector
            def _(v):
                def keep_z(b):
                    norm_x.wait(v, b)
                    for q in range(NQ):
                        norm_x.apply(q, tile_of(z, b, q), tile_of(c.x, b, q)).then_inc(z_ready, 1)
                    v.wait_ge(z_ready, b * NQ + NQ)
                    norm_z.statistics(v, b, lambda q: tile_of(z, b, q), rms=True)

                def keep_h(b):
                    norm_z.wait(v, b)
                    v.wait_ge(tr_done, b * KT + KT)
                    for q in range(NQ):
                        norm_z.apply(q, h[:, q, :], tile_of(z, b, q), rms=True).then_inc(h_ready, 1)

                def group(b, last):
                    if not last:
                        norm_x.statistics(v, b + 1, lambda q: tile_of(c.x, b + 1, q))
                    for cc in range(NC):
                        v.wait_ge(swapped, b * NC + (cc + 1))
                        v.wait_ge(rot_ready, b * NC + (cc + 1))
                        nc.vector.tensor_tensor(xc[:, cc % 2, :], ps[cc % 4][:, :], rope[:, cc // H, 0, :], ALU.mult).then_inc(terms, 1)
                        nc.vector.tensor_tensor(xs[:, cc % 2, :], xw[:, cc % 4, :], rope[:, cc // H, 1, :], ALU.mult).then_inc(terms, 1)
                        if cc == 5 and not last:
                            keep_z(b + 1)
                        if cc == 12 and not last:
                            keep_h(b + 1)
                    if not last:
                        low_hT(b + 1)

                def low_hT(b):
                    for k in range(KT):
                        v.wait_ge(hT_high, b * KT + (k + 1))
                        nc.vector.scalar_tensor_tensor(out=hT[1][:, k, :], in0=tr[k][:, :], scalar=col[:, k:k + 1], in1=hT[0][:, k, :],
                                                       op0=ALU.mult, op1=ALU.subtract).then_inc(hT_ready, 1)

                norm_x.statistics(v, 0, lambda q: tile_of(c.x, 0, q))
                keep_z(0)
                keep_h(0)
                v.wait_ge(w_high, 1)
                nc.vector.tensor_tensor(wv[1][:, :, :], raw_v, wv[0][:, :, :], ALU.subtract).then_inc(w_low, 1)
                low_hT(0)
                for i, half in enumerate(halves):
                    v.wait_ge(w_high, i + 2)
                    nc.vector.tensor_tensor(wqk[1][:, :, half], raw_qk[:, :, half], wqk[0][:, :, half], ALU.subtract).then_inc(w_low, 1)
                v.wait_ge(rope_in, 16)
                with v.Fori(0, B - 1) as b:
                    group(b, False)
                group(B - 1, True)

            @block.gpsimd
            def _(g):
                def group(b, last):
                    for cc in range(NC):
                        g.wait_ge(terms, 2 * NC * b + (2 * cc + 10))
                        if cc % 4 == 0:
                            g.wait_ge(stored[cc // 4], 16 * b + 16)
                        g.tensor_tensor(rot[:, cc, :], xc[:, cc % 2, :], xs[:, cc % 2, :], ALU.add).then_inc(rot_ready, 1)
                        if cc == 1 and not last:
                            norm_x.root(g, b + 1)
                        if cc == 6 and not last:
                            norm_z.root(g, b + 1, rms=True)

                norm_x.root(g, 0)
                norm_z.root(g, 0, rms=True)
                g.sem_inc(rot_ready, 2)
                g.wait_ge(w_low, 3)
                with g.Fori(0, B - 1) as b:
                    group(b, False)
                group(B - 1, True)

            @block.scalar
            def _(s):
                def keep_hT(b):
                    for k in range(KT):
                        s.wait_ge(tr_done, b * KT + (k + 1 + KT))
                        nc.scalar.activation(hT[0][:, k, :], tr[k][:, :], ACT.Copy, scale=col[:, k:k + 1]).then_inc(hT_high, 1)

                def group(b, last):
                    for q in range(NQ):
                        s.wait_ge(v_done, b * NQ + (q + 1))
                        hold(s, spare)
                        nc.scalar.copy(vals[:, bass.ds(b * KVH, KVH), q, :],
                                       pv[q % 2][:, :].rearrange("p (g d) -> p g d", d=GD)).then_inc(v_kept, 1)
                    for cc in range(NC):
                        s.wait_ge(qk_done, b * NC + (cc + 1))
                        nc.scalar.copy(xw[0:HALF, cc % 4, :], ps[cc % 4][HALF:P, :])
                        nc.scalar.copy(xw[HALF:P, cc % 4, :], ps[cc % 4][0:HALF, :]).then_inc(swapped, 1)
                    if not last:
                        keep_hT(b + 1)

                s.wait_ge(w_in, 32)
                nc.scalar.copy(wv[0][:, :, :], raw_v).then_inc(w_high, 1)
                keep_hT(0)
                for i, half in enumerate(halves):
                    s.wait_ge(qk_in[i], 16)
                    nc.scalar.copy(wqk[0][:, :, half], raw_qk[:, :, half]).then_inc(w_high, 1)
                with s.Fori(0, B - 1) as b:
                    group(b, False)
                group(B - 1, True)

            @block.tensor
            def _(pe):
                def turn(b):
                    for k in range(KT):
                        for q in range(NQ):
                            if k == 0:
                                pe.wait_ge(h_ready, b * NQ + (q + 1))
                            mm = nc.tensor.transpose(tr[k][:, q * P:(q + 1) * P], h[:, q, k * P:(k + 1) * P], c.ident[:, :])
                        mm.then_inc(tr_done, 1)

                def group(b, last):
                    pe.wait_ge(hT_ready, b * KT + KT)
                    for q in range(NQ):
                        if q >= 2:
                            pe.wait_ge(v_kept, b * NQ + (q - 1))
                        for k in range(KT):
                            for i, (x, y) in enumerate(PRODUCTS):
                                mm = nc.tensor.matmul(pv[q % 2][:, :], hT[x][:, k, q * P:(q + 1) * P], wv[y][:, k, :],
                                                      start=(k == 0 and i == 0), stop=(k == KT - 1 and i == 2))
                        mm.then_inc(v_done, 1)
                    for cc in range(NC):
                        if cc in (0, NC // 2):
                            pe.wait_ge(w_low, 2 + 2 * cc // NC)
                        pe.wait_ge(terms, 2 * NC * b + (2 * cc + 2))
                        for k in range(KT):
                            for i, (x, y) in enumerate(PRODUCTS):
                                mm = nc.tensor.matmul(ps[cc % 4][:, :], wqk[x][:, k, cc * P:(cc + 1) * P], hT[y][:, k, :],
                                                      start=(k == 0 and i == 0), stop=(k == KT - 1 and i == 2))
                        mm.then_inc(qk_done, 1)
                    if not last:
                        turn(b + 1)

                pe.sem_inc(tr_done, KT)
                pe.sem_inc(terms, 8)
                turn(0)
                pe.wait_ge(w_low, 1)
                with pe.Fori(0, B - 1) as b:
                    group(b, False)
                group(B - 1, True)


def grouped_output(c, name, o_dram, w_out, z):
    nc = c.nc
    PRODUCTS = [(0, 0), (0, 1), (1, 0)]
    GROUPS = [(b, i) for b in range(B) for i in range(4)]
    with ExitStack() as ctx:
        def sb(n, shape, dt=F32):
            return ctx.enter_context(nc.sbuf_tensor(f"{name}_{n}", shape, dt))

        def sem(n):
            return c.sem(f"{name}_{n}")

        w = sb("w", [P, H, D])
        wp = [sb(f"w_{part}", [P, H, D], F32R) for part in ("high", "low")]
        oT = [sb(f"oT{i}", [P, 4, S]) for i in range(4)]
        op = [[sb(f"oT{i}_{part}", [P, 4, S], F32R) for part in ("high", "low")] for i in range(2)]
        w_in, loaded = ([sem(f"{n}{i}") for i in range(4)] for n in ("w_in", "loaded"))
        w_high, w_low, high_ready, low_ready, used, y_done, z_ready = (
            sem(n) for n in ("w_high", "w_low", "high", "low", "used", "y_done", "z_ready"))

        block = nc.Block()
        with block:
            @block.sync
            def _(sp):
                for b, i in GROUPS:
                    if b == 0:
                        sp.dma_start(w[:, 4 * i:4 * i + 4, :], w_out.rearrange("(h p) n -> p h n", p=P)[:, 4 * i:4 * i + 4, :]
                                     ).then_inc(w_in[i], 16)
                    else:
                        sp.wait_ge(low_ready, 4 * b + i - 3)
                    sp.dma_start(oT[i][:, :, :], o_dram[b * H + 4 * i:b * H + 4 * i + 4, :, :].rearrange("h p t -> p h t")
                                 ).then_inc(loaded[i], 16)

            @block.scalar
            def _(a):
                for b, i in GROUPS:
                    n = 4 * b + i
                    if b == 0:
                        a.wait_ge(w_in[i], 16)
                        nc.scalar.copy(wp[0][:, 4 * i:4 * i + 4, :], w[:, 4 * i:4 * i + 4, :]).then_inc(w_high, 1)
                    a.wait_ge(loaded[i], 16 * b + 16)
                    if n >= 2:
                        b2, i2 = GROUPS[n - 2]
                        if i2 == 3:
                            a.wait_ge(y_done, NQ * b2 + NQ)
                        else:
                            a.wait_ge(used, 3 * b2 + i2 + 1)
                    nc.scalar.copy(op[i % 2][0][:, :, :], oT[i][:, :, :]).then_inc(high_ready, 1)

            @block.vector
            def _(v):
                def add(b):
                    for q in range(NQ):
                        v.wait_ge(y_done, NQ * b + q + 1)
                        nc.vector.tensor_tensor(z[:, NQ * b + q, :], c.bank[4 * (b % 2) + q][:, 0:D], z[:, NQ * b + q, :],
                                                ALU.add).then_inc(z_ready, 1)

                for b, i in GROUPS:
                    if b == 0:
                        v.wait_ge(w_high, i + 1)
                        nc.vector.tensor_tensor(wp[1][:, 4 * i:4 * i + 4, :], w[:, 4 * i:4 * i + 4, :],
                                                wp[0][:, 4 * i:4 * i + 4, :], ALU.subtract).then_inc(w_low, 1)
                    v.wait_ge(high_ready, 4 * b + i + 1)
                    nc.vector.tensor_tensor(op[i % 2][1][:, :, :], oT[i][:, :, :], op[i % 2][0][:, :, :], ALU.subtract
                                            ).then_inc(low_ready, 1)
                    if b and i == 1:
                        add(b - 1)
                add(B - 1)

            @block.tensor
            def _(pe):
                pe.sem_inc(z_ready, 2 * NQ)
                with pe.Fori(0, B // 2) as m:
                    for s in range(2):
                        for i in range(4):
                            pe.wait_ge(w_low, i + 1)
                            pe.wait_ge(low_ready, 8 * m + (4 * s + i + 1))
                            for q in range(NQ):
                                if i == 0:
                                    pe.wait_ge(z_ready, NQ * (2 * m + s) + q + 1)
                                for h in range(4):
                                    for k, (x, y) in enumerate(PRODUCTS):
                                        mm = nc.tensor.matmul(c.bank[4 * s + q][:, 0:D], op[i % 2][x][:, h, q * P:(q + 1) * P],
                                                              wp[y][:, 4 * i + h, :], start=(i == 0 and h == 0 and k == 0),
                                                              stop=(i == 3 and h == 3 and k == 2))
                                if i == 3:
                                    mm.then_inc(y_done, 1)
                            if i != 3:
                                mm.then_inc(used, 1)


def two_highest(c, name, logits, iota, eq, pair):
    nc = c.nc
    K = 2
    with ExitStack() as ctx:
        def sb(n, shape, dt=F32):
            return ctx.enter_context(nc.sbuf_tensor(f"{name}_{n}", shape, dt))

        top, idx, idxf = sb("top", [P, NT, 8]), sb("idx", [P, NT, 8], U32), sb("idxf", [P, NT, 8])
        diff, ex, den = sb("diff", [P, NT]), sb("ex", [P, NT]), sb("den", [P, NT])
        diff_ready, ex_ready, step = (c.sem(f"{name}_{n}") for n in ("diff", "ex", "step"))
        block = nc.Block()
        with block:
            @block.scalar
            def _(a):
                a.wait_ge(diff_ready, 1)
                nc.scalar.activation(ex[:, :], diff[:, :], ACT.Exp).then_inc(ex_ready, 1)

            @block.vector
            def _(v):
                nv = nc.vector
                link = Chain(v, step).link
                for t in range(NT):
                    ins = nv.max(top[:, t, :], logits[:, t, :])
                link(ins)
                nv.tensor_tensor(diff[:, :], top[:, :, 1], top[:, :, 0], ALU.subtract).then_inc(diff_ready, 1)
                for t in range(NT):
                    ins = nv.max_index(idx[:, t, :], top[:, t, :], logits[:, t, :])
                link(ins)
                link(nv.tensor_copy(idxf[:, :, :], idx[:, :, :]))
                link(nv.tensor_tensor(eq[:, :, :, :], idxf[:, :, 0:K].unsqueeze(2).to_broadcast([P, NT, E1, K]),
                                      iota[:, 0:E1].unsqueeze(1).unsqueeze(3).to_broadcast([P, NT, E1, K]), ALU.is_equal))
                v.wait_ge(ex_ready, 1)
                link(nv.tensor_scalar(den[:, :], ex[:, :], 1.0, None, ALU.add))
                link(nv.reciprocal(pair[:, :, 0], den[:, :]))
                link(nv.tensor_tensor(pair[:, :, 1], pair[:, :, 0], ex[:, :], ALU.mult))




def routed_slots(c, name, eq, before, iota, pos, block_expert):
    nc = c.nc
    with ExitStack() as ctx:
        def sb(n, shape, dt=F32):
            return ctx.enter_context(nc.sbuf_tensor(f"{name}_{n}", shape, dt))

        ones, chosen = sb("ones", [P, P]), sb("chosen", [P, NT, E1])
        total = sb("total", [P, NT, E1])
        cum = [sb("cum0", [P, NT, E1]), sb("cum1", [P, NT, E1])]
        above, thr = sb("above", [P, E1, 8]), sb("thr", [P, 8])
        nb, off = sb("nb", [P, E1]), [sb("off0", [P, E1]), sb("off1", [P, E1])]
        base, prod, posf = sb("base", [P, NT, E1]), sb("prod", [P, NT, E1]), sb("posf", [P, 2, NT])
        cmp, eb = sb("cmp", [P, BLOCKS, E1]), sb("eb", [P, BLOCKS])
        step, counted, ones_ready, chosen_ready = (c.sem(f"{name}_{n}") for n in ("step", "counted", "ones", "chosen"))
        rank, tile_total = c.bank[0], c.bank[1]
        block = nc.Block()
        with block:
            @block.gpsimd
            def _(g):
                g.memset(ones[:, :], 1.0).then_inc(ones_ready, 1)

            @block.tensor
            def _(pe):
                pe.wait_ge(ones_ready, 1)
                pe.wait_ge(chosen_ready, 1)
                flat = chosen[:, :, :].rearrange("p t e -> p (t e)")
                nc.tensor.matmul(rank[:, 0:NT * E1], before[:, :], flat, start=True, stop=True)
                nc.tensor.matmul(tile_total[:, 0:NT * E1], ones[:, :], flat, start=True, stop=True).then_inc(counted, 1)

            @block.vector
            def _(v):
                nv = nc.vector
                link = Chain(v, step).link
                nv.tensor_reduce(chosen[:, :, :], eq[:, :, :, :], AX.X, ALU.add).then_inc(chosen_ready, 1)
                link(nv.tensor_scalar(thr[:, :], iota[:, 0:8], float(SLOTS), None, ALU.mult))
                v.wait_ge(counted, 1)
                link(nv.tensor_copy(total[:, :, :].rearrange("p t e -> p (t e)"), tile_total[:, 0:NT * E1]))
                src = total
                for i, d in enumerate((1, 2, 4, 8)):
                    dst = cum[i % 2]
                    link(nv.tensor_copy(dst[:, 0:d, :], src[:, 0:d, :]))
                    link(nv.tensor_tensor(dst[:, d:, :], src[:, d:, :], src[:, 0:NT - d, :], ALU.add))
                    src = dst
                count = src[:, NT - 1, :]
                link(nv.tensor_tensor(above[:, :, :], count.unsqueeze(2).to_broadcast([P, E1, 8]),
                                      thr[:, :].unsqueeze(1).to_broadcast([P, E1, 8]), ALU.is_gt))
                link(nv.tensor_reduce(nb[:, :], above[:, :, :], AX.X, ALU.add))
                blocks = nb
                for i, d in enumerate((1, 2, 4)):
                    dst = off[i % 2]
                    link(nv.tensor_copy(dst[:, 0:d], blocks[:, 0:d]))
                    link(nv.tensor_tensor(dst[:, d:], blocks[:, d:], blocks[:, 0:E1 - d], ALU.add))
                    blocks = dst
                first = off[1]
                link(nv.tensor_tensor(first[:, :], blocks[:, :], nb[:, :], ALU.subtract))
                link(nv.tensor_tensor(base[:, :, :], src[:, :, :], total[:, :, :], ALU.subtract))
                link(nv.tensor_tensor(base[:, :, :].rearrange("p t e -> p (t e)"), rank[:, 0:NT * E1],
                                      base[:, :, :].rearrange("p t e -> p (t e)"), ALU.add))
                link(nv.tensor_scalar(off[0][:, :], first[:, :], float(SLOTS), None, ALU.mult))
                link(nv.tensor_tensor(base[:, :, :], base[:, :, :], off[0][:, :].unsqueeze(1).to_broadcast([P, NT, E1]), ALU.add))
                for k in range(2):
                    link(nv.tensor_tensor(prod[:, :, :], base[:, :, :], eq[:, :, :, k], ALU.mult))
                    link(nv.tensor_reduce(posf[:, k, :], prod[:, :, :], AX.X, ALU.add))
                    link(nv.tensor_copy(pos[k][:, :], posf[:, k, :]))
                link(nv.tensor_tensor(cmp[:, :, :], first[:, :].unsqueeze(1).to_broadcast([P, BLOCKS, E1]),
                                      iota[:, 0:BLOCKS].unsqueeze(2).to_broadcast([P, BLOCKS, E1]), ALU.is_le))
                link(nv.tensor_reduce(eb[:, :], cmp[:, :, :], AX.X, ALU.add))
                link(nv.tensor_scalar(eb[:, :], eb[:, :], -1.0, None, ALU.add))
                link(nv.tensor_copy(block_expert[:, :], eb[:, :]))


def scatter_rows(c, name, h, pos, h_slots):
    nc = c.nc
    done = c.sem(f"{name}_done")
    block = nc.Block()
    with block:
        @block.gpsimd
        def _(g):
            for t in range(NT):
                for k in range(2):
                    g.indirect_dma_start(h_slots[:, :], bass.IndirectOffsetOnAxis(ap=pos[k][:, t:t + 1], axis=0),
                                         h[:, t, :], None).then_inc(done, 16)
            g.wait_ge(done, 16 * 2 * NT)


def swiglu_blocks(c, name, h_slots, y_slots, w, col_scale, block_expert):
    nc = c.nc
    WU, WF = KT * 2 * F1, KT * 2 * F1 + FC1 * D
    NI = SLOTS // P
    LAST = BLOCKS - 1
    assert BLOCKS % 2 == 1
    with ExitStack() as ctx:
        def sb(n, shape):
            return ctx.enter_context(nc.sbuf_tensor(f"{name}_{n}", shape, F32))

        def sem(n):
            return c.sem(f"{name}_{n}")

        ws = [sb(f"w{s}", [P, WF]) for s in range(2)]
        hs = [sb(f"h{s}", [P, NI, D]) for s in range(2)]
        hT = [sb(f"hT{s}", [P, KT, SLOTS]) for s in range(2)]
        ys = [sb(f"y{s}", [P, NI, D]) for s in range(2)]
        col = sb("col", [P, KT])
        silu, act = sb("silu", [P, 4, SLOTS]), sb("act", [P, FC1, SLOTS])
        w_in, h_in, y_free = ([sem(f"{n}{s}") for s in range(2)] for n in ("w_in", "h_in", "y_free"))
        col_in, tr_done, hT_ready, up_done, silu_ready, act_ready, y_done, y_ready = (
            sem(n) for n in ("col_in", "tr", "hT", "up", "silu", "act", "y_done", "y_ready"))
        ph, py, tr = c.bank[0:4], c.bank[4:6], c.bank[6]
        block = nc.Block()
        with block:
            @block.sync
            def _(sp):
                def load(j, s):
                    expert = sp.value_load(block_expert[0:1, bass.ds(j, 1)], min_val=0, max_val=E1 - 1)
                    sp.dma_start(hs[s][:, :, :], h_slots[bass.ds(j * SLOTS, SLOTS), :].rearrange("(i p) d -> p i d", p=P)).then_inc(h_in[s], 16)
                    sp.dma_start(ws[s][:, :], w[bass.ds(expert, 1), :, :].rearrange("a p n -> p (a n)")).then_inc(w_in[s], 16)

                def store(j, s):
                    sp.wait_ge(y_ready, j + 1)
                    sp.dma_start(y_slots[bass.ds(j * SLOTS, SLOTS), :].rearrange("(i p) d -> p i d", p=P), ys[s][:, :, :]).then_inc(y_free[s], 16)

                for s in range(2):
                    sp.sem_inc(y_free[s], 16)
                sp.dma_start(col[:, :], col_scale).then_inc(col_in, 16)
                load(0, 0)
                load(1, 1)
                with sp.Fori(1, BLOCKS // 2) as m:
                    for s in range(2):
                        sp.wait_ge(y_done, 2 * m + (s - 1))
                        load(2 * m + s, s)
                        store(2 * m + (s - 2), s)
                sp.wait_ge(y_done, LAST - 1)
                load(LAST, 0)
                for j in range(LAST - 2, LAST + 1):
                    store(j, j % 2)
                sp.wait_ge(y_free[0], 16 * (BLOCKS // 2 + 2))
                sp.wait_ge(y_free[1], 16 * (BLOCKS // 2 + 1))

            @block.tensor
            def _(pe):
                def turn(m, s):
                    pe.wait_ge(h_in[s], 16 * m + 16)
                    for k in range(KT):
                        for i in range(NI):
                            mm = nc.tensor.transpose(tr[:, k * SLOTS + i * P:k * SLOTS + (i + 1) * P], hs[s][:, i, k * P:(k + 1) * P], c.ident[:, :])
                    mm.then_inc(tr_done, 1)

                def experts(m, s, following):
                    j = 2 * m + s
                    up, down = ws[s][:, 0:WU].rearrange("p (k i f) -> p k i f", k=KT, i=2), ws[s][:, WU:].rearrange("p (f n) -> p f n", n=D)
                    pe.wait_ge(hT_ready, 2 * j + 2)
                    pe.wait_ge(w_in[s], 16 * m + 16)
                    for f in range(FC1):
                        if f >= 4:
                            pe.wait_ge(act_ready, FC1 * j + (f - 3))
                        for i in range(2):
                            for k in range(KT):
                                mm = nc.tensor.matmul(ph[f % 4][:, i * SLOTS:(i + 1) * SLOTS], up[:, k, i, f * P:(f + 1) * P],
                                                      hT[s][:, k, :], start=(k == 0), stop=(k == KT - 1))
                        mm.then_inc(up_done, 1)
                    if following:
                        turn(*following)
                    for i in range(NI):
                        for f in range(FC1):
                            if i == 0:
                                pe.wait_ge(act_ready, FC1 * j + (f + 1))
                            mm = nc.tensor.matmul(py[s][:, i * D:(i + 1) * D], act[:, f, i * P:(i + 1) * P], down[:, f, :],
                                                  start=(f == 0), stop=(f == FC1 - 1))
                    mm.then_inc(y_done, 1)

                turn(0, 0)
                with pe.Fori(0, BLOCKS // 2) as m:
                    experts(m, 0, (m, 1))
                    experts(m, 1, (m + 1, 0))
                experts(LAST // 2, 0, None)

            @block.scalar
            def _(a):
                def keep_hT(j, s):
                    a.wait_ge(tr_done, j + 1)
                    for k in range(KT):
                        nc.scalar.activation(hT[s][:, k, :], tr[:, k * SLOTS:(k + 1) * SLOTS], ACT.Copy, scale=col[:, k:k + 1]).then_inc(hT_ready, 1)

                def silus(j):
                    for f in range(FC1):
                        a.wait_ge(up_done, FC1 * j + (f + 1))
                        nc.scalar.activation(silu[:, f % 4, :], ph[f % 4][:, 0:SLOTS], ACT.Silu).then_inc(silu_ready, 1)

                a.wait_ge(col_in, 16)
                keep_hT(0, 0)
                with a.Fori(0, BLOCKS // 2) as m:
                    for s in range(2):
                        silus(2 * m + s)
                        keep_hT(2 * m + s + 1, 1 - s)
                silus(LAST)

            @block.vector
            def _(v):
                def experts(m, s):
                    j = 2 * m + s
                    for f in range(FC1):
                        v.wait_ge(silu_ready, FC1 * j + (f + 1))
                        nc.vector.tensor_tensor(act[:, f, :], ph[f % 4][:, SLOTS:], silu[:, f % 4, :], ALU.mult).then_inc(act_ready, 1)
                    v.wait_ge(y_done, j + 1)
                    v.wait_ge(y_free[s], 16 * m + 16)
                    nc.vector.tensor_copy(ys[s][:, :, :].rearrange("p i d -> p (i d)"), py[s][:, :]).then_inc(y_ready, 1)

                with v.Fori(0, BLOCKS // 2) as m:
                    for s in range(2):
                        experts(m, s)
                experts(LAST // 2, 0)


def combine(c, name, y_slots, pos, pair, z):
    nc = c.nc
    with ExitStack() as ctx:
        def sb(n, shape):
            return ctx.enter_context(nc.sbuf_tensor(f"{name}_{n}", shape, F32))

        norm = Norm(c, ctx, name)
        got = [sb(f"got{k}", [P, NT, D]) for k in range(2)]
        y, t = sb("y", [P, NQ, D]), sb("t", [P, NQ, D])
        in_ = [c.sem(f"{name}_in{b}") for b in range(B)]
        y_ready, t_ready, x_ready = (c.sem(f"{name}_{n}") for n in ("y_ready", "t_ready", "x_ready"))
        block = nc.Block()
        with block:
            @block.gpsimd
            def _(g):
                for b in range(B):
                    for i in range(NQ * b, NQ * b + NQ):
                        for k in range(2):
                            g.indirect_dma_start(got[k][:, i, :], None, y_slots[:, :],
                                                 bass.IndirectOffsetOnAxis(ap=pos[k][:, i:i + 1], axis=0)).then_inc(in_[b], 16)
                    if b:
                        norm.root(g, b - 1)
                norm.root(g, B - 1)

            @block.vector
            def _(v):
                for b in range(B):
                    v.wait_ge(in_[b], 16 * 2 * NQ)
                    for q in range(NQ):
                        i = b * NQ + q
                        nc.vector.scalar_tensor_tensor(out=y[:, q, :], in0=got[0][:, i, :], scalar=pair[:, i, 0:1], in1=z[:, i, :],
                                                       op0=ALU.mult, op1=ALU.add).then_inc(y_ready, 1)
                    for q in range(NQ):
                        i = b * NQ + q
                        v.wait_ge(y_ready, 2 * NQ * b + q + 1)
                        nc.vector.scalar_tensor_tensor(out=y[:, q, :], in0=got[1][:, i, :], scalar=pair[:, i, 1:2], in1=y[:, q, :],
                                                       op0=ALU.mult, op1=ALU.add).then_inc(y_ready, 1)
                    v.wait_ge(y_ready, 2 * NQ * (b + 1))
                    norm.statistics(v, b, lambda q: y[:, q, :])
                    norm.wait(v, b)
                    add_normed(c, v, norm, b, lambda q: y[:, q, :], t, t_ready, x_ready)


def build(nc, a, out):
    with ExitStack() as ctx:
        c = Core(nc, ctx)
        iota = c.sb("iota", [P, E0], F32)
        before = c.sb("before", [P, P], F32)
        load_constants(c, a, iota, before)
        q_parts = nc.dram_tensor("q_parts", [3, QUADS, 4 * HD, S], BF16, kind="Internal").ap()
        k_parts = nc.dram_tensor("k_parts", [3, QUADS, 4 * HD, S], BF16, kind="Internal").ap()

        with ExitStack() as stage:
            vals = stage.enter_context(nc.sbuf_tensor("a_vals", [P, B * H, NQ, HD], F32))
            attended = stage.enter_context(nc.sbuf_tensor("a_attended", [P, NT, D], F32))
            narrow_projection(c, "a_in", a["a_wqk"], a["a_wv"], a["a_bqk"], a["a_bv"], None, q_parts, k_parts, vals)
            narrow_attention(c, "a_att", q_parts, k_parts, vals, attended, causal=True)
            narrow_output(c, "a_out", attended, a["a_wout"], a["a_bout"], 1.0)
        c.end_stage()

        with ExitStack() as stage:
            def sb(n, shape):
                return stage.enter_context(nc.sbuf_tensor(n, shape, F32))

            hT, logits, gates, acc = sb("b_hT", [P, KT, T]), sb("b_lg", [P, NT, E0]), sb("b_gates", [P, NT, E0]), sb("b_acc", [P, NT, D])
            router_input(c, "b_in", c.x, False, None, a["b_wr"], a["b_br"], E0, hT, None, logits)
            sigmoid_gates(c, "b_gate", logits, iota, gates)
            relu2_experts(c, "b_moe", hT, gates, a["b_w"], acc)
            add_normed_sum(c, "b_out", acc)
        c.end_stage()

        with ExitStack() as stage:
            vals = stage.enter_context(nc.sbuf_tensor("c_vals", [P, B * H, NQ, HD], F32))
            attended = stage.enter_context(nc.sbuf_tensor("c_attended", [P, NT, D], F32))
            lambdas = {"vectors": a["c_lambdas"], "halves": a["c_halves"]}
            narrow_projection(c, "c_in", a["c_wqk"], a["c_wv"], None, None, lambdas, q_parts, k_parts, vals)
            narrow_attention(c, "c_att", q_parts, k_parts, vals, attended, causal=False)
            narrow_output(c, "c_out", attended, a["c_wout"], None, 1.0 - LAMBDA_INIT)
        c.end_stage()

        q_dram = nc.dram_tensor("q_dram", [QUADS, P, 4, S], F32, kind="Internal").ap()
        k_dram = nc.dram_tensor("k_dram", [QUADS, P, 1, S], F32, kind="Internal").ap()
        o_dram = nc.dram_tensor("o_dram", [B * H, GD, S], F32, kind="Internal").ap()
        z = c.sb("z", [P, NT, D], F32)
        with ExitStack() as stage:
            vals = stage.enter_context(nc.sbuf_tensor("d_vals", [P, QUADS, NQ, GD], F32))
            grouped_projection(c, "d_in", a, z, vals, q_dram, k_dram)
            grouped_attention(c, "d_att", q_dram, k_dram, vals, o_dram)
            grouped_output(c, "d_out", o_dram, a["d_wo"], z)
        c.end_stage()
        with ExitStack() as stage:
            def sb(n, shape):
                return stage.enter_context(nc.sbuf_tensor(n, shape, F32))

            h_slots = nc.dram_tensor("h_slots", [BLOCKS * SLOTS, D], F32, kind="Internal").ap()
            y_slots = nc.dram_tensor("y_slots", [BLOCKS * SLOTS, D], F32, kind="Internal").ap()
            eq, pair = sb("e_eq", [P, NT, E1, 2]), sb("e_pair", [P, NT, 2])
            pos = [stage.enter_context(nc.sbuf_tensor(f"e_pos{k}", [P, NT], U32)) for k in range(2)]
            block_expert = stage.enter_context(nc.sbuf_tensor("e_block_expert", [P, BLOCKS], I32))
            with ExitStack() as routing:
                h = routing.enter_context(nc.sbuf_tensor("e_h", [P, NT, D], F32))
                logits = routing.enter_context(nc.sbuf_tensor("e_lg", [P, NT, E1], F32))
                router_input(c, "e_in", z, True, a["e_ln"], a["e_wr"], None, E1, None, h, logits, h_slots)
                two_highest(c, "e_gate", logits, iota, eq, pair)
                routed_slots(c, "e_slots", eq, before, iota, pos, block_expert)
                scatter_rows(c, "e_scatter", h, pos, h_slots)
            swiglu_blocks(c, "e_moe", h_slots, y_slots, a["e_w"], a["e_ln"], block_expert)
            combine(c, "e_out", y_slots, pos, pair, z)
        c.end_stage()

        done = c.sem("done")
        with nc.Block() as block:
            @block.sync
            def _(sp):
                sp.dma_start(out.rearrange("b (q p) d -> p (b q) d", p=P), c.x[:, :, :]).then_inc(done, 16)
                sp.wait_ge(done, 16)


def laid_out(i):
    import numpy as np
    i = {k: np.asarray(v) for k, v in i.items()}
    r = np.arange(P)
    wa, wc = i["L0_attn_W_qkv"], i["L1_attn_W_attn"]
    half = HD // 2
    pair = [wc[:, j * D // 2:(j + 1) * D // 2].reshape(D, H, half) for j in range(4)]
    w1 = np.concatenate([i["L0_ffn_W1"], i["L0_ffn_Ws1"].reshape(2, M0, D)])
    w2 = np.concatenate([i["L0_ffn_W2"], i["L0_ffn_Ws2"].reshape(D, 2, M0).transpose(1, 0, 2)])
    w1 = w1.transpose(0, 2, 1).reshape(E0 + 2, KT, P, M0).transpose(0, 2, 1, 3).reshape(E0 + 2, P, KT * M0)
    b_w = np.concatenate([w1, w2.transpose(0, 2, 1)], axis=2)
    evens_first = np.concatenate([np.arange(0, GD, 2), np.arange(1, GD, 2)])
    wq = i["L1_ffn_wq"].reshape(D, H, GD)[:, :, evens_first].reshape(D, H * GD)
    wk = i["L1_ffn_wk"].reshape(D, KVH, GD)[:, :, evens_first].reshape(D, KVH * GD)
    inv_freq = np.float32(1e6) ** (-np.arange(0, GD, 2, dtype=np.float32) / np.float32(GD))
    angle = (np.arange(S, dtype=np.float32)[:, None] * inv_freq[None, :]).T.astype(np.float64)
    rope = np.stack([np.concatenate([np.cos(angle), np.cos(angle)]),
                     np.concatenate([-np.sin(angle), np.sin(angle)])], axis=1)
    rope = np.stack([rope / np.sqrt(GD), rope], axis=1).astype(np.float32)
    e_up = np.stack([i["L1_ffn_w1"], i["L1_ffn_w3"]], axis=2)
    e_up = e_up.reshape(E1, KT, P, 2 * F1).transpose(0, 2, 1, 3).reshape(E1, P, KT * 2 * F1)
    e_down = i["L1_ffn_w2"].reshape(E1, FC1, P, D).transpose(0, 2, 1, 3).reshape(E1, P, FC1 * D)
    return {
        "d_wqk": np.concatenate([wq, wk], axis=1), "d_wv": i["L1_ffn_wv"], "d_wo": i["L1_ffn_wo"],
        "d_ln": i["L1_ffn_ln_w"].reshape(KT, P).T, "d_rope": rope,
        "e_ln": i["L1_ffn_ff_ln_w"].reshape(KT, P).T, "e_wr": i["L1_ffn_gate_w"],
        "e_w": np.concatenate([e_up, e_down], axis=2),
        "x": i["L0_attn_x"],
        "ident": np.eye(P, dtype=np.float32),
        "causal": np.where(r[None, :] <= r[:, None], 0.0, -1e38).astype(np.float32),
        "before": (r[:, None] < r[None, :]).astype(np.float32),
        "iota": np.arange(E0, dtype=np.float32),
        "a_wqk": wa[:, :2 * D], "a_wv": wa[:, 2 * D:], "a_bqk": i["L0_attn_b_qkv"][:2 * D].reshape(4, P).T,
        "a_bv": i["L0_attn_b_qkv"][2 * D:], "a_wout": i["L0_attn_W_out"], "a_bout": i["L0_attn_b_out"],
        "b_wr": i["L0_ffn_Wr"].T, "b_br": i["L0_ffn_br"],
        "b_w": b_w.reshape(E0 // 2 + 1, 2, P, KT * M0 + D).transpose(0, 2, 1, 3),
        "c_wqk": np.concatenate([np.concatenate([pair[j], pair[j + 2]], axis=2).reshape(D, D) for j in range(2)], axis=1),
        "c_wv": wc[:, 2 * D:], "c_wout": i["L1_attn_W_proj"],
        "c_lambdas": np.stack([i[f"L1_attn_lambda_{n}"] for n in ("q1", "k1", "q2", "k2")]),
        "c_halves": np.stack([-(r % HD >= half).astype(np.float32), (r % HD < half).astype(np.float32)], axis=1),
    }


def kernel(**inputs):
    import numpy as _np
    import concourse.bacc as _bacc
    from concourse import mybir as _mybir
    from concourse.bass_utils import run_bass_kernel_spmd as _run

    nc = _bacc.Bacc("TRN2", target_bir_lowering=False, num_devices=1)
    arrays, args = {}, {}
    for name, a in laid_out(inputs).items():
        a = _np.ascontiguousarray(a)
        arrays[f"in_{name}"] = a
        args[name] = nc.dram_tensor(f"in_{name}", a.shape, _mybir.dt.from_np(a.dtype), kind="ExternalInput").ap()
    out = nc.dram_tensor("out", (B, S, D), F32, kind="ExternalOutput").ap()
    build(nc, args, out)
    return _run(nc, [arrays], core_ids=[0]).results[0]["out"]
```
